# Optimizing a Trainium2 kernel written in Bass

```python
import numpy as np
import jax
import jax.numpy as jnp

def _softmax(x, axis=-1):
    return jax.nn.softmax(x, axis=axis)

def _gelu(x):
    return jax.nn.gelu(x, approximate=True)

def _silu(x):
    return jax.nn.silu(x)

def _sigmoid(x):
    return jax.nn.sigmoid(x)

def _layernorm(x, axis=-1, eps=1e-05):
    m = jnp.mean(x, axis=axis, keepdims=True)
    v = jnp.var(x, axis=axis, keepdims=True)
    return (x - m) / jnp.sqrt(v + eps)

def _scatter_add(tgt, idx, src, axis=0):
    return tgt.at[idx].add(src)

def _segment_sum(src, seg, n):
    return jax.ops.segment_sum(src, seg, n)
kernel_name = 'mk_gnn_preln_d4_gnn_r8_40f407'

def setup_inputs(seed: int=0):
    np.random.seed(seed)
    _w = jnp.asarray

    def _rec_inputs():
        import jax
        import jax.numpy as jnp
        _gk = jax.random.key(seed)
        x = -0.000202 + 1 * jax.random.normal(jax.random.fold_in(_gk, 1), (12500, 128), jnp.float32)
        _s = jax.random.randint(jax.random.fold_in(_gk, 2), (100000,), 0, 12500, jnp.int32)
        _d = jax.random.randint(jax.random.fold_in(_gk, 3), (100000,), 0, 12500, jnp.int32)
        _loop = jnp.arange(12500, dtype=jnp.int32)
        src = jnp.concatenate([_s, _d, _loop])
        dst = jnp.concatenate([_d, _s, _loop])
        _o = jnp.argsort(dst, stable=True)
        src = src[_o]
        dst = dst[_o]
        edge_attr_16 = -0.00010739 + 0.99994 * jax.random.normal(jax.random.fold_in(_gk, 12), (212500, 16), jnp.float32)
        edge_attr_20 = jax.random.uniform(jax.random.fold_in(_gk, 13), (212500, 20), jnp.float32, 0.0, 1)
        edge_attr_32 = 0.000196303 + 1.00016 * jax.random.normal(jax.random.fold_in(_gk, 14), (212500, 32), jnp.float32)
        edge_weight = jax.random.uniform(jax.random.fold_in(_gk, 16), (212500,), jnp.float32, 0.0, 0.999998)
        return (x, src, dst, edge_attr_16, edge_attr_20, edge_attr_32, edge_weight)
    x, src, dst, edge_attr_16, edge_attr_20, edge_attr_32, edge_weight = _rec_inputs()

    def _L0_gnn_setup():
        import jax, jax.numpy as jnp
        import numpy as np
        from jax.scipy.special import erf
        N_NODES = 6250
        N_EDGES = 100000
        N_BASIS = 128
        N_RBF = 20
        N_FILT = 128

        def smu(x, alpha=0.01, mu=2.5):
            return ((1 + alpha) * x + (1 - alpha) * x * erf(mu * (1 - alpha) * x)) / 2
        key = jax.random.key(seed)
        ks = jax.random.split(key, 16)
        x = jax.random.normal(ks[0], (N_NODES, N_BASIS), dtype=jnp.float32)
        f_ij = jax.random.uniform(ks[1], (N_EDGES, N_RBF), dtype=jnp.float32)
        rcut_ij = jax.random.uniform(ks[2], (N_EDGES,), dtype=jnp.float32)
        idx_i = jnp.sort(jax.random.randint(ks[3], (N_EDGES,), 0, N_NODES))
        idx_j = jax.random.randint(ks[4], (N_EDGES,), 0, N_NODES)
        s = lambda n: 1.0 / np.sqrt(n)
        W_in2f = jax.random.normal(ks[5], (N_FILT, N_BASIS), dtype=jnp.float32) * s(N_BASIS)
        W_f1 = jax.random.normal(ks[6], (N_FILT, N_RBF), dtype=jnp.float32) * s(N_RBF)
        b_f1 = jnp.zeros((N_FILT,), jnp.float32)
        W_f2 = jax.random.normal(ks[7], (N_FILT, N_FILT), dtype=jnp.float32) * s(N_FILT)
        b_f2 = jnp.zeros((N_FILT,), jnp.float32)
        W_o1 = jax.random.normal(ks[8], (N_BASIS, N_FILT), dtype=jnp.float32) * s(N_FILT)
        b_o1 = jnp.zeros((N_BASIS,), jnp.float32)
        W_o2 = jax.random.normal(ks[9], (N_BASIS, N_BASIS), dtype=jnp.float32) * s(N_BASIS)
        b_o2 = jnp.zeros((N_BASIS,), jnp.float32)
        return dict(x=x, f_ij=f_ij, rcut_ij=rcut_ij, idx_i=idx_i, idx_j=idx_j, W_in2f=W_in2f, W_f1=W_f1, b_f1=b_f1, W_f2=W_f2, b_f2=b_f2, W_o1=W_o1, b_o1=b_o1, W_o2=W_o2, b_o2=b_o2)
    _L0_gnn_all = _L0_gnn_setup()
    _L0_gnn_in = {k: v for k, v in _L0_gnn_all.items() if k in ('W_in2f', 'W_f1', 'b_f1', 'W_f2', 'b_f2', 'W_o1', 'b_o1', 'W_o2', 'b_o2')}
    del _L0_gnn_all

    def _L1_gnn_setup():
        import jax, jax.numpy as jnp
        import numpy as np
        N_NODES = 6250
        N_EDGES = 100000
        NODE_DIM = 128
        EDGE_FEAT_DIM = 32
        OUT_DIM = 128
        key = jax.random.key(seed)
        ks = jax.random.split(key, 7)
        h = jax.random.normal(ks[0], (N_NODES, NODE_DIM), dtype=jnp.float32)
        edge_index = jax.random.randint(ks[1], (2, N_EDGES), 0, N_NODES, dtype=jnp.int64)
        edge_features = jax.random.normal(ks[2], (N_EDGES, EDGE_FEAT_DIM), dtype=jnp.float32)
        in_dim = 2 * NODE_DIM + EDGE_FEAT_DIM
        W1 = jax.random.normal(ks[3], (in_dim, OUT_DIM), dtype=jnp.float32) * (1.0 / np.sqrt(in_dim))
        b1 = jax.random.normal(ks[4], (OUT_DIM,), dtype=jnp.float32) * 0.01
        W2 = jax.random.normal(ks[5], (OUT_DIM, OUT_DIM), dtype=jnp.float32) * (1.0 / np.sqrt(OUT_DIM))
        b2 = jax.random.normal(ks[6], (OUT_DIM,), dtype=jnp.float32) * 0.01
        return {'h': h, 'edge_index': edge_index, 'edge_features': edge_features, 'n': N_NODES, 'W1': W1, 'b1': b1, 'W2': W2, 'b2': b2}
    _L1_gnn_all = _L1_gnn_setup()
    _L1_gnn_in = {k: v for k, v in _L1_gnn_all.items() if k in ('W1', 'b1', 'W2', 'b2')}
    del _L1_gnn_all

    def _L2_gnn_setup():
        import jax, jax.numpy as jnp
        import numpy as np
        N_NODES = 12500
        key = jax.random.key(seed)
        k1, k2, k3 = jax.random.split(key, 3)
        x = jax.random.normal(k1, (N_NODES, 128), dtype=jnp.float32)
        src_idx = jax.random.randint(k2, (250000,), 0, N_NODES, dtype=jnp.int64)
        dst_idx = jax.random.randint(k3, (250000,), 0, N_NODES, dtype=jnp.int64)
        return {'x': x, 'src_idx': src_idx, 'dst_idx': dst_idx}
    _L2_gnn_all = _L2_gnn_setup()
    _L2_gnn_in = {k: v for k, v in _L2_gnn_all.items() if k in ()}
    del _L2_gnn_all

    def _L3_gnn_setup():
        import jax, jax.numpy as jnp
        import numpy as np
        N_NODES = 6250
        N_EDGES = 100000
        D_IN = 128
        D_SH = 16
        D_OUT = 128
        N_PATHS = 64
        key = jax.random.key(seed)
        k1, k2, k3, k4, k5, k6, k7, k8 = jax.random.split(key, 8)
        x = jax.random.normal(k1, (N_NODES, D_IN), dtype=jnp.float32)
        sh = jax.random.normal(k2, (N_EDGES, D_SH), dtype=jnp.float32)
        coeff = jax.random.normal(k3, (N_PATHS,), dtype=jnp.float32)
        src = jax.random.randint(k4, (N_EDGES,), 0, N_NODES, dtype=jnp.int64)
        dst = jax.random.randint(k5, (N_EDGES,), 0, N_NODES, dtype=jnp.int64)
        ki = jax.random.randint(k6, (N_PATHS,), 0, D_IN, dtype=jnp.int32)
        kj = jax.random.randint(k7, (N_PATHS,), 0, D_SH, dtype=jnp.int32)
        ko = jax.random.randint(k8, (N_PATHS,), 0, D_OUT, dtype=jnp.int32)
        return {'x': x, 'sh': sh, 'coeff': coeff, 'src': src, 'dst': dst, 'ki': ki, 'kj': kj, 'ko': ko}
    _L3_gnn_all = _L3_gnn_setup()
    _L3_gnn_in = {k: v for k, v in _L3_gnn_all.items() if k in ('coeff', 'ki', 'kj', 'ko')}
    del _L3_gnn_all
    return {'x': x, 'src': src, 'dst': dst, 'edge_attr_16': edge_attr_16, 'edge_attr_20': edge_attr_20, 'edge_attr_32': edge_attr_32, 'edge_weight': edge_weight, 'L0_gnn_W_in2f': _L0_gnn_in['W_in2f'], 'L0_gnn_W_f1': _L0_gnn_in['W_f1'], 'L0_gnn_b_f1': _L0_gnn_in['b_f1'], 'L0_gnn_W_f2': _L0_gnn_in['W_f2'], 'L0_gnn_b_f2': _L0_gnn_in['b_f2'], 'L0_gnn_W_o1': _L0_gnn_in['W_o1'], 'L0_gnn_b_o1': _L0_gnn_in['b_o1'], 'L0_gnn_W_o2': _L0_gnn_in['W_o2'], 'L0_gnn_b_o2': _L0_gnn_in['b_o2'], 'L1_gnn_W1': _L1_gnn_in['W1'], 'L1_gnn_b1': _L1_gnn_in['b1'], 'L1_gnn_W2': _L1_gnn_in['W2'], 'L1_gnn_b2': _L1_gnn_in['b2'], 'L3_gnn_coeff': _L3_gnn_in['coeff'], 'L3_gnn_ki': _L3_gnn_in['ki'], 'L3_gnn_kj': _L3_gnn_in['kj'], 'L3_gnn_ko': _L3_gnn_in['ko']}

def reference(x, src, dst, edge_attr_16, edge_attr_20, edge_attr_32, edge_weight, L0_gnn_W_in2f, L0_gnn_W_f1, L0_gnn_b_f1, L0_gnn_W_f2, L0_gnn_b_f2, L0_gnn_W_o1, L0_gnn_b_o1, L0_gnn_W_o2, L0_gnn_b_o2, L1_gnn_W1, L1_gnn_b1, L1_gnn_W2, L1_gnn_b2, L3_gnn_coeff, L3_gnn_ki, L3_gnn_kj, L3_gnn_ko):
    import jax
    import jax.numpy as jnp

    def _L0_gnn_ref(x, f_ij, rcut_ij, idx_i, idx_j, W_in2f, W_f1, b_f1, W_f2, b_f2, W_o1, b_o1, W_o2, b_o2):
        import jax, jax.numpy as jnp
        import numpy as np
        from jax.scipy.special import erf
        N_NODES = 6250
        N_EDGES = 100000
        N_BASIS = 128
        N_RBF = 20
        N_FILT = 128

        def smu(x, alpha=0.01, mu=2.5):
            return ((1 + alpha) * x + (1 - alpha) * x * erf(mu * (1 - alpha) * x)) / 2
        h = x @ W_in2f.T
        Wij = smu(f_ij @ W_f1.T + b_f1) @ W_f2.T + b_f2
        Wij = Wij * rcut_ij[:, None]
        x_ij = h[idx_j] * Wij
        agg = jax.ops.segment_sum(x_ij, idx_i, num_segments=h.shape[0])
        out = smu(agg @ W_o1.T + b_o1) @ W_o2.T + b_o2
        return out

    def _L1_gnn_ref(h, edge_index, edge_features, n, W1, b1, W2, b2):
        import jax, jax.numpy as jnp
        import numpy as np
        N_NODES = 6250
        N_EDGES = 100000
        NODE_DIM = 128
        EDGE_FEAT_DIM = 32
        OUT_DIM = 128
        rows, cols = (edge_index[0], edge_index[1])
        msg_input = jnp.concatenate([h[rows], h[cols], edge_features], axis=-1)
        hidden = jax.nn.gelu(msg_input @ W1 + b1, approximate=False)
        messages = hidden @ W2 + b2
        out = jax.ops.segment_sum(messages, rows, num_segments=n)
        return out

    def _L2_gnn_ref(x, src_idx, dst_idx):
        import jax, jax.numpy as jnp
        import numpy as np
        N_NODES = 12500
        x_j = x[src_idx]
        agg = jax.ops.segment_sum(x_j, dst_idx, num_segments=x.shape[0])
        return x + agg

    def _L3_gnn_ref(x, sh, coeff, src, dst, ki, kj, ko):
        import jax, jax.numpy as jnp
        import numpy as np
        N_NODES = 6250
        N_EDGES = 100000
        D_IN = 128
        D_SH = 16
        D_OUT = 128
        N_PATHS = 64
        xg = x[src]
        vals = coeff[None, :] * xg[:, ki] * sh[:, kj]
        msg = jnp.zeros((sh.shape[0], D_OUT), dtype=x.dtype).at[:, ko].add(vals)
        out = jnp.zeros((x.shape[0], D_OUT), dtype=x.dtype).at[dst].add(msg)
        return out
    edge_index = jnp.stack([src, dst])
    h = jnp.maximum(_layernorm(x, axis=-1), 0.0)
    x = x + _L0_gnn_ref(h, edge_attr_20, edge_weight, src, dst, L0_gnn_W_in2f, L0_gnn_W_f1, L0_gnn_b_f1, L0_gnn_W_f2, L0_gnn_b_f2, L0_gnn_W_o1, L0_gnn_b_o1, L0_gnn_W_o2, L0_gnn_b_o2)
    h = jnp.maximum(_layernorm(x, axis=-1), 0.0)
    x = x + _L1_gnn_ref(h, edge_index, edge_attr_32, 12500, L1_gnn_W1, L1_gnn_b1, L1_gnn_W2, L1_gnn_b2)
    h = jnp.maximum(_layernorm(x, axis=-1), 0.0)
    x = x + _L2_gnn_ref(h, src, dst)
    h = jnp.maximum(_layernorm(x, axis=-1), 0.0)
    x = x + _L3_gnn_ref(h, edge_attr_16, L3_gnn_coeff, src, dst, L3_gnn_ki, L3_gnn_kj, L3_gnn_ko)
    return x

_drawn_inputs = setup_inputs


def setup_inputs(seed=0):
    import zlib

    import numpy as np

    out = dict(_drawn_inputs(seed))
    spreads = {'L0_gnn_b_f1': (0.0, 0.1),
     'L0_gnn_b_f2': (0.0, 0.1),
     'L0_gnn_b_o1': (0.0, 0.1),
     'L0_gnn_b_o2': (0.0, 0.1)}
    factors = {'L1_gnn_b1': 3.429}
    for name, (base, spread) in spreads.items():
        noise = np.random.default_rng([zlib.crc32(name.encode()), seed]).standard_normal(out[name].shape)
        drawn = base * np.exp(spread * noise) if base else spread * noise
        out[name] = jnp.asarray(drawn.astype(out[name].dtype))
    for name, factor in factors.items():
        out[name] = (out[name] * factor).astype(out[name].dtype)
    return out
```

```python
from contextlib import ExitStack

import concourse.bass as bass
from concourse import mybir

F32 = mybir.dt.float32
BF16 = mybir.dt.bfloat16
I32 = mybir.dt.int32
ALU = mybir.AluOpType
ACT = mybir.ActivationFunctionType
AX = mybir.AxisListType

P = 128
F = 128
G = 4
SLOTS = 4
BODY = G * SLOTS
BANK = 512
NRBF, NEF, NSH, NPATH = 20, 32, 16, 64

C_RBF, C_ONE, C_WEIGHT, C_SH = 0, NRBF, NRBF + 1, NRBF + 2
C_SRC = C_SH + NSH
C_POS = C_SRC + 1
C_DLOC = C_POS + 1
C_EF = C_DLOC + 1
C_DST = C_EF + NEF
C_SLOC = C_DST + 1
ROW = C_SLOC + 2
CARRY = C_SLOC + 1 - C_EF
S_EF, S_DST, S_SLOC = F, F + NEF, F + NEF + 1
SROW = F + CARRY

FAR = float(1 << 22)
SMU = 2.5 * 0.99 * 2.0 ** 0.5
SMU_LIN = 0.01 / 0.99 * SMU
EPS = 1e-5


def edge_tiles(edges):
    return -(-edges // (P * BODY)) * BODY


def ordered_tiles(edges, windows):
    return -(-((edges + windows * (P - 1)) // P) // BODY) * BODY


class Memory:
    pass


def parts_of(tensor, *columns):
    flat, parts, at = tensor[:, :, :].rearrange("p w f -> p (w f)"), [], 0
    for n in columns:
        assert at + n <= flat.shape[1]
        parts.append(flat[:, at:at + n])
        at += n
    return parts


def allocate(nc, ctx, m):
    def sb(name, shape, dt=F32):
        return ctx.enter_context(nc.sbuf_tensor(name, shape, dt))

    W = m.windows
    m.blanks_d = ctx.enter_context(nc.semaphore("blanks_d"))
    m.blanks_s = ctx.enter_context(nc.semaphore("blanks_s"))
    m.norm_chain, m.norm_rooted = (ctx.enter_context(nc.semaphore(n)) for n in ("norm_chain", "norm_rooted"))
    m.project_steps = [Steps(nc, ctx, f"p_{n}", head)
                       for n, head in (("relued", 0), ("turned", 1), ("copied", 1), ("multiplied", 1), ("taken", 1))]
    m.waits_apart = {e.engine: ctx.enter_context(nc.semaphore(f"waits_apart_{n}"))
                     for n, e in (("sp", nc.sync), ("pool", nc.gpsimd), ("pe", nc.tensor))}
    m.blanks = 16 * (m.tiles // BODY)
    m.x = sb("x_nodes", [P, W, F])
    m.table = sb("node_table", [P, W, F])
    m.acc = sb("segment_sums", [P, W, F + 1])
    T = m.edge_tiles
    keys_dst, keys_src, pre_dst, pre_src, m.wf_dst, m.wf_src = parts_of(m.acc, *[T] * 6)
    m.keys_dst, m.keys_src = keys_dst.bitcast(I32), keys_src.bitcast(I32)
    m.pre_dst, m.pre_src = pre_dst[0:W, :], pre_src[0:W, :]
    parts = parts_of(m.table, BODY * ROW, BODY * SROW, T, m.tiles, m.tiles, m.tiles // 2)
    m.blank_d, m.blank_s = (p.rearrange("p (t c) -> p t c", t=BODY) for p in parts[:2])
    m.shifted = parts[2].bitcast(I32)
    m.tile_iota, m.tile_iota_f = parts[3][0:W, :].bitcast(I32), parts[4][0:W, :]
    m.started = parts[5][0:W, :].bitcast(BF16)
    m.iota_nodes = sb("iota_nodes", [P, P])
    m.iota_windows = sb("iota_windows", [P, W])
    m.ident = sb("ident", [P, P])
    m.ident_bf = sb("ident_bf", [P, P], BF16)
    m.before_bf = sb("before_bf", [P, P], BF16)
    m.before = sb("before", [P, P])
    m.ones_bf = sb("ones_bf", [P, 1], BF16)
    m.ones = sb("ones", [P, 1])
    m.eps = sb("eps", [P, 1])
    m.tile_window_dst = sb("tile_window_dst", [1, m.tiles], I32)
    m.tile_window_src = sb("tile_window_src", [1, m.tiles], I32)
    m.mean = sb("mean", [P, W])
    m.rstd = sb("rstd", [P, W])
    m.w_in2f = sb("w_in2f", [F, F])
    m.w_f1 = sb("w_f1", [NRBF + 1, F])
    m.w_f2 = sb("w_f2", [F, F])
    m.b_f2 = sb("b_f2", [P, F])
    m.w_o1 = sb("w_o1", [F, F])
    m.b_o1 = sb("b_o1", [F, 1])
    m.b_o1_gelu = sb("b_o1_gelu", [F, 1])
    m.b_o1_lin = sb("b_o1_lin", [F, 1])
    m.w_o2 = sb("w_o2", [F, F])
    m.b_o2 = sb("b_o2", [P, F])
    m.w1_ab = sb("w1_ab", [F, 2 * F])
    m.w1_ef = sb("w1_ef", [NEF, F])
    m.b1 = sb("b1", [P, F])
    m.w2 = sb("w2", [F, F])
    m.b2 = sb("b2", [P, F])
    m.pick_in = sb("pick_in", [F, NPATH])
    m.pick_sh = sb("pick_sh", [NSH, NPATH])
    m.pick_out = sb("pick_out", [NPATH, F])

    def dram(name, shape):
        return nc.dram_tensor(name, shape, F32, kind="Internal").ap()

    m.by_dst = dram("edges_by_dst", [P * m.tiles, ROW])
    m.by_src = dram("edges_by_src", [P * m.tiles, SROW])
    m.b_rows = dram("b_rows", [W * P, F])
    m.h_rows = dram("h_rows", [W * P, F])
    m.g_rows = dram("g_rows", [W * P, NPATH])


def tiles_of(table, tiles, t, first, last):
    return table.rearrange("(p t) c -> p t c", t=tiles)[:, bass.ds(t, G), first:last]


def window_registers(nc, eng, tile_window, t, windows):
    _, got = nc.values_load_multi_w_load_instructions(
        tile_window[0:1, bass.ds(t, G)], engines=[eng.engine], min_val=0, max_val=windows - 1,
        skip_runtime_bounds_check_because="each entry is a count of 1 to `windows` bases, less one")
    return got


class Steps:

    def __init__(self, nc, ctx, name, head=0, per=1):
        self.sem, self.first, self.per = ctx.enter_context(nc.semaphore(name)), head, per
        self.head = head

    def after(self, q):
        return q * self.per + (self.head + self.per)

    def before_reuse(self, q, slots):
        return q * self.per + (self.head + self.per - self.per * slots)

    def start(self, eng):
        eng.sem_inc(self.sem, self.first)

    def again(self, groups):
        self.head += self.per * groups + self.first


def wait_apart(m, eng, sem, value):
    eng.wait_ge(sem, value).then_inc(m.waits_apart[eng.engine], 1)


def in_step(eng, groups, slots, *stages):
    most = max(lead for lead, _ in stages)

    def step(q, at):
        for lead, emit in stages:
            if not isinstance(q, int) or 0 <= q + lead < groups:
                emit(q + lead, (at + lead) % slots)

    for q in range(-most, 0):
        step(q, q)
    looped = max(groups - most, 0) // slots * slots
    if looped:
        with eng.Fori(0, looped // slots) as turn:
            for k in range(slots):
                step(turn * slots + k, k)
    for q in range(looped, groups):
        step(q, q)


def load_constants(nc, m, w):
    with ExitStack() as ctx:
        def sem(name):
            return ctx.enter_context(nc.semaphore(name))

        loaded, made, cast, dve = sem("c_loaded"), sem("c_made"), sem("c_cast"), sem("c_dve")
        iota_i = ctx.enter_context(nc.sbuf_tensor("iota_i", [P, P], I32))
        ki = ctx.enter_context(nc.sbuf_tensor("ki", [F, NPATH], I32))
        kj = ctx.enter_context(nc.sbuf_tensor("kj", [NSH, NPATH], I32))
        ko = ctx.enter_context(nc.sbuf_tensor("ko", [NPATH, 1], I32))
        ki_f = ctx.enter_context(nc.sbuf_tensor("ki_f", [F, NPATH], F32))
        kj_f = ctx.enter_context(nc.sbuf_tensor("kj_f", [NSH, NPATH], F32))
        ko_f = ctx.enter_context(nc.sbuf_tensor("ko_f", [NPATH, 1], F32))
        place = ctx.enter_context(nc.sbuf_tensor("place", [P, 1], F32))
        coeff = ctx.enter_context(nc.sbuf_tensor("coeff", [NSH, NPATH], F32))
        block = ctx.enter_context(nc.Block())

        def rows(v, n):
            return v.rearrange("(a n) -> a n", a=1).to_broadcast([n, v.shape[0]])

        loads = [
            (m.w_in2f[:, :], w["w_in2f_t"]), (m.w_f1[0:NRBF, :], w["w_f1_t"]),
            (m.w_f1[NRBF:NRBF + 1, :], rows(w["b_f1"], 1)),
            (m.w_f2[:, :], w["w_f2_t"]), (m.b_f2[:, :], rows(w["b_f2"], P)),
            (m.w_o1[:, :], w["w_o1_t"]), (m.b_o1[:, :], w["b_o1"].rearrange("(n a) -> n a", a=1)),
            (m.w_o2[:, :], w["w_o2_t"]), (m.b_o2[:, :], rows(w["b_o2"], P)),
            (m.w1_ab[:, 0:F], w["w1"][0:F, :]), (m.w1_ab[:, F:2 * F], w["w1"][F:2 * F, :]),
            (m.w1_ef[:, :], w["w1"][2 * F:2 * F + NEF, :]), (m.b1[:, :], rows(w["b1"], P)),
            (m.w2[:, :], w["w2"]), (m.b2[:, :], rows(w["b2"], P)),
            (ki[:, :], rows(w["ki"], F)), (kj[:, :], rows(w["kj"], NSH)),
            (ko[:, :], w["ko"].rearrange("(n a) -> n a", a=1)), (coeff[:, :], rows(w["coeff"], NSH)),
            (m.x[:, :, :], w["x"].rearrange("(w p) f -> p w f", p=P)),
        ]

        @block.sync
        def _(sp):
            for to, of in loads:
                sp.dma_start(to, of).then_inc(loaded, 16)
            sp.wait_ge(loaded, 16 * len(loads))

        @block.gpsimd
        def _(pool):
            pool.iota(iota_i[:, :], pattern=[[1, P]], base=0, channel_multiplier=0).then_inc(made, 1)
            pool.memset(m.ident[:, :], 0.0).then_inc(made, 1)
            pool.memset(m.before[:, :], 1.0).then_inc(made, 1)
            pool.memset(m.ones_bf[:, :], 1.0)
            pool.memset(m.ones[:, :], 1.0)
            pool.memset(m.eps[:, :], EPS)
            pool.wait_ge(made, 3)
            pool.affine_select(out=m.ident[:, :], in_=m.ident[:, :], compare_op=ALU.not_equal, fill=1.0,
                               base=0, pattern=[[-1, P]], channel_multiplier=1).then_inc(made, 1)
            pool.affine_select(out=m.before[:, :], in_=m.before[:, :], compare_op=ALU.is_gt, fill=0.0,
                               base=0, pattern=[[1, P]], channel_multiplier=-1).then_inc(made, 1)

        @block.vector
        def _(v):
            v.wait_ge(made, 5)
            v.tensor_copy(m.iota_nodes[:, :], iota_i[:, :]).then_inc(cast, 1)
            v.tensor_copy(m.iota_windows[:, :], iota_i[:, 0:m.windows])
            v.tensor_copy(m.ident_bf[:, :], m.ident[:, :])
            v.tensor_copy(m.before_bf[:, :], m.before[:, :])
            v.wait_ge(cast, 1)
            v.tensor_tensor(m.table[:, 0, :], m.iota_nodes[:, :], m.ident[:, :], ALU.mult).then_inc(dve, 1)
            v.wait_ge(dve, 1)
            v.tensor_reduce(place[:, :], m.table[:, 0, :], AX.X, ALU.add).then_inc(dve, 1)
            v.wait_ge(loaded, 16 * len(loads))
            v.tensor_copy(ki_f[:, :], ki[:, :])
            v.tensor_copy(kj_f[:, :], kj[:, :])
            v.tensor_copy(ko_f[:, :], ko[:, :]).then_inc(dve, 1)
            v.tensor_scalar(m.w_f2[:, :], m.w_f2[:, :], 0.99 / SMU, None, ALU.mult)
            v.tensor_scalar(m.w_o2[:, :], m.w_o2[:, :], 0.99 / SMU, None, ALU.mult)
            v.tensor_scalar(m.b_o1_gelu[:, :], m.b_o1[:, :], SMU, None, ALU.mult)
            v.tensor_scalar(m.b_o1_lin[:, :], m.b_o1[:, :], SMU_LIN, None, ALU.mult)
            v.wait_ge(dve, 3)
            v.tensor_scalar(m.pick_in[:, :], ki_f[:, :], place[:, 0:1], None, ALU.is_equal)
            v.scalar_tensor_tensor(m.pick_sh[:, :], kj_f[:, :], place[0:NSH, 0:1], coeff[:, :],
                                   ALU.is_equal, ALU.mult)
            v.tensor_scalar(m.pick_out[:, :], m.iota_nodes[0:NPATH, :], ko_f[:, 0:1], None, ALU.is_equal)


def count_windows(nc, m, src_keys, dst_keys):
    W, T, TP = m.windows, m.edge_tiles, m.tiles
    with ExitStack() as ctx:
        def sem(name):
            return ctx.enter_context(nc.semaphore(name))

        keys_in, keys_done, split = sem("k_keys_in"), sem("k_keys_done"), sem("k_split")
        onehot, counted, scan = sem("k_onehot"), sem("k_counted"), sem("k_scan")
        based, tabled, blank_made = sem("k_based"), sem("k_tabled"), sem("k_blank_made")
        iotas, started_ready = sem("k_iotas"), sem("k_started_ready")
        shifted, tile_iota, tile_iota_f, started = m.shifted, m.tile_iota, m.tile_iota_f, m.started
        oh = ctx.enter_context(nc.sbuf_tensor("count_onehot", [P, 2, G, W], BF16))
        blank_d, blank_s, blanks_d, blanks_s = m.blank_d, m.blank_s, m.blanks_d, m.blanks_s
        n_i = ctx.enter_context(nc.sbuf_tensor("n_i", [W, 2], I32))
        n_t = ctx.enter_context(nc.sbuf_tensor("n_t", [W, 2], I32))
        n_f = ctx.enter_context(nc.sbuf_tensor("n_f", [W, 2], F32))
        base = ctx.enter_context(nc.sbuf_tensor("base", [W, 2], F32))
        base_slot = ctx.enter_context(nc.sbuf_tensor("base_slot", [W, 2], F32))
        banks = -(-max(T, TP) // BANK)
        window_keys = (m.wf_dst, m.wf_src)
        pres = (m.pre_dst, m.pre_src)
        tile_windows = (m.tile_window_dst, m.tile_window_src)

        counts = [ctx.enter_context(nc.psum_tensor(f"counts{k}", [P, banks * BANK], F32)) for k in range(2)]
        with nc.Block() as block:
            @block.sync
            def _(sp):
                sp.dma_start(m.keys_dst, dst_keys).then_inc(keys_in, 16)
                sp.dma_start(m.keys_src, src_keys).then_inc(keys_in, 16)
                sp.wait_ge(blank_made, 2)
                with sp.Fori(0, TP // BODY) as t:
                    sp.dma_start(m.by_dst.rearrange("(p t) c -> p t c", t=TP)[:, bass.ds(t * BODY, BODY), :],
                                 blank_d[:, :, :]).then_inc(blanks_d, 16)
                with sp.Fori(0, TP // BODY) as t:
                    sp.dma_start(m.by_src.rearrange("(p t) c -> p t c", t=TP)[:, bass.ds(t * BODY, BODY), :],
                                 blank_s[:, :, :]).then_inc(blanks_s, 16)

            @block.gpsimd
            def _(pool):
                pool.memset(blank_d[:, :, :], 0.0)
                pool.memset(blank_s[:, :, :], 0.0)
                pool.iota(tile_iota[:, :], pattern=[[1, TP]], base=0, channel_multiplier=0).then_inc(iotas, 1)
                pool.wait_ge(iotas, 1)
                pool.memset(blank_d[:, :, C_DLOC:C_DLOC + 1], -1.0)
                pool.memset(blank_d[:, :, C_SLOC:C_SLOC + 1], -1.0)
                pool.memset(blank_d[:, :, C_POS:C_POS + 1].bitcast(I32), int(FAR)).then_inc(blank_made, 1)
                pool.memset(blank_s[:, :, S_SLOC:S_SLOC + 1], -1.0).then_inc(blank_made, 1)

            @block.vector
            def _(v):
                v.wait_ge(keys_in, 32)
                for k, (keys, windows) in enumerate(zip((m.keys_dst, m.keys_src), window_keys)):
                    if k:
                        v.wait_ge(split, 2)
                    v.tensor_scalar(shifted[:, :], keys, 7, None, ALU.arith_shift_right).then_inc(split, 1)
                    v.wait_ge(split, 2 * k + 1)
                    v.tensor_copy(windows, shifted[:, :]).then_inc(split, 1)
                v.wait_ge(split, 4)
                with v.Fori(0, T // G) as q:
                    for k, windows in enumerate(window_keys):
                        v.wait_ge(counted, q * 2 + k)
                        v.tensor_tensor(
                            oh[:, k, :, :],
                            windows[:, bass.ds(q * G, G)].unsqueeze(2).to_broadcast([P, G, W]),
                            m.iota_windows[:, :].unsqueeze(1).to_broadcast([P, G, W]),
                            ALU.is_equal).then_inc(onehot, 1)

            @block.tensor
            def _(pe):
                with pe.Fori(0, T // G) as q:
                    for k in range(2):
                        pe.wait_ge(onehot, q * 2 + k + 1)
                        for j in range(G):
                            last = pe.matmul(counts[k][0:W, bass.ds(q * G + j, 1)], oh[:, k, j, :],
                                             m.ones_bf[:, 0:1], start=True, stop=True)
                        last.then_inc(counted, 1)

        with nc.Block() as block:
            @block.vector
            def _(v):
                v.tensor_copy(tile_iota_f[:, :], tile_iota[:, :]).then_inc(iotas, 1)
                for k, pre in enumerate(pres):
                    v.tensor_tensor_scan(pre, m.ones[0:W, 0:1].to_broadcast([W, T]), counts[k][0:W, 0:T],
                                         0.0, ALU.mult, ALU.add).then_inc(scan, 1)
                v.wait_ge(scan, 2)
                for k, pre in enumerate(pres):
                    v.tensor_scalar(n_i[:, k:k + 1], pre[:, T - 1:T], float(P - 1), None, ALU.add).then_inc(scan, 1)
                v.wait_ge(scan, 4)
                v.tensor_scalar(n_t[:, :], n_i[:, :], 7, None, ALU.arith_shift_right).then_inc(scan, 1)
                v.wait_ge(scan, 5)
                v.tensor_copy(n_f[:, :], n_t[:, :]).then_inc(scan, 1)
                for k, pre in enumerate(pres):
                    v.tensor_tensor(pre, pre, counts[k][0:W, 0:T], ALU.subtract).then_inc(scan, 1)
                v.wait_ge(scan, 8)

        with nc.Block() as block:
            @block.tensor
            def _(pe):
                pe.matmul(counts[0][0:W, 0:2], m.before[0:W, 0:W], n_f[:, :], start=True, stop=True).then_inc(based, 1)
                for k in range(2):
                    pe.wait_ge(started_ready, k + 1)
                    for c in range(0, TP, BANK):
                        n = min(BANK, TP - c)
                        last = pe.matmul(counts[1 - k][0:1, c:c + n], m.ones_bf[0:W, 0:1], started[:, c:c + n],
                                         start=True, stop=True)
                    last.then_inc(tabled, 1)

            @block.vector
            def _(v):
                v.wait_ge(based, 1)
                v.tensor_copy(base[:, :], counts[0][0:W, 0:2]).then_inc(based, 1)
                v.wait_ge(based, 2)
                v.tensor_scalar(base_slot[:, :], base[:, :], float(P), None, ALU.mult).then_inc(based, 1)
                v.wait_ge(based, 3)
                for k, pre in enumerate(pres):
                    v.tensor_scalar(pre, pre, base_slot[:, k:k + 1], None, ALU.add)
                    if k:
                        v.wait_ge(tabled, k)
                    v.tensor_scalar(started[:, :], tile_iota_f[:, :], base[:, k:k + 1], None,
                                    ALU.is_ge).then_inc(started_ready, 1)
                for k, tile_window in enumerate(tile_windows):
                    v.wait_ge(tabled, k + 1)
                    v.tensor_scalar(tile_window[:, :], counts[1 - k][0:1, 0:TP], -1.0, None, ALU.add)


def order_edges(nc, m, edges):
    W, T, TP = m.windows, m.edge_tiles, m.tiles
    with ExitStack() as ctx:
        def sb(name, shape, dt=F32):
            return ctx.enter_context(nc.sbuf_tensor(name, shape, dt))

        def bank(name, shape, dt=F32):
            return ctx.enter_context(nc.psum_tensor(name, shape, dt))

        rows = sb("o_rows", [P, SLOTS, G, ROW])
        index = sb("o_index", [P, SLOTS, G], I32)
        oh = sb("o_onehot", [P, 2, 2, G, W], BF16)
        oh_t = sb("o_onehot_t", [W, 2, 2 * G * P])
        prod = sb("o_prod", [P, 2, G, W])
        rank = sb("o_rank", [P, 2, G])
        slot_i = sb("o_slot_i", [P, 2, G], I32)
        lo = sb("o_lo", [P, 2, G], I32)
        hi = sb("o_hi", [P, 2, G], I32)
        row = sb("o_row", [P, 2, G])
        none = sb("o_none", [P, G])
        rank_ps = [[bank(f"o_rank_ps{b}{k}", [P, BANK]) for k in range(2)] for b in range(2)]
        oh_t_ps = bank("o_onehot_t_ps", [P, 2 * BANK], BF16)
        look_ps = [bank(f"o_look_ps{b}", [P, BANK]) for b in range(2)]

        row_in = [ctx.enter_context(nc.semaphore(f"o_row_in{k}")) for k in range(SLOTS)]
        sent = [ctx.enter_context(nc.semaphore(f"o_sent{k}")) for k in range(SLOTS)]
        onehot = Steps(nc, ctx, "o_onehot_made")
        turned = Steps(nc, ctx, "o_turned", head=1)
        copied = Steps(nc, ctx, "o_copied", head=1)
        looked = Steps(nc, ctx, "o_looked", head=1)
        chain = Steps(nc, ctx, "o_chain", per=7)
        placed = Steps(nc, ctx, "o_placed", head=1)
        block = ctx.enter_context(nc.Block())

        @block.sync
        def _(sp):
            def load(q, k):
                wait_apart(m, sp, sent[k], (q - k) * (16 * G // SLOTS))
                sp.dma_start(rows[:, k, :, :], tiles_of(edges, T, q * G, 0, ROW)).then_inc(row_in[k], 16)

            in_step(sp, T // G, SLOTS, (0, load))
            sp.wait_ge(m.blanks_s, m.blanks)

        @block.vector
        def _(v):
            turned_free = turned

            def make_onehot(q, k):
                v.wait_ge(turned_free.sem, turned_free.before_reuse(q, 2))
                for key, windows in enumerate((m.wf_dst, m.wf_src)):
                    last = v.tensor_tensor(
                        oh[:, k % 2, key, :, :],
                        windows[:, bass.ds(q * G, G)].unsqueeze(2).to_broadcast([P, G, W]),
                        m.iota_windows[:, :].unsqueeze(1).to_broadcast([P, G, W]), ALU.is_equal)
                last.then_inc(onehot.sem, 1)

            def place(q, k):
                b = k % 2
                base = chain.after(q) - chain.per
                keys_d, keys_s = m.keys_dst[:, bass.ds(q * G, G)], m.keys_src[:, bass.ds(q * G, G)]
                wins_d, wins_s = m.wf_dst[:, bass.ds(q * G, G)], m.wf_src[:, bass.ds(q * G, G)]
                v.wait_ge(row_in[k], (q - k) * (16 // SLOTS) + 16)
                v.scalar_tensor_tensor(rows[:, k, :, C_DLOC], wins_d, -float(P), keys_d, ALU.mult, ALU.add)
                v.scalar_tensor_tensor(rows[:, k, :, C_SLOC], wins_s, -float(P), keys_s, ALU.mult, ALU.add)
                v.tensor_copy(rows[:, k, :, C_DST], keys_d)
                v.wait_ge(placed.sem, placed.after(q) - 1)
                v.tensor_scalar(none[:, :], wins_d, 0.0, FAR, ALU.is_lt, ALU.mult).then_inc(chain.sem, 1)
                v.wait_ge(turned.sem, turned.after(q))
                for key in range(2):
                    last = v.tensor_tensor(prod[:, key, :, :],
                                           rank_ps[b][key][:, 0:G * W].rearrange("p (g w) -> p g w", g=G),
                                           oh[:, b, key, :, :], ALU.mult)
                last.then_inc(chain.sem, 1)
                v.wait_ge(chain.sem, base + 2)
                v.tensor_reduce(rank[:, :, :], prod[:, :, :, :], AX.X, ALU.add).then_inc(chain.sem, 1)
                v.wait_ge(looked.sem, looked.after(q))
                v.wait_ge(chain.sem, base + 3)
                v.tensor_tensor(slot_i[:, :, :], rank[:, :, :],
                                look_ps[b][:, 0:2 * G].rearrange("p (k g) -> p k g", k=2),
                                ALU.add).then_inc(chain.sem, 1)
                v.wait_ge(chain.sem, base + 4)
                v.tensor_scalar(lo[:, :, :], slot_i[:, :, :], P - 1, None, ALU.bitwise_and)
                v.tensor_scalar(hi[:, :, :], slot_i[:, :, :], 7, None, ALU.arith_shift_right).then_inc(chain.sem, 1)
                v.wait_ge(chain.sem, base + 5)
                v.scalar_tensor_tensor(row[:, :, :], lo[:, :, :], float(TP), hi[:, :, :], ALU.mult,
                                       ALU.add).then_inc(chain.sem, 1)
                v.wait_ge(chain.sem, base + 6)
                v.tensor_copy(rows[:, k, :, C_POS].bitcast(I32), row[:, 1, :]).then_inc(chain.sem, 1)
                v.tensor_tensor(index[:, k, :], row[:, 0, :], none[:, :], ALU.add).then_inc(placed.sem, 1)

            placed.start(v)
            in_step(v, T // G, SLOTS, (1, make_onehot), (0, place))

        @block.tensor
        def _(pe):
            def rank_and_turn(q, k):
                b = k % 2
                pe.wait_ge(placed.sem, placed.before_reuse(q, 2))
                pe.wait_ge(onehot.sem, onehot.after(q))
                for key in range(2):
                    pe.matmul(rank_ps[b][key][:, 0:G * W], m.before_bf[:, :],
                              oh[:, b, key, :, :].rearrange("p g w -> p (g w)"), start=True, stop=True)
                pe.wait_ge(copied.sem, copied.before_reuse(q, 1))
                for key in range(2):
                    for j in range(G):
                        c = (key * G + j) * P
                        last = pe.transpose(oh_t_ps[0:W, c:c + P], oh[:, b, key, j, :], m.ident_bf[:, :])
                last.then_inc(turned.sem, 1)

            def look_up(q, k):
                b = k % 2
                pe.wait_ge(copied.sem, copied.after(q))
                for key, pre in enumerate((m.pre_dst, m.pre_src)):
                    for j in range(G):
                        c = key * G + j
                        last = pe.matmul(look_ps[b][:, c:c + 1], oh_t[:, b, c * P:(c + 1) * P],
                                         pre[:, bass.ds(q * G + j, 1)], start=True, stop=True)
                last.then_inc(looked.sem, 1)

            turned.start(pe)
            looked.start(pe)
            in_step(pe, T // G, SLOTS, (1, rank_and_turn), (0, look_up))

        @block.scalar
        def _(act):
            def copy(q, k):
                act.wait_ge(looked.sem, looked.before_reuse(q, 2))
                act.wait_ge(turned.sem, turned.after(q))
                act.activation(oh_t[:, k % 2, :], oh_t_ps[0:W, :], ACT.Copy).then_inc(copied.sem, 1)

            copied.start(act)
            in_step(act, T // G, SLOTS, (0, copy))

        @block.gpsimd
        def _(pool):
            def send(q, k):
                pool.wait_ge(m.blanks_d, m.blanks)
                wait_apart(m, pool, placed.sem, placed.after(q))
                for j in range(G):
                    pool.indirect_dma_start(
                        m.by_dst, bass.IndirectOffsetOnAxis(ap=index[:, k, j:j + 1], axis=0),
                        rows[:, k, j, :], None, bounds_check=P * TP - 1, oob_is_err=False).then_inc(sent[k], 16)

            in_step(pool, T // G, SLOTS, (0, send))
            for k in range(SLOTS):
                pool.wait_ge(sent[k], 16 * G * (T // G // SLOTS))


def normalise(nc, m, layer, out):
    W = m.windows
    with ExitStack() as ctx:
        chain, rooted = m.norm_chain, m.norm_rooted
        done = 7 * layer
        var = ctx.enter_context(nc.sbuf_tensor(f"n_var_{layer}", [P, W], F32))
        std = ctx.enter_context(nc.sbuf_tensor(f"n_std_{layer}", [P, W], F32))
        spare = m.acc[:, :, 0:F]
        block = ctx.enter_context(nc.Block())

        def spread(a):
            return a[:, :].unsqueeze(2).to_broadcast([P, W, F])

        @block.vector
        def _(v):
            v.tensor_reduce(m.mean[:, :], m.x[:, :, :], AX.X, ALU.add).then_inc(chain, 1)
            v.wait_ge(chain, done + 1)
            v.tensor_scalar(m.mean[:, :], m.mean[:, :], 1.0 / F, None, ALU.mult).then_inc(chain, 1)
            v.wait_ge(chain, done + 2)
            v.tensor_tensor(out, m.x[:, :, :], spread(m.mean), ALU.subtract).then_inc(chain, 1)
            v.wait_ge(chain, done + 3)
            v.tensor_tensor(spare, out, out, ALU.mult).then_inc(chain, 1)
            v.wait_ge(chain, done + 4)
            v.tensor_reduce(var[:, :], spare, AX.X, ALU.add).then_inc(chain, 1)
            v.wait_ge(rooted, layer + 1)
            v.reciprocal(m.rstd[:, :], std[:, :]).then_inc(chain, 1)
            v.wait_ge(chain, done + 6)
            v.tensor_tensor(out, out, spread(m.rstd), ALU.mult).then_inc(chain, 1)

        @block.scalar
        def _(act):
            act.wait_ge(chain, done + 5)
            act.activation(std[:, :], var[:, :], ACT.Sqrt, bias=m.eps[:, 0:1], scale=1.0 / F).then_inc(rooted, 1)


def project(nc, m, layer, weights, columns, bias, kept, rows_out, out_columns):
    W, PAIR = m.windows, 2
    with ExitStack() as ctx:
        def sb(name, shape, dt=F32):
            return ctx.enter_context(nc.sbuf_tensor(name, shape, dt))

        h = sb(f"p_h_{layer}", [P, PAIR, F])
        h_t = sb(f"p_h_t_{layer}", [F, PAIR, P])
        away = sb(f"p_away_{layer}", [P, PAIR, out_columns or 2])
        turn_ps = [ctx.enter_context(nc.psum_tensor(f"p_turn{b}_{layer}", [P, BANK], F32)) for b in range(PAIR)]
        prod_ps = [ctx.enter_context(nc.psum_tensor(f"p_prod{b}_{layer}", [P, BANK], F32)) for b in range(PAIR)]
        relued, turned, copied, multiplied, taken = m.project_steps
        stored = [ctx.enter_context(nc.semaphore(f"p_stored{b}_{layer}")) for b in range(PAIR if out_columns else 0)]
        block = ctx.enter_context(nc.Block())

        @block.scalar
        def _(act):
            def relu(w, b):
                act.wait_ge(turned.sem, turned.before_reuse(w, PAIR))
                act.activation(h[:, b, :], m.table[:, bass.ds(w, 1), :].rearrange("p w f -> p (w f)"),
                               ACT.Relu).then_inc(relued.sem, 1)

            in_step(act, W, PAIR, (0, relu))

        @block.tensor
        def _(pe):
            def turn(w, b):
                pe.wait_ge(copied.sem, copied.before_reuse(w, PAIR))
                pe.wait_ge(relued.sem, relued.after(w))
                pe.transpose(turn_ps[b][:, 0:P], h[:, b, :], m.ident[:, :]).then_inc(turned.sem, 1)

            def multiply(w, b):
                pe.wait_ge(taken.sem, taken.before_reuse(w, PAIR))
                pe.wait_ge(copied.sem, copied.after(w))
                pe.matmul(prod_ps[b][:, 0:columns], h_t[:, b, :], weights, start=True,
                          stop=True).then_inc(multiplied.sem, 1)

            turned.start(pe)
            multiplied.start(pe)
            in_step(pe, W, PAIR, (1, turn), (0, multiply))

        @block.vector
        def _(v):
            def copy(w, b):
                v.wait_ge(multiplied.sem, multiplied.before_reuse(w, PAIR))
                v.wait_ge(turned.sem, turned.after(w))
                v.tensor_copy(h_t[:, b, :], turn_ps[b][:, 0:P]).then_inc(copied.sem, 1)

            def take(w, b):
                if out_columns:
                    v.wait_ge(stored[b], (w - b) * (16 // PAIR))
                v.wait_ge(multiplied.sem, multiplied.after(w))
                window = m.table[:, bass.ds(w, 1), :].rearrange("p w f -> p (w f)")
                if kept and bias is not None:
                    last = v.tensor_tensor(window, prod_ps[b][:, 0:kept], bias, ALU.add)
                elif kept:
                    last = v.tensor_copy(window, prod_ps[b][:, 0:kept])
                if out_columns:
                    last = v.tensor_copy(away[:, b, :], prod_ps[b][:, kept:kept + out_columns])
                last.then_inc(taken.sem, 1)

            copied.start(v)
            taken.start(v)
            in_step(v, W, PAIR, (1, copy), (0, take))

        if out_columns:
            @block.sync
            def _(sp):
                def store(w, b):
                    wait_apart(m, sp, taken.sem, taken.after(w))
                    sp.dma_start(rows_out.rearrange("(w p) c -> p w c", p=P)[:, bass.ds(w, 1), :],
                                 away[:, b:b + 1, :]).then_inc(stored[b], 16)

                in_step(sp, W, PAIR, (0, store))
                for b in range(PAIR):
                    sp.wait_ge(stored[b], 16 * (W // PAIR))
        for steps in m.project_steps:
            steps.again(W)


def update_nodes(nc, m, layer):
    W, PAIR = m.windows, 2
    K = NPATH if layer == 3 else F
    with ExitStack() as ctx:
        def sb(name, shape, dt=F32):
            return ctx.enter_context(nc.sbuf_tensor(name, shape, dt))

        sums = sb(f"u_sums_{layer}", [P, PAIR, K])
        sums_t = sb(f"u_sums_t_{layer}", [K, PAIR, P])
        gelu = sb(f"u_gelu_{layer}", [F, PAIR, P])
        line = sb(f"u_line_{layer}", [F, PAIR, P])
        smu = sb(f"u_smu_{layer}", [F, PAIR, P])
        part = sb(f"u_part_{layer}", [P, PAIR, F])
        banks = [[ctx.enter_context(nc.psum_tensor(f"u_{n}{b}_{layer}", [P, BANK], F32)) for b in range(PAIR)]
                 for n in ("turn", "hidden", "out")]
        turn_ps, hid_ps, out_ps = banks
        staged, turned = Steps(nc, ctx, f"u_staged_{layer}"), Steps(nc, ctx, f"u_turned_{layer}", 1)
        copied, mapped = Steps(nc, ctx, f"u_copied_{layer}", 1), Steps(nc, ctx, f"u_mapped_{layer}", 1)
        parted, added = Steps(nc, ctx, f"u_parted_{layer}"), Steps(nc, ctx, f"u_added_{layer}", 1)
        if layer == 0:
            hidden, bent, summed = (Steps(nc, ctx, f"u_{n}", 1) for n in ("hidden", "bent", "summed"))
        weights = {0: m.w_o2, 1: m.w2, 3: m.pick_out}[layer]
        block = ctx.enter_context(nc.Block())

        @block.scalar
        def _(act):
            def stage(w, b):
                act.wait_ge(turned.sem, turned.before_reuse(w, PAIR))
                act.activation(sums[:, b, :], m.acc[:, bass.ds(w, 1), 0:K].rearrange("p w f -> p (w f)"),
                               ACT.Copy).then_inc(staged.sem, 1)

            def bend(w, b):
                act.wait_ge(summed.sem, summed.before_reuse(w, PAIR))
                act.wait_ge(hidden.sem, hidden.after(w))
                act.activation(gelu[:, b, :], hid_ps[b][:, 0:P], ACT.Gelu, bias=m.b_o1_gelu[:, 0:1], scale=SMU)
                act.activation(line[:, b, :], hid_ps[b][:, 0:P], ACT.Identity, bias=m.b_o1_lin[:, 0:1],
                               scale=SMU_LIN).then_inc(bent.sem, 1)

            if layer == 0:
                bent.start(act)
                in_step(act, W, PAIR, (2, stage), (0, bend))
            else:
                in_step(act, W, PAIR, (0, stage))

        @block.tensor
        def _(pe):
            def turn(w, b):
                pe.wait_ge(copied.sem, copied.before_reuse(w, PAIR))
                wait_apart(m, pe, staged.sem, staged.after(w))
                pe.transpose(turn_ps[b][0:K, 0:P], sums[:, b, :], m.ident[:, :]).then_inc(turned.sem, 1)

            def hide(w, b):
                pe.wait_ge(bent.sem, bent.before_reuse(w, PAIR))
                pe.wait_ge(copied.sem, copied.after(w))
                pe.matmul(hid_ps[b][:, 0:P], m.w_o1[:, :], sums_t[:, b, :], start=True,
                          stop=True).then_inc(hidden.sem, 1)

            def map_out(w, b):
                pe.wait_ge(added.sem, added.before_reuse(w, PAIR))
                if layer == 0:
                    pe.wait_ge(summed.sem, summed.after(w))
                    left = smu[:, b, :]
                else:
                    pe.wait_ge(copied.sem, copied.after(w))
                    left = sums_t[:, b, :]
                pe.matmul(out_ps[b][:, 0:F], left, weights[:, :], start=True, stop=True).then_inc(mapped.sem, 1)

            turned.start(pe)
            mapped.start(pe)
            if layer == 0:
                hidden.start(pe)
                in_step(pe, W, PAIR, (2, turn), (1, hide), (0, map_out))
            else:
                in_step(pe, W, PAIR, (1, turn), (0, map_out))

        @block.vector
        def _(v):
            def copy(w, b):
                reader = hidden if layer == 0 else mapped
                v.wait_ge(reader.sem, reader.before_reuse(w, PAIR))
                v.wait_ge(turned.sem, turned.after(w))
                v.tensor_copy(sums_t[:, b, :], turn_ps[b][0:K, 0:P]).then_inc(copied.sem, 1)

            def sum_smu(w, b):
                v.wait_ge(mapped.sem, mapped.before_reuse(w, PAIR))
                v.wait_ge(bent.sem, bent.after(w))
                v.tensor_tensor(smu[:, b, :], gelu[:, b, :], line[:, b, :], ALU.add).then_inc(summed.sem, 1)

            def add(w, b):
                node = m.x[:, bass.ds(w, 1), :].rearrange("p w f -> p (w f)")
                out = out_ps[b][:, 0:F]
                v.wait_ge(mapped.sem, mapped.after(w))
                if layer == 3:
                    v.tensor_tensor(node, node, out, ALU.add).then_inc(added.sem, 1)
                    return
                if layer == 0:
                    v.tensor_tensor(part[:, b, :], m.b_o2[:, :], out, ALU.add).then_inc(parted.sem, 1)
                else:
                    v.scalar_tensor_tensor(part[:, b, :], m.b2[:, :],
                                           m.acc[:, bass.ds(w, 1), F:F + 1].rearrange("p w f -> p (w f)"), out,
                                           ALU.mult, ALU.add).then_inc(parted.sem, 1)
                v.wait_ge(parted.sem, parted.after(w))
                v.tensor_tensor(node, node, part[:, b, :], ALU.add).then_inc(added.sem, 1)

            copied.start(v)
            added.start(v)
            if layer == 0:
                summed.start(v)
                in_step(v, W, PAIR, (2, copy), (1, sum_smu), (0, add))
            else:
                in_step(v, W, PAIR, (1, copy), (0, add))


def layer0_messages(nc, m):
    W, TP, N = m.windows, m.tiles, m.tiles // G
    with ExitStack() as ctx:
        def sb(name, shape, dt=F32):
            return ctx.enter_context(nc.sbuf_tensor(name, shape, dt))

        def bank(name):
            return ctx.enter_context(nc.psum_tensor(name, [P, BANK], F32))

        rows = sb("a_rows", [P, SLOTS, G, ROW])
        index = sb("a_index", [P, SLOTS, G], I32)
        GP = G * P
        out, oh, oh_t, rbf_t, gelu, smu, own, filt = parts_of(
            m.acc, SLOTS * G * SROW, 2 * GP, SLOTS * GP, SLOTS * GP, 2 * GP, 2 * GP, 2 * GP, 2 * GP)
        out = out.rearrange("p (s g c) -> p s g c", s=SLOTS, g=G)
        oh, own, filt = (a.rearrange("p (b g f) -> p b g f", b=2, g=G) for a in (oh, own, filt))
        gelu, smu = (a.rearrange("p (b e) -> p b e", b=2) for a in (gelu, smu))
        oh_t = oh_t.rearrange("p (s e) -> p s e", s=SLOTS)
        rbf_t = rbf_t[0:NRBF + 1, :].rearrange("p (s e) -> p s e", s=SLOTS)
        oh_t_ps, rbf_t_ps = bank("a_onehot_t_ps"), bank("a_rbf_t_ps")
        hid_ps = [bank(f"a_hidden{b}") for b in range(2)]
        own_ps = [bank(f"a_own_ps{b}") for b in range(2)]
        filt_ps = [bank(f"a_filt_ps{b}") for b in range(2)]

        row_in = [ctx.enter_context(nc.semaphore(f"a_row_in{k}")) for k in range(SLOTS)]
        sent = [ctx.enter_context(nc.semaphore(f"a_sent{k}")) for k in range(SLOTS)]
        onehot = Steps(nc, ctx, "a_onehot_made")
        turned = Steps(nc, ctx, "a_turned", head=1)
        copied = Steps(nc, ctx, "a_copied", head=1)
        hidden = Steps(nc, ctx, "a_hidden", head=3)
        gelued = Steps(nc, ctx, "a_gelued", head=1)
        smued = Steps(nc, ctx, "a_smued", head=1)
        filtered = Steps(nc, ctx, "a_filtered", head=3)
        scaled = Steps(nc, ctx, "a_scaled", head=3)
        biased = Steps(nc, ctx, "a_biased", head=1)
        made = Steps(nc, ctx, "a_made", head=3)
        block = ctx.enter_context(nc.Block())

        @block.sync
        def _(sp):
            def load(q, k):
                sp.wait_ge(scaled.sem, scaled.before_reuse(q, SLOTS))
                wait_apart(m, sp, made.sem, made.before_reuse(q, SLOTS))
                sp.dma_start(rows[:, k, :, :], tiles_of(m.by_dst, TP, q * G, 0, ROW)).then_inc(row_in[k], 16)

            in_step(sp, N, SLOTS, (0, load))

        @block.vector
        def _(v):
            def make_onehot(q, k):
                v.wait_ge(row_in[k], (q - k) * (16 // SLOTS) + 16)
                v.wait_ge(turned.sem, turned.before_reuse(q, 2))
                v.tensor_tensor(oh[:, k % 2, :, :], rows[:, k, :, C_DLOC:C_DLOC + 1].to_broadcast([P, G, P]),
                                m.iota_nodes[:, :].unsqueeze(1).to_broadcast([P, G, P]),
                                ALU.is_equal).then_inc(onehot.sem, 1)

            def sum_smu(q, k):
                b = k % 2
                v.wait_ge(filtered.sem, filtered.before_reuse(q, 2))
                v.wait_ge(gelued.sem, gelued.after(q))
                v.scalar_tensor_tensor(smu[:, b, :], hid_ps[b][:, :], SMU_LIN, gelu[:, b, :], ALU.mult,
                                       ALU.add).then_inc(smued.sem, 1)

            def message(q, k):
                b = k % 2
                v.wait_ge(filtered.sem, filtered.after(q))
                v.tensor_tensor(filt[:, b, :, :], filt_ps[b][:, :].rearrange("p (g f) -> p g f", g=G),
                                m.b_f2[:, :].unsqueeze(1).to_broadcast([P, G, F]), ALU.add).then_inc(biased.sem, 1)
                v.wait_ge(sent[k], (q - k) * (16 * G // SLOTS))
                v.tensor_copy(index[:, k, :], rows[:, k, :, C_POS].bitcast(I32))
                v.wait_ge(scaled.sem, scaled.after(q))
                v.wait_ge(biased.sem, biased.after(q))
                v.tensor_tensor(out[:, k, :, 0:F], filt[:, b, :, :], own[:, b, :, :], ALU.mult).then_inc(made.sem, 1)

            smued.start(v)
            biased.start(v)
            made.start(v)
            in_step(v, N, SLOTS, (2, make_onehot), (1, sum_smu), (0, message))

        @block.tensor
        def _(pe):
            def turn(q, k):
                pe.wait_ge(copied.sem, copied.before_reuse(q, 1))
                pe.wait_ge(onehot.sem, onehot.after(q))
                for j in range(G):
                    pe.transpose(rbf_t_ps[0:NRBF + 1, j * P:(j + 1) * P], rows[:, k, j, C_RBF:C_ONE + 1],
                                 m.ident[:, :])
                    last = pe.transpose(oh_t_ps[:, j * P:(j + 1) * P], oh[:, k % 2, j, :], m.ident[:, :])
                last.then_inc(turned.sem, 1)

            def hide(q, k):
                pe.wait_ge(copied.sem, copied.after(q))
                pe.wait_ge(smued.sem, smued.before_reuse(q, 2))
                pe.matmul(hid_ps[k % 2][:, :], m.w_f1[:, :], rbf_t[:, k, :], start=True,
                          stop=True).then_inc(hidden.sem, 1)

            def products(q, k):
                b = k % 2
                windows = window_registers(nc, pe, m.tile_window_dst, q * G, W)
                pe.wait_ge(scaled.sem, scaled.before_reuse(q, 2))
                pe.wait_ge(made.sem, made.before_reuse(q, 2))
                for j in range(G):
                    pe.matmul(own_ps[b][:, j * F:(j + 1) * F], oh_t[:, k, j * P:(j + 1) * P],
                              m.table[:, bass.ds(windows[j], 1), :].rearrange("p w f -> p (w f)"),
                              start=True, stop=True)
                pe.wait_ge(smued.sem, smued.after(q))
                for j in range(G):
                    last = pe.matmul(filt_ps[b][:, j * F:(j + 1) * F], smu[:, b, j * P:(j + 1) * P],
                                     m.w_f2[:, :], start=True, stop=True)
                last.then_inc(filtered.sem, 1)

            turned.start(pe)
            hidden.start(pe)
            filtered.start(pe)
            in_step(pe, N, SLOTS, (2, turn), (1, hide), (0, products))

        @block.scalar
        def _(act):
            def copy(q, k):
                act.wait_ge(filtered.sem, filtered.before_reuse(q, SLOTS))
                act.wait_ge(turned.sem, turned.after(q))
                act.activation(rbf_t[:, k, :], rbf_t_ps[0:NRBF + 1, :], ACT.Copy)
                act.activation(oh_t[:, k, :], oh_t_ps[:, :], ACT.Copy).then_inc(copied.sem, 1)

            def bend(q, k):
                act.wait_ge(smued.sem, smued.before_reuse(q, 2))
                act.wait_ge(hidden.sem, hidden.after(q))
                act.activation(gelu[:, k % 2, :], hid_ps[k % 2][:, :], ACT.Gelu, scale=SMU).then_inc(gelued.sem, 1)

            def scale(q, k):
                b = k % 2
                act.wait_ge(sent[k], (q - k) * (16 * G // SLOTS))
                act.activation(out[:, k, :, F:SROW], rows[:, k, :, C_EF:C_EF + CARRY], ACT.Copy)
                act.wait_ge(made.sem, made.before_reuse(q, 2))
                act.wait_ge(filtered.sem, filtered.after(q))
                for j in range(G):
                    last = act.activation(own[:, b, j, :], own_ps[b][:, j * F:(j + 1) * F], ACT.Copy,
                                          scale=rows[:, k, j, C_WEIGHT:C_WEIGHT + 1])
                last.then_inc(scaled.sem, 1)

            copied.start(act)
            gelued.start(act)
            scaled.start(act)
            in_step(act, N, SLOTS, (2, copy), (1, bend), (0, scale))

        @block.gpsimd
        def _(pool):
            def send(q, k):
                pool.wait_ge(m.blanks_s, m.blanks)
                pool.wait_ge(scaled.sem, scaled.after(q))
                wait_apart(m, pool, made.sem, made.after(q))
                for j in range(G):
                    pool.indirect_dma_start(
                        m.by_src, bass.IndirectOffsetOnAxis(ap=index[:, k, j:j + 1], axis=0),
                        out[:, k, j, :], None, bounds_check=P * TP - 1, oob_is_err=False).then_inc(sent[k], 16)

            in_step(pool, N, SLOTS, (0, send))
            for k in range(SLOTS):
                pool.wait_ge(sent[k], 16 * G * (N // SLOTS))


def sum_into_windows(nc, v, m, added, totals_ps, columns, windows, q):
    for j in range(G):
        acc = m.acc[:, bass.ds(windows[j], 1), 0:columns].rearrange("p w f -> p (w f)")
        v.wait_ge(added.sem, added.after(q) - added.per + j)
        v.tensor_tensor(acc, acc, totals_ps(j), ALU.add).then_inc(added.sem, 1)


def layer0_sums(nc, m):
    W, TP, N = m.windows, m.tiles, m.tiles // G
    with ExitStack() as ctx:
        rows = ctx.enter_context(nc.sbuf_tensor("b_rows_in", [P, SLOTS, G, SROW], F32))
        oh = ctx.enter_context(nc.sbuf_tensor("b_onehot", [P, SLOTS, G, P], F32))
        sum_ps = [ctx.enter_context(nc.psum_tensor(f"b_sum_ps{b}", [P, BANK], F32)) for b in range(SLOTS)]
        row_in = [ctx.enter_context(nc.semaphore(f"b_row_in{k}")) for k in range(SLOTS)]
        onehot = Steps(nc, ctx, "b_onehot_made")
        summed = Steps(nc, ctx, "b_summed", head=3)
        added = Steps(nc, ctx, "b_added", head=3 * G, per=G)
        block = ctx.enter_context(nc.Block())

        @block.sync
        def _(sp):
            def load(q, k):
                wait_apart(m, sp, summed.sem, summed.before_reuse(q, SLOTS))
                sp.dma_start(rows[:, k, :, :], tiles_of(m.by_src, TP, q * G, 0, SROW)).then_inc(row_in[k], 16)

            in_step(sp, N, SLOTS, (0, load))

        @block.tensor
        def _(pe):
            def sums(q, k):
                pe.wait_ge(added.sem, added.before_reuse(q, SLOTS))
                pe.wait_ge(onehot.sem, onehot.after(q))
                for j in range(G):
                    last = pe.matmul(sum_ps[k][:, j * F:(j + 1) * F], oh[:, k, j, :], rows[:, k, j, 0:F],
                                     start=True, stop=True)
                last.then_inc(summed.sem, 1)

            summed.start(pe)
            in_step(pe, N, SLOTS, (0, sums))

        @block.vector
        def _(v):
            def make_onehot(q, k):
                v.wait_ge(row_in[k], (q - k) * (16 // SLOTS) + 16)
                v.wait_ge(summed.sem, summed.before_reuse(q, SLOTS))
                v.tensor_tensor(oh[:, k, :, :], rows[:, k, :, S_SLOC:S_SLOC + 1].to_broadcast([P, G, P]),
                                m.iota_nodes[:, :].unsqueeze(1).to_broadcast([P, G, P]),
                                ALU.is_equal).then_inc(onehot.sem, 1)

            def add(q, k):
                windows = window_registers(nc, v, m.tile_window_src, q * G, W)
                v.wait_ge(summed.sem, summed.after(q))
                sum_into_windows(nc, v, m, added, lambda j: sum_ps[k][:, j * F:(j + 1) * F], F, windows, q)

            v.memset(m.acc[:, :, :], 0.0).then_inc(added.sem, added.head)
            in_step(v, N, SLOTS, (1, make_onehot), (0, add))


def layer1_edges(nc, m):
    W, TP, N = m.windows, m.tiles, m.tiles // G
    with ExitStack() as ctx:
        def sb(name, shape, dt=F32):
            return ctx.enter_context(nc.sbuf_tensor(name, shape, dt))

        def bank(name, n=1):
            return ctx.enter_context(nc.psum_tensor(name, [P, n * BANK], F32))

        rows = sb("c_rows", [P, SLOTS, G, CARRY])
        index = sb("c_index", [P, SLOTS, G], I32)
        other = sb("c_other", [P, SLOTS, G, F])
        oh = sb("c_onehot", [P, SLOTS, G, P])
        oh_t = sb("c_onehot_t", [P, 2, G * P])
        ef_t = sb("c_ef_t", [NEF, 2, G * P])
        total = sb("c_total", [P, 2, G, F])
        hid = sb("c_hid", [P, 2, G, F + 1])
        oh_t_ps, ef_t_ps = bank("c_onehot_t_ps"), bank("c_ef_t_ps")
        own_ps = [bank(f"c_own_ps{b}") for b in range(2)]
        sum_ps = [bank(f"c_sum_ps{b}", 2) for b in range(2)]
        row_in = [ctx.enter_context(nc.semaphore(f"c_row_in{k}")) for k in range(SLOTS)]
        came = [ctx.enter_context(nc.semaphore(f"c_came{k}")) for k in range(SLOTS)]
        ones = ctx.enter_context(nc.semaphore("c_ones"))
        indexed = Steps(nc, ctx, "c_indexed", head=3)
        onehot = Steps(nc, ctx, "c_onehot_made", head=3)
        turned = Steps(nc, ctx, "c_turned", head=3)
        copied = Steps(nc, ctx, "c_copied", head=1)
        owned = Steps(nc, ctx, "c_owned", head=1)
        totalled = Steps(nc, ctx, "c_totalled", head=3)
        gelued = Steps(nc, ctx, "c_gelued", head=1)
        summed = Steps(nc, ctx, "c_summed", head=3)
        added = Steps(nc, ctx, "c_added", head=G, per=G)
        block = ctx.enter_context(nc.Block())

        def sums(b, j):
            at = (j // 2) * BANK + (j % 2) * (F + 1)
            return sum_ps[b][:, at:at + F + 1]

        @block.sync
        def _(sp):
            def load(q, k):
                wait_apart(m, sp, turned.sem, turned.before_reuse(q, SLOTS))
                sp.dma_start(rows[:, k, :, :], tiles_of(m.by_src, TP, q * G, S_EF, SROW)).then_inc(row_in[k], 16)

            in_step(sp, N, SLOTS, (0, load))

        @block.gpsimd
        def _(pool):
            def gather(q, k):
                pool.wait_ge(totalled.sem, totalled.before_reuse(q, SLOTS))
                wait_apart(m, pool, indexed.sem, indexed.after(q))
                for j in range(G):
                    pool.indirect_dma_start(
                        other[:, k, j, :], None, m.b_rows,
                        bass.IndirectOffsetOnAxis(ap=index[:, k, j:j + 1], axis=0)).then_inc(came[k], 16)

            pool.memset(hid[:, :, :, F:F + 1], 1.0).then_inc(ones, 1)
            in_step(pool, N, SLOTS, (0, gather))

        @block.vector
        def _(v):
            def make_index(q, k):
                v.wait_ge(came[k], (q - k) * (16 * G // SLOTS))
                v.wait_ge(row_in[k], (q - k) * (16 // SLOTS) + 16)
                v.tensor_copy(index[:, k, :], rows[:, k, :, S_DST - S_EF]).then_inc(indexed.sem, 1)

            def make_onehot(q, k):
                v.wait_ge(summed.sem, summed.before_reuse(q, SLOTS))
                v.tensor_tensor(oh[:, k, :, :], rows[:, k, :, CARRY - 1:CARRY].to_broadcast([P, G, P]),
                                m.iota_nodes[:, :].unsqueeze(1).to_broadcast([P, G, P]),
                                ALU.is_equal).then_inc(onehot.sem, 1)

            def total_up(q, k):
                b = k % 2
                v.wait_ge(came[k], (q - k) * (16 * G // SLOTS) + 16 * G)
                v.wait_ge(gelued.sem, gelued.before_reuse(q, 2))
                v.wait_ge(owned.sem, owned.after(q))
                v.tensor_tensor(total[:, b, :, :], own_ps[b][:, :].rearrange("p (g f) -> p g f", g=G),
                                other[:, k, :, :], ALU.add).then_inc(totalled.sem, 1)

            def add(q, k):
                windows = window_registers(nc, v, m.tile_window_src, q * G, W)
                v.wait_ge(summed.sem, summed.after(q))
                sum_into_windows(nc, v, m, added, lambda j: sums(k % 2, j), F + 1, windows, q)

            v.memset(m.acc[:, :, :], 0.0).then_inc(added.sem, added.head)
            indexed.start(v)
            onehot.start(v)
            totalled.start(v)
            in_step(v, N, SLOTS, (3, make_index), (2, make_onehot), (1, total_up), (0, add))

        @block.tensor
        def _(pe):
            def turn(q, k):
                pe.wait_ge(copied.sem, copied.before_reuse(q, 1))
                pe.wait_ge(onehot.sem, onehot.after(q))
                for j in range(G):
                    pe.transpose(ef_t_ps[0:NEF, j * P:(j + 1) * P], rows[:, k, j, 0:NEF], m.ident[:, :])
                    last = pe.transpose(oh_t_ps[:, j * P:(j + 1) * P], oh[:, k, j, :], m.ident[:, :])
                last.then_inc(turned.sem, 1)

            def own(q, k):
                b = k % 2
                windows = window_registers(nc, pe, m.tile_window_src, q * G, W)
                pe.wait_ge(totalled.sem, totalled.before_reuse(q, 2))
                pe.wait_ge(copied.sem, copied.after(q))
                for j in range(G):
                    to, of = own_ps[b][:, j * F:(j + 1) * F], slice(j * P, (j + 1) * P)
                    pe.matmul(to, oh_t[:, b, of], m.table[:, bass.ds(windows[j], 1), :].rearrange("p w f -> p (w f)"),
                              start=True, stop=False)
                    last = pe.matmul(to, ef_t[:, b, of], m.w1_ef[:, :], start=False, stop=True)
                last.then_inc(owned.sem, 1)

            def sum_up(q, k):
                b = k % 2
                pe.wait_ge(added.sem, added.before_reuse(q, 2))
                pe.wait_ge(gelued.sem, gelued.after(q))
                pe.wait_ge(ones, 1)
                for j in range(G):
                    last = pe.matmul(sums(b, j), oh[:, k, j, :], hid[:, b, j, :], start=True, stop=True)
                last.then_inc(summed.sem, 1)

            turned.start(pe)
            owned.start(pe)
            summed.start(pe)
            in_step(pe, N, SLOTS, (2, turn), (1, own), (0, sum_up))

        @block.scalar
        def _(act):
            def copy(q, k):
                act.wait_ge(owned.sem, owned.before_reuse(q, 2))
                act.wait_ge(turned.sem, turned.after(q))
                act.activation(ef_t[:, k % 2, :], ef_t_ps[0:NEF, :], ACT.Copy)
                act.activation(oh_t[:, k % 2, :], oh_t_ps[:, :], ACT.Copy).then_inc(copied.sem, 1)

            def bend(q, k):
                b = k % 2
                act.wait_ge(summed.sem, summed.before_reuse(q, 2))
                act.wait_ge(totalled.sem, totalled.after(q))
                act.activation(hid[:, b, :, 0:F], total[:, b, :, :], ACT.Gelu).then_inc(gelued.sem, 1)

            copied.start(act)
            gelued.start(act)
            in_step(act, N, SLOTS, (1, copy), (0, bend))


def sums_by_dst(nc, m, layer, source, columns, weighted):
    W, TP, N = m.windows, m.tiles, m.tiles // G
    with ExitStack() as ctx:
        def sb(name, shape, dt=F32):
            return ctx.enter_context(nc.sbuf_tensor(name, shape, dt))

        def bank(name):
            return ctx.enter_context(nc.psum_tensor(name, [P, BANK], F32))

        rows = sb(f"d_rows_{layer}", [P, SLOTS, G, ROW])
        other = sb(f"d_other_{layer}", [P, SLOTS, G, columns])
        oh = sb(f"d_onehot_{layer}", [P, SLOTS, G, P])
        sum_ps = [bank(f"d_sum_ps{b}_{layer}") for b in range(2)]
        sh_t_ps = [bank(f"d_sh_t_ps{b}_{layer}") for b in range(2)]
        path_ps = [bank(f"d_path_ps{b}_{layer}") for b in range(2)]
        sh_t = sb(f"d_sh_t_{layer}", [NSH, 2, G * P])
        value = sb(f"d_value_{layer}", [P, 2, G, columns])
        row_in = [ctx.enter_context(nc.semaphore(f"d_row_in{k}_{layer}")) for k in range(SLOTS)]
        came = [ctx.enter_context(nc.semaphore(f"d_came{k}_{layer}")) for k in range(SLOTS)]
        onehot = Steps(nc, ctx, f"d_onehot_made_{layer}", head=3)
        if weighted:
            turned = Steps(nc, ctx, f"d_turned_{layer}", head=3)
            copied = Steps(nc, ctx, f"d_copied_{layer}", head=1)
            pathed = Steps(nc, ctx, f"d_pathed_{layer}", head=1)
            valued = Steps(nc, ctx, f"d_valued_{layer}", head=3)
        summed = Steps(nc, ctx, f"d_summed_{layer}", head=3)
        added = Steps(nc, ctx, f"d_added_{layer}", head=G, per=G)
        block = ctx.enter_context(nc.Block())
        users = valued if weighted else summed

        @block.sync
        def _(sp):
            def load(q, k):
                wait_apart(m, sp, came[k], (q - k) * (16 * G // SLOTS))
                if weighted:
                    sp.wait_ge(turned.sem, turned.before_reuse(q, SLOTS))
                wait_apart(m, sp, onehot.sem, onehot.before_reuse(q, SLOTS))
                sp.dma_start(rows[:, k, :, :], tiles_of(m.by_dst, TP, q * G, 0, ROW)).then_inc(row_in[k], 16)

            in_step(sp, N, SLOTS, (0, load))

        @block.gpsimd
        def _(pool):
            def gather(q, k):
                pool.wait_ge(users.sem, users.before_reuse(q, SLOTS))
                wait_apart(m, pool, row_in[k], (q - k) * (16 // SLOTS) + 16)
                for j in range(G):
                    pool.indirect_dma_start(
                        other[:, k, j, :], None, source,
                        bass.IndirectOffsetOnAxis(ap=rows[:, k, j, C_SRC:C_SRC + 1].bitcast(I32), axis=0)
                    ).then_inc(came[k], 16)

            in_step(pool, N, SLOTS, (0, gather))

        @block.vector
        def _(v):
            def make_onehot(q, k):
                v.wait_ge(row_in[k], (q - k) * (16 // SLOTS) + 16)
                v.wait_ge(summed.sem, summed.before_reuse(q, SLOTS))
                v.tensor_tensor(oh[:, k, :, :], rows[:, k, :, C_DLOC:C_DLOC + 1].to_broadcast([P, G, P]),
                                m.iota_nodes[:, :].unsqueeze(1).to_broadcast([P, G, P]),
                                ALU.is_equal).then_inc(onehot.sem, 1)

            def weigh(q, k):
                b = k % 2
                v.wait_ge(came[k], (q - k) * (16 * G // SLOTS) + 16 * G)
                v.wait_ge(summed.sem, summed.before_reuse(q, 2))
                v.wait_ge(pathed.sem, pathed.after(q))
                v.tensor_tensor(value[:, b, :, :],
                                path_ps[b][:, 0:G * columns].rearrange("p (g f) -> p g f", g=G),
                                other[:, k, :, :], ALU.mult).then_inc(valued.sem, 1)

            def add(q, k):
                windows = window_registers(nc, v, m.tile_window_dst, q * G, W)
                v.wait_ge(summed.sem, summed.after(q))
                sum_into_windows(nc, v, m, added,
                                 lambda j: sum_ps[k % 2][:, j * columns:(j + 1) * columns], columns, windows, q)

            if weighted:
                v.memset(m.acc[:, :, :], 0.0).then_inc(added.sem, added.head)
            else:
                added.start(v)
            onehot.start(v)
            if weighted:
                valued.start(v)
                in_step(v, N, SLOTS, (2, make_onehot), (1, weigh), (0, add))
            else:
                in_step(v, N, SLOTS, (2, make_onehot), (0, add))

        @block.tensor
        def _(pe):
            def turn(q, k):
                pe.wait_ge(row_in[k], (q - k) * (16 // SLOTS) + 16)
                pe.wait_ge(copied.sem, copied.before_reuse(q, 2))
                for j in range(G):
                    last = pe.transpose(sh_t_ps[k % 2][0:NSH, j * P:(j + 1) * P],
                                        rows[:, k, j, C_SH:C_SH + NSH], m.ident[:, :])
                last.then_inc(turned.sem, 1)

            def path(q, k):
                b = k % 2
                pe.wait_ge(valued.sem, valued.before_reuse(q, 2))
                pe.wait_ge(copied.sem, copied.after(q))
                for j in range(G):
                    last = pe.matmul(path_ps[b][:, j * columns:(j + 1) * columns],
                                     sh_t[:, b, j * P:(j + 1) * P], m.pick_sh[:, :], start=True, stop=True)
                last.then_inc(pathed.sem, 1)

            def sum_up(q, k):
                b = k % 2
                pe.wait_ge(added.sem, added.before_reuse(q, 2))
                if weighted:
                    pe.wait_ge(valued.sem, valued.after(q))
                    of = value[:, b, :, :]
                else:
                    pe.wait_ge(came[k], (q - k) * (16 * G // SLOTS) + 16 * G)
                    of = other[:, k, :, :]
                pe.wait_ge(onehot.sem, onehot.after(q))
                for j in range(G):
                    last = pe.matmul(sum_ps[b][:, j * columns:(j + 1) * columns], oh[:, k, j, :], of[:, j, :],
                                     start=True, stop=True)
                last.then_inc(summed.sem, 1)

            summed.start(pe)
            if weighted:
                turned.start(pe)
                pathed.start(pe)
                in_step(pe, N, SLOTS, (2, turn), (1, path), (0, sum_up))
            else:
                in_step(pe, N, SLOTS, (0, sum_up))

        @block.scalar
        def _(act):
            def copy(q, k):
                act.wait_ge(pathed.sem, pathed.before_reuse(q, 2))
                act.wait_ge(turned.sem, turned.after(q))
                act.activation(sh_t[:, k % 2, :], sh_t_ps[k % 2][0:NSH, :], ACT.Copy).then_inc(copied.sem, 1)

            if weighted:
                copied.start(act)
                in_step(act, N, SLOTS, (1, copy))


def keep_h(nc, m):
    with ExitStack() as ctx:
        relued, stored = ctx.enter_context(nc.semaphore("h_relued")), ctx.enter_context(nc.semaphore("h_stored"))
        block = ctx.enter_context(nc.Block())

        @block.scalar
        def _(act):
            act.activation(m.acc[:, :, 0:F], m.table[:, :, :], ACT.Relu).then_inc(relued, 1)

        @block.sync
        def _(sp):
            sp.wait_ge(relued, 1)
            sp.dma_start(m.h_rows.rearrange("(w p) f -> p w f", p=P), m.acc[:, :, 0:F]).then_inc(stored, 16)
            sp.wait_ge(stored, 16)


def add_sums(nc, m):
    with nc.Block() as block:
        @block.vector
        def _(v):
            v.tensor_tensor(m.x[:, :, :], m.x[:, :, :], m.acc[:, :, 0:F], ALU.add)


def store(nc, m, out):
    full, rest = m.nodes // P, m.nodes % P
    with ExitStack() as ctx:
        stored = ctx.enter_context(nc.semaphore("stored"))
        block = ctx.enter_context(nc.Block())

        @block.sync
        def _(sp):
            sp.dma_start(out[0:full * P, :].rearrange("(w p) f -> p w f", p=P), m.x[:, 0:full, :]).then_inc(stored, 16)
            if rest:
                sp.dma_start(out[full * P:m.nodes, :], m.x[0:rest, full, :]).then_inc(stored, 16)
            sp.wait_ge(stored, 16 * (1 + (rest > 0)))


def program(nc, out, nodes, edge_count, src_keys, dst_keys, edges, **w):
    with ExitStack() as ctx:
        m = Memory()
        m.nodes, m.windows = nodes, -(-nodes // (2 * P)) * 2
        m.edge_tiles, m.tiles = edge_tiles(edge_count), ordered_tiles(edge_count, m.windows)
        allocate(nc, ctx, m)
        load_constants(nc, m, w)
        count_windows(nc, m, src_keys, dst_keys)
        order_edges(nc, m, edges)
        normalise(nc, m, 0, m.table[:, :, :])
        project(nc, m, 0, m.w_in2f[:, :], F, None, F, None, 0)
        layer0_messages(nc, m)
        layer0_sums(nc, m)
        update_nodes(nc, m, 0)
        normalise(nc, m, 1, m.table[:, :, :])
        project(nc, m, 1, m.w1_ab[:, :], 2 * F, m.b1[:, :], F, m.b_rows, F)
        layer1_edges(nc, m)
        update_nodes(nc, m, 1)
        normalise(nc, m, 2, m.table[:, :, :])
        keep_h(nc, m)
        sums_by_dst(nc, m, 2, m.h_rows, F, False)
        add_sums(nc, m)
        normalise(nc, m, 3, m.table[:, :, :])
        project(nc, m, 3, m.pick_in[:, :], NPATH, None, 0, m.g_rows, NPATH)
        sums_by_dst(nc, m, 3, m.g_rows, NPATH, True)
        update_nodes(nc, m, 3)
        store(nc, m, out)


def kernel(**inputs):
    import numpy as np
    import concourse.bacc as bacc
    from concourse.bass_utils import run_bass_kernel_spmd as run

    a = {k: np.ascontiguousarray(v) for k, v in inputs.items()}
    nodes, count = a["x"].shape[0], a["src"].shape[0]
    T, windows = edge_tiles(count), -(-nodes // (2 * P)) * 2
    x = np.zeros((windows * P, F), np.float32)
    x[:nodes] = a["x"]
    edges = np.zeros((P * T, ROW), np.float32)
    edges[:count, C_RBF:C_ONE] = a["edge_attr_20"]
    edges[:, C_ONE] = 1.0
    edges[:count, C_WEIGHT] = a["edge_weight"]
    edges[:count, C_SH:C_SH + NSH] = a["edge_attr_16"]
    edges[:count, C_SRC] = a["src"].astype(np.int32, copy=False).view(np.float32)
    edges[:count, C_EF:C_EF + NEF] = a["edge_attr_32"]
    keys = np.full((2, P * T), -1, np.int32)
    keys[0, :count], keys[1, :count] = a["src"], a["dst"]
    arrays = {
        "src_keys": keys[0].reshape(P, T), "dst_keys": keys[1].reshape(P, T), "edges": edges, "x": x,
        "w_in2f_t": a["L0_gnn_W_in2f"].T, "w_f1_t": a["L0_gnn_W_f1"].T, "b_f1": a["L0_gnn_b_f1"],
        "w_f2_t": a["L0_gnn_W_f2"].T, "b_f2": a["L0_gnn_b_f2"], "w_o1_t": a["L0_gnn_W_o1"].T,
        "b_o1": a["L0_gnn_b_o1"], "w_o2_t": a["L0_gnn_W_o2"].T, "b_o2": a["L0_gnn_b_o2"],
        "w1": a["L1_gnn_W1"], "b1": a["L1_gnn_b1"], "w2": a["L1_gnn_W2"], "b2": a["L1_gnn_b2"],
        "coeff": a["L3_gnn_coeff"], "ki": a["L3_gnn_ki"], "kj": a["L3_gnn_kj"], "ko": a["L3_gnn_ko"],
    }
    arrays = {f"in_{k}": np.ascontiguousarray(v) for k, v in arrays.items()}
    nc = bacc.Bacc("TRN2", target_bir_lowering=False, num_devices=1)
    aps = {k[3:]: nc.dram_tensor(k, v.shape, mybir.dt.from_np(v.dtype), kind="ExternalInput").ap()
           for k, v in arrays.items()}
    out = nc.dram_tensor("out_0", (nodes, F), F32, kind="ExternalOutput").ap()
    program(nc, out, nodes, count, **aps)
    return run(nc, [arrays], core_ids=[0]).results[0]["out_0"]
```

```python
from contextlib import ExitStack

import concourse.bass as bass
from concourse import mybir

F32 = mybir.dt.float32
BF16 = mybir.dt.bfloat16
F16 = mybir.dt.float16
I32 = mybir.dt.int32
I16 = mybir.dt.int16
ALU = mybir.AluOpType
ACT = mybir.ActivationFunctionType
AX = mybir.AxisListType

P = 128
F = 128
G = 4
SLOTS = 4
BODY = G * SLOTS
DEEP = 8
BANK = 512
NRBF, NEF, NSH, NPATH = 20, 32, 16, 64

C_RBF, C_ONE, C_WEIGHT, C_SH = 0, NRBF, NRBF + 1, NRBF + 2
C_SRC = C_SH + NSH
C_POS = C_SRC + 1
C_DLOC = C_POS + 1
C_EF = C_DLOC + 1
C_DST = C_EF + NEF
C_SLOC = C_DST + 1
ROW = C_SLOC + 2
CARRY = C_SLOC + 1 - C_EF
S_EF, S_DST, S_SLOC = F, F + NEF, F + NEF + 1
SROW = F + CARRY

FAR = float(1 << 22)
SMU = 2.5 * 0.99 * 2.0 ** 0.5
SMU_LIN = 0.01 / 0.99 * SMU
EPS = 1e-5


def edge_tiles(edges):
    return -(-edges // (P * BODY)) * BODY


def ordered_tiles(edges, windows):
    return -(-((edges + windows * (P - 1)) // P) // (G * DEEP)) * (G * DEEP)


class Memory:
    pass


def parts_of(tensor, *columns):
    flat, parts, at = tensor[:, :, :].rearrange("p w f -> p (w f)"), [], 0
    for n in columns:
        assert at + n <= flat.shape[1]
        parts.append(flat[:, at:at + n])
        at += n
    return parts


def allocate(nc, ctx, m):
    def sb(name, shape, dt=F32):
        return ctx.enter_context(nc.sbuf_tensor(name, shape, dt))

    W = m.windows
    m.blanks_d = ctx.enter_context(nc.semaphore("blanks_d"))
    m.blanks_s = ctx.enter_context(nc.semaphore("blanks_s"))
    m.norm_chain, m.norm_rooted = (ctx.enter_context(nc.semaphore(n)) for n in ("norm_chain", "norm_rooted"))
    m.project_steps = [Steps(nc, ctx, f"p_{n}", head)
                       for n, head in (("relued", 0), ("turned", 1), ("copied", 1), ("multiplied", 1), ("taken", 1))]
    m.waits_apart = {e.engine: ctx.enter_context(nc.semaphore(f"waits_apart_{n}"))
                     for n, e in (("sp", nc.sync), ("pool", nc.gpsimd), ("pe", nc.tensor))}
    m.blanks = 16 * (m.tiles // BODY)
    m.row_in, m.moved = Moves(nc, ctx, "row_in", DEEP), Moves(nc, ctx, "moved", DEEP)
    m.x = sb("x_nodes", [P, W, F])
    m.table = sb("node_table", [P, W, F])
    m.acc = sb("segment_sums", [P, W, F + 1])
    T = m.edge_tiles
    keys, pre_dst, pre_src, windows, some_slots = parts_of(m.acc, 2 * T, T, T, 2 * T, T)
    m.some_slots = some_slots[0:W, :].bitcast(I32)
    m.keys = keys.bitcast(I32).rearrange("p (k t) -> p k t", k=2)
    m.key_windows = windows.rearrange("p (k t) -> p k t", k=2)
    m.pre_dst, m.pre_src = pre_dst[0:W, :], pre_src[0:W, :]
    parts = parts_of(m.table, BODY * ROW, BODY * SROW, 2 * T, m.tiles, m.tiles, m.tiles // 2)
    m.blank_d, m.blank_s = (p.rearrange("p (t c) -> p t c", t=BODY) for p in parts[:2])
    m.shifted = parts[2].bitcast(I32).rearrange("p (k t) -> p k t", k=2)
    m.next_slot = parts[2][0:W, :].bitcast(F16).rearrange("w (k t c) -> w k t c", k=2, c=2)
    assert m.tiles <= 2048
    m.tile_iota, m.tile_iota_f = parts[3][0:W, :].bitcast(I32), parts[4][0:W, :]
    m.started = parts[5][0:W, :].bitcast(BF16)
    m.iota_nodes = sb("iota_nodes", [P, P])
    m.iota_windows = sb("iota_windows", [P, W])
    m.ident = sb("ident", [P, P])
    m.ident_bf = sb("ident_bf", [P, P], BF16)
    m.before_bf = sb("before_bf", [P, P], BF16)
    m.before = sb("before", [P, P])
    m.ones_bf = sb("ones_bf", [P, 1], BF16)
    m.ones = sb("ones", [P, 1])
    m.eps = sb("eps", [P, 1])
    m.tile_window_dst = sb("tile_window_dst", [1, m.tiles], I16)
    m.tile_window_src = sb("tile_window_src", [1, m.tiles], I16)
    m.mean = sb("mean", [P, W])
    m.rstd = sb("rstd", [P, W])
    m.w_in2f = sb("w_in2f", [F, F])
    m.w_f1 = sb("w_f1", [NRBF + 1, F])
    m.w_f2 = sb("w_f2", [F, F])
    m.b_f2 = sb("b_f2", [P, F])
    m.w_o1 = sb("w_o1", [F, F])
    m.b_o1 = sb("b_o1", [F, 1])
    m.b_o1_gelu = sb("b_o1_gelu", [F, 1])
    m.b_o1_lin = sb("b_o1_lin", [F, 1])
    m.w_o2 = sb("w_o2", [F, F])
    m.b_o2 = sb("b_o2", [P, F])
    m.w1_ab = sb("w1_ab", [F, 2 * F])
    m.w1_ef = sb("w1_ef", [NEF, F])
    m.b1 = sb("b1", [P, F])
    m.w2 = sb("w2", [F, F])
    m.b2 = sb("b2", [P, F])
    m.pick_in = sb("pick_in", [F, NPATH])
    m.pick_sh = sb("pick_sh", [NSH, NPATH])
    m.pick_out = sb("pick_out", [NPATH, F])

    def dram(name, shape):
        return nc.dram_tensor(name, shape, F32, kind="Internal").ap()

    m.by_dst = dram("edges_by_dst", [P * m.tiles, ROW])
    m.by_src = dram("edges_by_src", [P * m.tiles, SROW])
    m.b_rows = dram("b_rows", [W * P, F])
    m.h_rows = dram("h_rows", [W * P, F])
    m.g_rows = dram("g_rows", [W * P, NPATH])


def tiles_of(table, tiles, t, first, last):
    return table.rearrange("(p t) c -> p t c", t=tiles)[:, bass.ds(t, G), first:last]


def window_registers(nc, eng, tile_window, t, windows):
    _, got = nc.values_load_multi_w_load_instructions(
        tile_window[0:1, bass.ds(t, G)], engines=[eng.engine], min_val=0, max_val=windows - 1,
        skip_runtime_bounds_check_because="each entry is a count of 1 to `windows` bases, less one")
    return got


class Steps:

    def __init__(self, nc, ctx, name, head=0, per=1):
        self.sem, self.first, self.per = ctx.enter_context(nc.semaphore(name)), head, per
        self.head = head

    def after(self, q):
        return q * self.per + (self.head + self.per)

    def before_reuse(self, q, slots):
        return q * self.per + (self.head + self.per - self.per * slots)

    def start(self, eng):
        eng.sem_inc(self.sem, self.first)

    def again(self, groups):
        self.head += self.per * groups + self.first


class Moves:

    def __init__(self, nc, ctx, name, slots):
        self.sems = [ctx.enter_context(nc.semaphore(f"{name}{k}")) for k in range(slots)]
        self.head = [0] * slots

    def use(self, slots, per):
        self.slots, self.per = slots, 16 * per

    def before(self, q, k):
        return (q - k) * (self.per // self.slots) + self.head[k]

    def after(self, q, k):
        return (q - k) * (self.per // self.slots) + (self.head[k] + self.per)

    def again(self, groups):
        assert groups % self.slots == 0
        for k in range(self.slots):
            self.head[k] += self.per * (groups // self.slots)


def wait_apart(m, eng, sem, value):
    eng.wait_ge(sem, value).then_inc(m.waits_apart[eng.engine], 1)


def in_step(eng, groups, slots, *stages):
    most = max(lead for lead, _ in stages)

    def step(q, at):
        for lead, emit in stages:
            if not isinstance(q, int) or 0 <= q + lead < groups:
                emit(q + lead, (at + lead) % slots)

    for q in range(-most, 0):
        step(q, q)
    looped = max(groups - most, 0) // slots * slots
    if looped:
        with eng.Fori(0, looped // slots) as turn:
            for k in range(slots):
                step(turn * slots + k, k)
    for q in range(looped, groups):
        step(q, q)


def load_constants(nc, m, w):
    with ExitStack() as ctx:
        def sem(name):
            return ctx.enter_context(nc.semaphore(name))

        loaded, made, cast, dve = sem("c_loaded"), sem("c_made"), sem("c_cast"), sem("c_dve")
        iota_i = ctx.enter_context(nc.sbuf_tensor("iota_i", [P, P], I32))
        ki = ctx.enter_context(nc.sbuf_tensor("ki", [F, NPATH], I32))
        kj = ctx.enter_context(nc.sbuf_tensor("kj", [NSH, NPATH], I32))
        ko = ctx.enter_context(nc.sbuf_tensor("ko", [NPATH, 1], I32))
        ki_f = ctx.enter_context(nc.sbuf_tensor("ki_f", [F, NPATH], F32))
        kj_f = ctx.enter_context(nc.sbuf_tensor("kj_f", [NSH, NPATH], F32))
        ko_f = ctx.enter_context(nc.sbuf_tensor("ko_f", [NPATH, 1], F32))
        place = ctx.enter_context(nc.sbuf_tensor("place", [P, 1], F32))
        coeff = ctx.enter_context(nc.sbuf_tensor("coeff", [NSH, NPATH], F32))
        block = ctx.enter_context(nc.Block())

        def rows(v, n):
            return v.rearrange("(a n) -> a n", a=1).to_broadcast([n, v.shape[0]])

        loads = [
            (m.w_in2f[:, :], w["w_in2f_t"]), (m.w_f1[0:NRBF, :], w["w_f1_t"]),
            (m.w_f1[NRBF:NRBF + 1, :], rows(w["b_f1"], 1)),
            (m.w_f2[:, :], w["w_f2_t"]), (m.b_f2[:, :], rows(w["b_f2"], P)),
            (m.w_o1[:, :], w["w_o1_t"]), (m.b_o1[:, :], w["b_o1"].rearrange("(n a) -> n a", a=1)),
            (m.w_o2[:, :], w["w_o2_t"]), (m.b_o2[:, :], rows(w["b_o2"], P)),
            (m.w1_ab[:, 0:F], w["w1"][0:F, :]), (m.w1_ab[:, F:2 * F], w["w1"][F:2 * F, :]),
            (m.w1_ef[:, :], w["w1"][2 * F:2 * F + NEF, :]), (m.b1[:, :], rows(w["b1"], P)),
            (m.w2[:, :], w["w2"]), (m.b2[:, :], rows(w["b2"], P)),
            (ki[:, :], rows(w["ki"], F)), (kj[:, :], rows(w["kj"], NSH)),
            (ko[:, :], w["ko"].rearrange("(n a) -> n a", a=1)), (coeff[:, :], rows(w["coeff"], NSH)),
            (m.x[:, :, :], w["x"].rearrange("(w p) f -> p w f", p=P)),
        ]

        @block.sync
        def _(sp):
            for to, of in loads:
                sp.dma_start(to, of).then_inc(loaded, 16)
            sp.wait_ge(loaded, 16 * len(loads))

        @block.gpsimd
        def _(pool):
            pool.iota(iota_i[:, :], pattern=[[1, P]], base=0, channel_multiplier=0).then_inc(made, 1)
            pool.memset(m.ident[:, :], 0.0).then_inc(made, 1)
            pool.memset(m.before[:, :], 1.0).then_inc(made, 1)
            pool.memset(m.ones_bf[:, :], 1.0)
            pool.memset(m.ones[:, :], 1.0)
            pool.memset(m.eps[:, :], EPS)
            pool.wait_ge(made, 3)
            pool.affine_select(out=m.ident[:, :], in_=m.ident[:, :], compare_op=ALU.not_equal, fill=1.0,
                               base=0, pattern=[[-1, P]], channel_multiplier=1).then_inc(made, 1)
            pool.affine_select(out=m.before[:, :], in_=m.before[:, :], compare_op=ALU.is_gt, fill=0.0,
                               base=0, pattern=[[1, P]], channel_multiplier=-1).then_inc(made, 1)

        @block.vector
        def _(v):
            v.wait_ge(made, 5)
            v.tensor_copy(m.iota_nodes[:, :], iota_i[:, :]).then_inc(cast, 1)
            v.tensor_copy(m.iota_windows[:, :], iota_i[:, 0:m.windows])
            v.tensor_copy(m.ident_bf[:, :], m.ident[:, :])
            v.tensor_copy(m.before_bf[:, :], m.before[:, :])
            v.wait_ge(cast, 1)
            v.tensor_tensor(m.table[:, 0, :], m.iota_nodes[:, :], m.ident[:, :], ALU.mult).then_inc(dve, 1)
            v.wait_ge(dve, 1)
            v.tensor_reduce(place[:, :], m.table[:, 0, :], AX.X, ALU.add).then_inc(dve, 1)
            v.wait_ge(loaded, 16 * len(loads))
            v.tensor_copy(ki_f[:, :], ki[:, :])
            v.tensor_copy(kj_f[:, :], kj[:, :])
            v.tensor_copy(ko_f[:, :], ko[:, :]).then_inc(dve, 1)
            v.tensor_scalar(m.w_f2[:, :], m.w_f2[:, :], 0.99 / SMU, None, ALU.mult)
            v.tensor_scalar(m.w_o2[:, :], m.w_o2[:, :], 0.99 / SMU, None, ALU.mult)
            v.tensor_scalar(m.b_o1_gelu[:, :], m.b_o1[:, :], SMU, None, ALU.mult)
            v.tensor_scalar(m.b_o1_lin[:, :], m.b_o1[:, :], SMU_LIN, None, ALU.mult)
            v.wait_ge(dve, 3)
            v.tensor_scalar(m.pick_in[:, :], ki_f[:, :], place[:, 0:1], None, ALU.is_equal)
            v.scalar_tensor_tensor(m.pick_sh[:, :], kj_f[:, :], place[0:NSH, 0:1], coeff[:, :],
                                   ALU.is_equal, ALU.mult)
            v.tensor_scalar(m.pick_out[:, :], m.iota_nodes[0:NPATH, :], ko_f[:, 0:1], None, ALU.is_equal)


def count_windows(nc, m, src_keys, dst_keys):
    W, T, TP = m.windows, m.edge_tiles, m.tiles
    with ExitStack() as ctx:
        def sem(name):
            return ctx.enter_context(nc.semaphore(name))

        keys_in, keys_done, split = sem("k_keys_in"), sem("k_keys_done"), sem("k_split")
        onehot, counted, scan = Steps(nc, ctx, "k_onehot"), Steps(nc, ctx, "k_counted", 1), sem("k_scan")
        based, tabled, blank_made = sem("k_based"), sem("k_tabled"), sem("k_blank_made")
        iotas, started_ready = sem("k_iotas"), sem("k_started_ready")
        halved, placed = sem("k_halved"), sem("k_placed")
        shifted, tile_iota, tile_iota_f, started = m.shifted, m.tile_iota, m.tile_iota_f, m.started
        oh = ctx.enter_context(nc.sbuf_tensor("count_onehot", [P, 2, 2, G, W], BF16))
        blank_d, blank_s, blanks_d, blanks_s = m.blank_d, m.blank_s, m.blanks_d, m.blanks_s
        n_i = ctx.enter_context(nc.sbuf_tensor("n_i", [W, 2], I32))
        n_t = ctx.enter_context(nc.sbuf_tensor("n_t", [W, 2], I32))
        n_f = ctx.enter_context(nc.sbuf_tensor("n_f", [W, 2], F32))
        base = ctx.enter_context(nc.sbuf_tensor("base", [W, 2], F32))
        base_slot = ctx.enter_context(nc.sbuf_tensor("base_slot", [W, 2], F32))
        banks = -(-max(T, TP) // BANK)
        pres = (m.pre_dst, m.pre_src)
        tile_windows = (m.tile_window_dst, m.tile_window_src)

        counts = [ctx.enter_context(nc.psum_tensor(f"counts{k}", [P, banks * BANK], F32)) for k in range(2)]
        with nc.Block() as block:
            @block.sync
            def _(sp):
                sp.dma_start(m.keys[:, 0, :], dst_keys).then_inc(keys_in, 16)
                sp.dma_start(m.keys[:, 1, :], src_keys).then_inc(keys_in, 16)
                sp.wait_ge(blank_made, 2)
                with sp.Fori(0, TP // BODY) as t:
                    sp.dma_start(m.by_dst.rearrange("(p t) c -> p t c", t=TP)[:, bass.ds(t * BODY, BODY), :],
                                 blank_d[:, :, :]).then_inc(blanks_d, 16)
                with sp.Fori(0, TP // BODY) as t:
                    sp.dma_start(m.by_src.rearrange("(p t) c -> p t c", t=TP)[:, bass.ds(t * BODY, BODY), :],
                                 blank_s[:, :, :]).then_inc(blanks_s, 16)

            @block.gpsimd
            def _(pool):
                pool.memset(blank_d[:, :, :], 0.0)
                pool.memset(blank_s[:, :, :], 0.0)
                pool.iota(tile_iota[:, :], pattern=[[1, TP]], base=0, channel_multiplier=0).then_inc(iotas, 1)
                pool.wait_ge(iotas, 1)
                pool.memset(blank_d[:, :, C_DLOC:C_DLOC + 1], -1.0)
                pool.memset(blank_d[:, :, C_SLOC:C_SLOC + 1], -1.0)
                pool.memset(blank_d[:, :, C_POS:C_POS + 1].bitcast(I32), int(FAR)).then_inc(blank_made, 1)
                pool.memset(blank_s[:, :, S_SLOC:S_SLOC + 1], -1.0).then_inc(blank_made, 1)

            @block.vector
            def _(v):
                v.wait_ge(keys_in, 32)
                v.tensor_scalar(shifted[:, :, :], m.keys, 7, None, ALU.arith_shift_right).then_inc(split, 1)
                v.wait_ge(split, 1)
                v.tensor_copy(m.key_windows, shifted[:, :, :]).then_inc(split, 1)
                v.wait_ge(split, 2)

                def make_onehot(q, k):
                    v.wait_ge(counted.sem, counted.before_reuse(q, 2))
                    v.tensor_tensor(
                        oh[:, k, :, :, :],
                        m.key_windows[:, :, bass.ds(q * G, G)].unsqueeze(3).to_broadcast([P, 2, G, W]),
                        m.iota_windows[:, :].unsqueeze(1).unsqueeze(1).to_broadcast([P, 2, G, W]),
                        ALU.is_equal).then_inc(onehot.sem, 1)

                in_step(v, T // G, 2, (0, make_onehot))

            @block.tensor
            def _(pe):
                def count(q, k):
                    pe.wait_ge(onehot.sem, onehot.after(q))
                    for key in range(2):
                        for j in range(G):
                            last = pe.matmul(counts[key][0:W, bass.ds(q * G + j, 1)], oh[:, k, key, j, :],
                                             m.ones_bf[:, 0:1], start=True, stop=True)
                    last.then_inc(counted.sem, 1)

                counted.start(pe)
                in_step(pe, T // G, 2, (0, count))

        with nc.Block() as block:
            @block.vector
            def _(v):
                v.tensor_copy(tile_iota_f[:, :], tile_iota[:, :]).then_inc(iotas, 1)
                for k, pre in enumerate(pres):
                    v.tensor_tensor_scan(pre, m.ones[0:W, 0:1].to_broadcast([W, T]), counts[k][0:W, 0:T],
                                         0.0, ALU.mult, ALU.add).then_inc(scan, 1)
                v.wait_ge(scan, 2)
                for k, pre in enumerate(pres):
                    v.tensor_scalar(n_i[:, k:k + 1], pre[:, T - 1:T], float(P - 1), None, ALU.add).then_inc(scan, 1)
                v.wait_ge(scan, 4)
                v.tensor_scalar(n_t[:, :], n_i[:, :], 7, None, ALU.arith_shift_right).then_inc(scan, 1)
                v.wait_ge(scan, 5)
                v.tensor_copy(n_f[:, :], n_t[:, :]).then_inc(scan, 1)
                for k, pre in enumerate(pres):
                    v.tensor_tensor(pre, pre, counts[k][0:W, 0:T], ALU.subtract).then_inc(scan, 1)
                v.wait_ge(scan, 8)

        with nc.Block() as block:
            @block.tensor
            def _(pe):
                pe.matmul(counts[0][0:W, 0:2], m.before[0:W, 0:W], n_f[:, :], start=True, stop=True).then_inc(based, 1)
                for k in range(2):
                    pe.wait_ge(started_ready, k + 1)
                    for c in range(0, TP, BANK):
                        n = min(BANK, TP - c)
                        last = pe.matmul(counts[1 - k][0:1, c:c + n], m.ones_bf[0:W, 0:1], started[:, c:c + n],
                                         start=True, stop=True)
                    last.then_inc(tabled, 1)

            @block.vector
            def _(v):
                v.wait_ge(based, 1)
                v.tensor_copy(base[:, :], counts[0][0:W, 0:2]).then_inc(based, 1)
                v.wait_ge(based, 2)
                v.tensor_scalar(base_slot[:, :], base[:, :], float(P), None, ALU.mult).then_inc(based, 1)
                v.wait_ge(based, 3)
                for k, pre in enumerate(pres):
                    v.tensor_scalar(pre, pre, base_slot[:, k:k + 1], None, ALU.add).then_inc(based, 1)
                    if k:
                        v.wait_ge(tabled, k)
                    v.tensor_scalar(started[:, :], tile_iota_f[:, :], base[:, k:k + 1], None,
                                    ALU.is_ge).then_inc(started_ready, 1)
                n = 0
                for k, pre in enumerate(pres):
                    for half, (op, by) in enumerate(((ALU.arith_shift_right, 7), (ALU.bitwise_and, P - 1))):
                        if not half:
                            v.wait_ge(based, 4 + k)
                            v.wait_ge(placed, 3 * k)
                            v.tensor_copy(pre.bitcast(I32), pre).then_inc(placed, 1)
                        v.wait_ge(placed, n + k + 1)
                        v.tensor_scalar(m.some_slots, pre.bitcast(I32), by, None, op).then_inc(halved, 1)
                        v.wait_ge(halved, n + 1)
                        v.tensor_copy(m.next_slot[:, k, :, half], m.some_slots).then_inc(placed, 1)
                        n += 1
                for k, tile_window in enumerate(tile_windows):
                    v.wait_ge(tabled, k + 1)
                    v.tensor_scalar(tile_window[:, :], counts[1 - k][0:1, 0:TP], -1.0, None, ALU.add)


def order_edges(nc, m, edges):
    W, T, TP = m.windows, m.edge_tiles, m.tiles
    with ExitStack() as ctx:
        def sb(name, shape, dt=F32):
            return ctx.enter_context(nc.sbuf_tensor(name, shape, dt))

        def bank(name, shape, dt=F32):
            return ctx.enter_context(nc.psum_tensor(name, shape, dt))

        rows = sb("o_rows", [P, SLOTS, G, ROW])
        index = sb("o_index", [P, SLOTS, G], I32)
        oh = sb("o_onehot", [P, 2, 2, G, W], BF16)
        oh_t = sb("o_onehot_t", [W, 2, 2 * G * P], BF16)
        place_in = sb("o_place_in", [P, 2, 2, G])
        prod = sb("o_prod", [P, 2, G, W])
        rank = sb("o_rank", [P, 2, 2, G])
        slot_i = sb("o_slot_i", [P, 2, G], I32)
        lo = sb("o_lo", [P, 2, G], I32)
        hi = sb("o_hi", [P, 2, G], I32)
        row = sb("o_row", [P, 2, G])
        none = sb("o_none", [P, G])
        rank_ps = [[bank(f"o_rank_ps{b}{k}", [P, BANK]) for k in range(2)] for b in range(2)]
        oh_t_ps = bank("o_onehot_t_ps", [P, 2 * BANK], BF16)
        look_ps = [bank(f"o_look_ps{b}", [P, BANK]) for b in range(2)]

        row_in = [ctx.enter_context(nc.semaphore(f"o_row_in{k}")) for k in range(SLOTS)]
        sent = [ctx.enter_context(nc.semaphore(f"o_sent{k}")) for k in range(SLOTS)]
        onehot = Steps(nc, ctx, "o_onehot_made")
        turned = Steps(nc, ctx, "o_turned", head=1)
        copied = Steps(nc, ctx, "o_copied", head=1)
        looked = Steps(nc, ctx, "o_looked", head=1)
        multiplied = Steps(nc, ctx, "o_multiplied", head=1)
        ranked = Steps(nc, ctx, "o_ranked", head=1)
        slotted = Steps(nc, ctx, "o_slotted", head=1)
        summed = Steps(nc, ctx, "o_summed", head=1)
        halved = Steps(nc, ctx, "o_halved")
        rowed = Steps(nc, ctx, "o_rowed")
        placed = Steps(nc, ctx, "o_placed", head=1)
        block = ctx.enter_context(nc.Block())

        @block.sync
        def _(sp):
            def load(q, k):
                wait_apart(m, sp, sent[k], (q - k) * (16 * G // SLOTS))
                sp.dma_start(rows[:, k, :, :], tiles_of(edges, T, q * G, 0, ROW)).then_inc(row_in[k], 16)

            in_step(sp, T // G, SLOTS, (0, load))
            sp.wait_ge(m.blanks_s, m.blanks)

        @block.vector
        def _(v):
            def make_onehot(q, k):
                v.wait_ge(turned.sem, turned.before_reuse(q, 2))
                v.wait_ge(multiplied.sem, multiplied.before_reuse(q, 2))
                v.tensor_tensor(
                    oh[:, k % 2, :, :, :],
                    m.key_windows[:, :, bass.ds(q * G, G)].unsqueeze(3).to_broadcast([P, 2, G, W]),
                    m.iota_windows[:, :].unsqueeze(1).unsqueeze(1).to_broadcast([P, 2, G, W]),
                    ALU.is_equal).then_inc(onehot.sem, 1)

            def multiply(q, k):
                b = k % 2
                v.wait_ge(ranked.sem, ranked.before_reuse(q, 1))
                v.wait_ge(turned.sem, turned.after(q))
                for key in range(2):
                    last = v.tensor_tensor(prod[:, key, :, :],
                                           rank_ps[b][key][:, 0:G * W].rearrange("p (g w) -> p g w", g=G),
                                           oh[:, b, key, :, :], ALU.mult)
                last.then_inc(multiplied.sem, 1)

            def reduce(q, k):
                v.wait_ge(summed.sem, summed.before_reuse(q, 2))
                v.wait_ge(multiplied.sem, multiplied.after(q))
                v.tensor_reduce(rank[:, k % 2, :, :], prod[:, :, :, :], AX.X, ALU.add).then_inc(ranked.sem, 1)

            def looked_up(q, k):
                return look_ps[k % 2][:, 0:4 * G].rearrange("p (k g c) -> p k g c", k=2, c=2)

            def add_rank(q, k):
                v.wait_ge(slotted.sem, slotted.before_reuse(q, 2))
                v.wait_ge(ranked.sem, ranked.after(q))
                v.wait_ge(looked.sem, looked.after(q))
                v.tensor_tensor(place_in[:, k % 2, :, :], rank[:, k % 2, :, :], looked_up(q, k)[:, :, :, 1],
                                ALU.add).then_inc(summed.sem, 1)

            def find_slot(q, k):
                v.wait_ge(halved.sem, halved.after(q) - 1)
                v.wait_ge(summed.sem, summed.after(q))
                v.scalar_tensor_tensor(slot_i[:, :, :], looked_up(q, k)[:, :, :, 0], float(P),
                                       place_in[:, k % 2, :, :], ALU.mult, ALU.add).then_inc(slotted.sem, 1)

            def fill_in(q, k):
                keys, windows = m.keys[:, :, bass.ds(q * G, G)], m.key_windows[:, :, bass.ds(q * G, G)]
                v.wait_ge(row_in[k], (q - k) * (16 // SLOTS) + 16)
                v.scalar_tensor_tensor(
                    rows[:, k, :, C_DLOC:C_SLOC + 1:C_SLOC - C_DLOC].rearrange("p g k -> p k g"),
                    windows, -float(P), keys, ALU.mult, ALU.add)
                v.tensor_copy(rows[:, k, :, C_DST], keys[:, 0, :])
                v.wait_ge(placed.sem, placed.before_reuse(q, 1))
                v.tensor_scalar(none[:, :], windows[:, 0, :], 0.0, FAR, ALU.is_lt, ALU.mult)

            def halve(q, k):
                v.wait_ge(rowed.sem, rowed.after(q) - 1)
                v.wait_ge(slotted.sem, slotted.after(q))
                v.tensor_scalar(lo[:, :, :], slot_i[:, :, :], P - 1, None, ALU.bitwise_and)
                v.tensor_scalar(hi[:, :, :], slot_i[:, :, :], 7, None, ALU.arith_shift_right).then_inc(halved.sem, 1)

            def make_row(q, k):
                v.wait_ge(placed.sem, placed.before_reuse(q, 1))
                v.wait_ge(halved.sem, halved.after(q))
                v.scalar_tensor_tensor(row[:, :, :], lo[:, :, :], float(TP), hi[:, :, :], ALU.mult,
                                       ALU.add).then_inc(rowed.sem, 1)

            def place(q, k):
                v.wait_ge(rowed.sem, rowed.after(q))
                v.tensor_copy(rows[:, k, :, C_POS].bitcast(I32), row[:, 1, :])
                v.tensor_tensor(index[:, k, :], row[:, 0, :], none[:, :], ALU.add).then_inc(placed.sem, 1)

            multiplied.start(v)
            ranked.start(v)
            slotted.start(v)
            summed.start(v)
            placed.start(v)
            in_step(v, T // G, SLOTS, (2, make_onehot), (0, add_rank), (0, fill_in), (0, find_slot),
                    (1, multiply), (0, halve), (1, reduce), (0, make_row), (0, place))

        @block.tensor
        def _(pe):
            def rank_and_turn(q, k):
                b = k % 2
                pe.wait_ge(multiplied.sem, multiplied.before_reuse(q, 2))
                pe.wait_ge(onehot.sem, onehot.after(q))
                for key in range(2):
                    pe.matmul(rank_ps[b][key][:, 0:G * W], m.before_bf[:, :],
                              oh[:, b, key, :, :].rearrange("p g w -> p (g w)"), start=True, stop=True)
                pe.wait_ge(copied.sem, copied.before_reuse(q, 1))
                for key in range(2):
                    for j in range(G):
                        c = (key * G + j) * P
                        last = pe.transpose(oh_t_ps[0:W, c:c + P], oh[:, b, key, j, :], m.ident_bf[:, :])
                last.then_inc(turned.sem, 1)

            def look_up(q, k):
                b = k % 2
                pe.wait_ge(slotted.sem, slotted.before_reuse(q, 2))
                pe.wait_ge(copied.sem, copied.after(q))
                for key in range(2):
                    for j in range(G):
                        c = key * G + j
                        last = pe.matmul(look_ps[b][:, 2 * c:2 * c + 2], oh_t[:, b, c * P:(c + 1) * P],
                                         m.next_slot[:, key, bass.ds(q * G + j, 1), :].rearrange("w t c -> w (t c)"),
                                         start=True, stop=True)
                last.then_inc(looked.sem, 1)

            turned.start(pe)
            looked.start(pe)
            in_step(pe, T // G, SLOTS, (2, rank_and_turn), (1, look_up))

        @block.scalar
        def _(act):
            def copy(q, k):
                act.wait_ge(looked.sem, looked.before_reuse(q, 2))
                act.wait_ge(turned.sem, turned.after(q))
                act.activation(oh_t[:, k % 2, :], oh_t_ps[0:W, :], ACT.Copy).then_inc(copied.sem, 1)

            copied.start(act)
            in_step(act, T // G, SLOTS, (1, copy))

        @block.gpsimd
        def _(pool):
            def send(q, k):
                pool.wait_ge(m.blanks_d, m.blanks)
                wait_apart(m, pool, placed.sem, placed.after(q))
                for j in range(G):
                    pool.indirect_dma_start(
                        m.by_dst, bass.IndirectOffsetOnAxis(ap=index[:, k, j:j + 1], axis=0),
                        rows[:, k, j, :], None, bounds_check=P * TP - 1, oob_is_err=False).then_inc(sent[k], 16)

            in_step(pool, T // G, SLOTS, (0, send))
            for k in range(SLOTS):
                pool.wait_ge(sent[k], 16 * G * (T // G // SLOTS))


def normalise(nc, m, layer, out):
    W = m.windows
    with ExitStack() as ctx:
        chain, rooted = m.norm_chain, m.norm_rooted
        done = 7 * layer
        var = ctx.enter_context(nc.sbuf_tensor(f"n_var_{layer}", [P, W], F32))
        std = ctx.enter_context(nc.sbuf_tensor(f"n_std_{layer}", [P, W], F32))
        spare = m.acc[:, :, 0:F]
        block = ctx.enter_context(nc.Block())

        def spread(a):
            return a[:, :].unsqueeze(2).to_broadcast([P, W, F])

        @block.vector
        def _(v):
            v.tensor_reduce(m.mean[:, :], m.x[:, :, :], AX.X, ALU.add).then_inc(chain, 1)
            v.wait_ge(chain, done + 1)
            v.tensor_scalar(m.mean[:, :], m.mean[:, :], 1.0 / F, None, ALU.mult).then_inc(chain, 1)
            v.wait_ge(chain, done + 2)
            v.tensor_tensor(out, m.x[:, :, :], spread(m.mean), ALU.subtract).then_inc(chain, 1)
            v.wait_ge(chain, done + 3)
            v.tensor_tensor(spare, out, out, ALU.mult).then_inc(chain, 1)
            v.wait_ge(chain, done + 4)
            v.tensor_reduce(var[:, :], spare, AX.X, ALU.add).then_inc(chain, 1)
            v.wait_ge(rooted, layer + 1)
            v.reciprocal(m.rstd[:, :], std[:, :]).then_inc(chain, 1)
            v.wait_ge(chain, done + 6)
            v.tensor_tensor(out, out, spread(m.rstd), ALU.mult).then_inc(chain, 1)

        @block.scalar
        def _(act):
            act.wait_ge(chain, done + 5)
            act.activation(std[:, :], var[:, :], ACT.Sqrt, bias=m.eps[:, 0:1], scale=1.0 / F).then_inc(rooted, 1)


def project(nc, m, layer, weights, columns, bias, kept, rows_out, out_columns):
    W, PAIR = m.windows, 2
    with ExitStack() as ctx:
        def sb(name, shape, dt=F32):
            return ctx.enter_context(nc.sbuf_tensor(name, shape, dt))

        h = sb(f"p_h_{layer}", [P, PAIR, F])
        h_t = sb(f"p_h_t_{layer}", [F, PAIR, P])
        away = sb(f"p_away_{layer}", [P, PAIR, out_columns or 2])
        turn_ps = [ctx.enter_context(nc.psum_tensor(f"p_turn{b}_{layer}", [P, BANK], F32)) for b in range(PAIR)]
        prod_ps = [ctx.enter_context(nc.psum_tensor(f"p_prod{b}_{layer}", [P, BANK], F32)) for b in range(PAIR)]
        relued, turned, copied, multiplied, taken = m.project_steps
        stored = [ctx.enter_context(nc.semaphore(f"p_stored{b}_{layer}")) for b in range(PAIR if out_columns else 0)]
        block = ctx.enter_context(nc.Block())

        @block.scalar
        def _(act):
            def relu(w, b):
                act.wait_ge(turned.sem, turned.before_reuse(w, PAIR))
                act.activation(h[:, b, :], m.table[:, bass.ds(w, 1), :].rearrange("p w f -> p (w f)"),
                               ACT.Relu).then_inc(relued.sem, 1)

            in_step(act, W, PAIR, (0, relu))

        @block.tensor
        def _(pe):
            def turn(w, b):
                pe.wait_ge(copied.sem, copied.before_reuse(w, PAIR))
                pe.wait_ge(relued.sem, relued.after(w))
                pe.transpose(turn_ps[b][:, 0:P], h[:, b, :], m.ident[:, :]).then_inc(turned.sem, 1)

            def multiply(w, b):
                pe.wait_ge(taken.sem, taken.before_reuse(w, PAIR))
                pe.wait_ge(copied.sem, copied.after(w))
                pe.matmul(prod_ps[b][:, 0:columns], h_t[:, b, :], weights, start=True,
                          stop=True).then_inc(multiplied.sem, 1)

            turned.start(pe)
            multiplied.start(pe)
            in_step(pe, W, PAIR, (1, turn), (0, multiply))

        @block.vector
        def _(v):
            def copy(w, b):
                v.wait_ge(multiplied.sem, multiplied.before_reuse(w, PAIR))
                v.wait_ge(turned.sem, turned.after(w))
                v.tensor_copy(h_t[:, b, :], turn_ps[b][:, 0:P]).then_inc(copied.sem, 1)

            def take(w, b):
                if out_columns:
                    v.wait_ge(stored[b], (w - b) * (16 // PAIR))
                v.wait_ge(multiplied.sem, multiplied.after(w))
                window = m.table[:, bass.ds(w, 1), :].rearrange("p w f -> p (w f)")
                if kept and bias is not None:
                    last = v.tensor_tensor(window, prod_ps[b][:, 0:kept], bias, ALU.add)
                elif kept:
                    last = v.tensor_copy(window, prod_ps[b][:, 0:kept])
                if out_columns:
                    last = v.tensor_copy(away[:, b, :], prod_ps[b][:, kept:kept + out_columns])
                last.then_inc(taken.sem, 1)

            copied.start(v)
            taken.start(v)
            in_step(v, W, PAIR, (1, copy), (0, take))

        if out_columns:
            @block.sync
            def _(sp):
                def store(w, b):
                    wait_apart(m, sp, taken.sem, taken.after(w))
                    sp.dma_start(rows_out.rearrange("(w p) c -> p w c", p=P)[:, bass.ds(w, 1), :],
                                 away[:, b:b + 1, :]).then_inc(stored[b], 16)

                in_step(sp, W, PAIR, (0, store))
                for b in range(PAIR):
                    sp.wait_ge(stored[b], 16 * (W // PAIR))
        for steps in m.project_steps:
            steps.again(W)


def update_nodes(nc, m, layer):
    W, PAIR = m.windows, 2
    K = NPATH if layer == 3 else F
    with ExitStack() as ctx:
        def sb(name, shape, dt=F32):
            return ctx.enter_context(nc.sbuf_tensor(name, shape, dt))

        sums = sb(f"u_sums_{layer}", [P, PAIR, K])
        sums_t = sb(f"u_sums_t_{layer}", [K, PAIR, P])
        gelu = sb(f"u_gelu_{layer}", [F, PAIR, P])
        line = sb(f"u_line_{layer}", [F, PAIR, P])
        smu = sb(f"u_smu_{layer}", [F, PAIR, P])
        part = sb(f"u_part_{layer}", [P, PAIR, F])
        banks = [[ctx.enter_context(nc.psum_tensor(f"u_{n}{b}_{layer}", [P, BANK], F32)) for b in range(PAIR)]
                 for n in ("turn", "hidden", "out")]
        turn_ps, hid_ps, out_ps = banks
        staged, turned = Steps(nc, ctx, f"u_staged_{layer}"), Steps(nc, ctx, f"u_turned_{layer}", 1)
        copied, mapped = Steps(nc, ctx, f"u_copied_{layer}", 1), Steps(nc, ctx, f"u_mapped_{layer}", 1)
        parted, added = Steps(nc, ctx, f"u_parted_{layer}"), Steps(nc, ctx, f"u_added_{layer}", 1)
        if layer == 0:
            hidden, bent, summed = (Steps(nc, ctx, f"u_{n}", 1) for n in ("hidden", "bent", "summed"))
        weights = {0: m.w_o2, 1: m.w2, 3: m.pick_out}[layer]
        block = ctx.enter_context(nc.Block())

        @block.scalar
        def _(act):
            def stage(w, b):
                act.wait_ge(turned.sem, turned.before_reuse(w, PAIR))
                act.activation(sums[:, b, :], m.acc[:, bass.ds(w, 1), 0:K].rearrange("p w f -> p (w f)"),
                               ACT.Copy).then_inc(staged.sem, 1)

            def bend(w, b):
                act.wait_ge(summed.sem, summed.before_reuse(w, PAIR))
                act.wait_ge(hidden.sem, hidden.after(w))
                act.activation(gelu[:, b, :], hid_ps[b][:, 0:P], ACT.Gelu, bias=m.b_o1_gelu[:, 0:1], scale=SMU)
                act.activation(line[:, b, :], hid_ps[b][:, 0:P], ACT.Identity, bias=m.b_o1_lin[:, 0:1],
                               scale=SMU_LIN).then_inc(bent.sem, 1)

            if layer == 0:
                bent.start(act)
                in_step(act, W, PAIR, (2, stage), (0, bend))
            else:
                in_step(act, W, PAIR, (0, stage))

        @block.tensor
        def _(pe):
            def turn(w, b):
                pe.wait_ge(copied.sem, copied.before_reuse(w, PAIR))
                wait_apart(m, pe, staged.sem, staged.after(w))
                pe.transpose(turn_ps[b][0:K, 0:P], sums[:, b, :], m.ident[:, :]).then_inc(turned.sem, 1)

            def hide(w, b):
                pe.wait_ge(bent.sem, bent.before_reuse(w, PAIR))
                pe.wait_ge(copied.sem, copied.after(w))
                pe.matmul(hid_ps[b][:, 0:P], m.w_o1[:, :], sums_t[:, b, :], start=True,
                          stop=True).then_inc(hidden.sem, 1)

            def map_out(w, b):
                pe.wait_ge(added.sem, added.before_reuse(w, PAIR))
                if layer == 0:
                    pe.wait_ge(summed.sem, summed.after(w))
                    left = smu[:, b, :]
                else:
                    pe.wait_ge(copied.sem, copied.after(w))
                    left = sums_t[:, b, :]
                pe.matmul(out_ps[b][:, 0:F], left, weights[:, :], start=True, stop=True).then_inc(mapped.sem, 1)

            turned.start(pe)
            mapped.start(pe)
            if layer == 0:
                hidden.start(pe)
                in_step(pe, W, PAIR, (2, turn), (1, hide), (0, map_out))
            else:
                in_step(pe, W, PAIR, (1, turn), (0, map_out))

        @block.vector
        def _(v):
            def copy(w, b):
                reader = hidden if layer == 0 else mapped
                v.wait_ge(reader.sem, reader.before_reuse(w, PAIR))
                v.wait_ge(turned.sem, turned.after(w))
                v.tensor_copy(sums_t[:, b, :], turn_ps[b][0:K, 0:P]).then_inc(copied.sem, 1)

            def sum_smu(w, b):
                v.wait_ge(mapped.sem, mapped.before_reuse(w, PAIR))
                v.wait_ge(bent.sem, bent.after(w))
                v.tensor_tensor(smu[:, b, :], gelu[:, b, :], line[:, b, :], ALU.add).then_inc(summed.sem, 1)

            def add(w, b):
                node = m.x[:, bass.ds(w, 1), :].rearrange("p w f -> p (w f)")
                out = out_ps[b][:, 0:F]
                v.wait_ge(mapped.sem, mapped.after(w))
                if layer == 3:
                    v.tensor_tensor(node, node, out, ALU.add).then_inc(added.sem, 1)
                    return
                if layer == 0:
                    v.tensor_tensor(part[:, b, :], m.b_o2[:, :], out, ALU.add).then_inc(parted.sem, 1)
                else:
                    v.scalar_tensor_tensor(part[:, b, :], m.b2[:, :],
                                           m.acc[:, bass.ds(w, 1), F:F + 1].rearrange("p w f -> p (w f)"), out,
                                           ALU.mult, ALU.add).then_inc(parted.sem, 1)
                v.wait_ge(parted.sem, parted.after(w))
                v.tensor_tensor(node, node, part[:, b, :], ALU.add).then_inc(added.sem, 1)

            copied.start(v)
            added.start(v)
            if layer == 0:
                summed.start(v)
                in_step(v, W, PAIR, (2, copy), (1, sum_smu), (0, add))
            else:
                in_step(v, W, PAIR, (1, copy), (0, add))


def layer0_messages(nc, m):
    W, TP, N = m.windows, m.tiles, m.tiles // G
    with ExitStack() as ctx:
        def sb(name, shape, dt=F32):
            return ctx.enter_context(nc.sbuf_tensor(name, shape, dt))

        def bank(name):
            return ctx.enter_context(nc.psum_tensor(name, [P, BANK], F32))

        rows = sb("a_rows", [P, DEEP, G, ROW])
        index = sb("a_index", [P, SLOTS, G], I32)
        GP = G * P
        out, oh, oh_t, rbf_t, gelu, smu, own, filt = parts_of(
            m.acc, SLOTS * G * SROW, 2 * GP, SLOTS * GP, 2 * GP, 2 * GP, 2 * GP, 2 * GP, 2 * GP)
        out = out.rearrange("p (s g c) -> p s g c", s=SLOTS, g=G)
        oh = oh.bitcast(BF16).rearrange("p (s g f) -> p s g f", s=SLOTS, g=G)
        own, filt = (a.rearrange("p (b g f) -> p b g f", b=2, g=G) for a in (own, filt))
        gelu, smu = (a.rearrange("p (b e) -> p b e", b=2) for a in (gelu, smu))
        oh_t = oh_t.rearrange("p (s e) -> p s e", s=SLOTS)
        rbf_t = rbf_t[0:NRBF + 1, :].rearrange("p (b e) -> p b e", b=2)
        oh_t_ps = ctx.enter_context(nc.psum_tensor("a_onehot_t_ps", [P, BANK], BF16))
        rbf_t_ps = bank("a_rbf_t_ps")
        hid_ps = [bank(f"a_hidden{b}") for b in range(2)]
        own_ps = [bank(f"a_own_ps{b}") for b in range(2)]
        filt_ps = [bank(f"a_filt_ps{b}") for b in range(2)]

        row_in, sent = m.row_in, m.moved
        row_in.use(DEEP, 1)
        sent.use(SLOTS, G)
        onehot = Steps(nc, ctx, "a_onehot_made", head=1)
        turned = Steps(nc, ctx, "a_turned", head=3)
        copied = Steps(nc, ctx, "a_copied", head=1)
        hidden = Steps(nc, ctx, "a_hidden", head=1)
        gelued = Steps(nc, ctx, "a_gelued", head=1)
        smued = Steps(nc, ctx, "a_smued", head=1)
        filtered = Steps(nc, ctx, "a_filtered", head=3)
        scaled = Steps(nc, ctx, "a_scaled", head=7)
        biased = Steps(nc, ctx, "a_biased", head=1)
        made = Steps(nc, ctx, "a_made", head=7)
        block = ctx.enter_context(nc.Block())

        @block.sync
        def _(sp):
            def load(q, k):
                sp.wait_ge(scaled.sem, scaled.before_reuse(q, DEEP))
                wait_apart(m, sp, made.sem, made.before_reuse(q, DEEP))
                sp.dma_start(rows[:, k, :, :], tiles_of(m.by_dst, TP, q * G, 0, ROW)).then_inc(row_in.sems[k], 16)

            in_step(sp, N, DEEP, (0, load))

        @block.vector
        def _(v):
            def bias(q, k):
                v.wait_ge(made.sem, made.before_reuse(q, 2))
                v.wait_ge(filtered.sem, filtered.after(q))
                v.tensor_tensor(filt[:, k % 2, :, :], filt_ps[k % 2][:, :].rearrange("p (g f) -> p g f", g=G),
                                m.b_f2[:, :].unsqueeze(1).to_broadcast([P, G, F]), ALU.add).then_inc(biased.sem, 1)

            def make_onehot(q, k):
                v.wait_ge(row_in.sems[k], row_in.after(q, k))
                v.wait_ge(turned.sem, turned.before_reuse(q, SLOTS))
                v.tensor_tensor(oh[:, k % SLOTS, :, :], rows[:, k, :, C_DLOC:C_DLOC + 1].to_broadcast([P, G, P]),
                                m.iota_nodes[:, :].unsqueeze(1).to_broadcast([P, G, P]),
                                ALU.is_equal).then_inc(onehot.sem, 1)

            def message(q, k):
                s = k % SLOTS
                v.wait_ge(sent.sems[s], sent.before(q, s))
                v.tensor_copy(index[:, s, :], rows[:, k, :, C_POS].bitcast(I32))
                v.wait_ge(scaled.sem, scaled.after(q))
                v.wait_ge(biased.sem, biased.after(q))
                v.tensor_tensor(out[:, s, :, 0:F], filt[:, k % 2, :, :], own[:, k % 2, :, :],
                                ALU.mult).then_inc(made.sem, 1)

            def sum_smu(q, k):
                b = k % 2
                v.wait_ge(filtered.sem, filtered.before_reuse(q, 2))
                v.wait_ge(gelued.sem, gelued.after(q))
                v.scalar_tensor_tensor(smu[:, b, :], hid_ps[b][:, :], SMU_LIN, gelu[:, b, :], ALU.mult,
                                       ALU.add).then_inc(smued.sem, 1)

            smued.start(v)
            biased.start(v)
            made.start(v)
            onehot.start(v)
            in_step(v, N, DEEP, (0, bias), (4, make_onehot), (0, message), (2, sum_smu))

        @block.tensor
        def _(pe):
            def hide(q, k):
                pe.wait_ge(copied.sem, copied.after(q))
                pe.wait_ge(smued.sem, smued.before_reuse(q, 2))
                pe.matmul(hid_ps[k % 2][:, :], m.w_f1[:, :], rbf_t[:, k % 2, :], start=True,
                          stop=True).then_inc(hidden.sem, 1)

            def turn(q, k):
                pe.wait_ge(copied.sem, copied.before_reuse(q, 1))
                pe.wait_ge(onehot.sem, onehot.after(q))
                for j in range(G):
                    pe.transpose(rbf_t_ps[0:NRBF + 1, j * P:(j + 1) * P], rows[:, k, j, C_RBF:C_ONE + 1],
                                 m.ident[:, :])
                    last = pe.transpose(oh_t_ps[:, j * P:(j + 1) * P], oh[:, k % SLOTS, j, :], m.ident_bf[:, :])
                last.then_inc(turned.sem, 1)

            def products(q, k):
                b = k % 2
                windows = window_registers(nc, pe, m.tile_window_dst, q * G, W)
                pe.wait_ge(scaled.sem, scaled.before_reuse(q, 2))
                pe.wait_ge(biased.sem, biased.before_reuse(q, 2))
                for j in range(G):
                    pe.matmul(own_ps[b][:, j * F:(j + 1) * F], oh_t[:, k % SLOTS, j * P:(j + 1) * P],
                              m.table[:, bass.ds(windows[j], 1), :].rearrange("p w f -> p (w f)"),
                              start=True, stop=True)
                pe.wait_ge(smued.sem, smued.after(q))
                for j in range(G):
                    last = pe.matmul(filt_ps[b][:, j * F:(j + 1) * F], smu[:, b, j * P:(j + 1) * P],
                                     m.w_f2[:, :], start=True, stop=True)
                last.then_inc(filtered.sem, 1)

            turned.start(pe)
            hidden.start(pe)
            filtered.start(pe)
            in_step(pe, N, DEEP, (2, hide), (3, turn), (1, products))

        @block.scalar
        def _(act):
            def scale(q, k):
                b, s = k % 2, k % SLOTS
                act.wait_ge(sent.sems[s], sent.before(q, s))
                act.activation(out[:, s, :, F:SROW], rows[:, k, :, C_EF:C_EF + CARRY], ACT.Copy)
                act.wait_ge(made.sem, made.before_reuse(q, 2))
                act.wait_ge(filtered.sem, filtered.after(q))
                for j in range(G):
                    last = act.activation(own[:, b, j, :], own_ps[b][:, j * F:(j + 1) * F], ACT.Copy,
                                          scale=rows[:, k, j, C_WEIGHT:C_WEIGHT + 1])
                last.then_inc(scaled.sem, 1)

            def bend(q, k):
                act.wait_ge(smued.sem, smued.before_reuse(q, 2))
                act.wait_ge(hidden.sem, hidden.after(q))
                act.activation(gelu[:, k % 2, :], hid_ps[k % 2][:, :], ACT.Gelu, scale=SMU).then_inc(gelued.sem, 1)

            def copy(q, k):
                act.wait_ge(hidden.sem, hidden.before_reuse(q, 2))
                act.wait_ge(filtered.sem, filtered.before_reuse(q, SLOTS))
                act.wait_ge(turned.sem, turned.after(q))
                act.activation(rbf_t[:, k % 2, :], rbf_t_ps[0:NRBF + 1, :], ACT.Copy)
                act.activation(oh_t[:, k % SLOTS, :], oh_t_ps[:, :], ACT.Copy).then_inc(copied.sem, 1)

            copied.start(act)
            gelued.start(act)
            scaled.start(act)
            in_step(act, N, DEEP, (0, scale), (2, bend), (3, copy))

        @block.gpsimd
        def _(pool):
            def send(q, k):
                pool.wait_ge(m.blanks_s, m.blanks)
                pool.wait_ge(scaled.sem, scaled.after(q))
                wait_apart(m, pool, made.sem, made.after(q))
                for j in range(G):
                    pool.indirect_dma_start(
                        m.by_src, bass.IndirectOffsetOnAxis(ap=index[:, k, j:j + 1], axis=0),
                        out[:, k, j, :], None, bounds_check=P * TP - 1, oob_is_err=False
                    ).then_inc(sent.sems[k], 16)

            in_step(pool, N, SLOTS, (0, send))
            for k in range(SLOTS):
                pool.wait_ge(sent.sems[k], sent.after(N - SLOTS + k, k))
        row_in.again(N)
        sent.again(N)


def adding(nc, v, m, added, tile_window, totals_ps, columns):
    windows = [None] * G

    def add(j, q, k):
        acc = m.acc[:, bass.ds(windows[j], 1), 0:columns].rearrange("p w f -> p (w f)")
        v.wait_ge(added.sem, added.after(q) - added.per + j)
        v.tensor_tensor(acc, acc, totals_ps(k, j), ALU.add).then_inc(added.sem, 1)

    def add_first(summed):
        def stage(q, k):
            windows[:] = window_registers(nc, v, tile_window, q * G, m.windows)
            v.wait_ge(summed.sem, summed.after(q))
            add(0, q, k)
        return stage

    def add_next(j):
        return lambda q, k: add(j, q, k)

    return add_first, add_next


def layer0_sums(nc, m):
    TP, N = m.tiles, m.tiles // G
    with ExitStack() as ctx:
        rows = ctx.enter_context(nc.sbuf_tensor("b_rows_in", [P, SLOTS, G, SROW], F32))
        oh = ctx.enter_context(nc.sbuf_tensor("b_onehot", [P, SLOTS, G, P], F32))
        sum_ps = [ctx.enter_context(nc.psum_tensor(f"b_sum_ps{b}", [P, BANK], F32)) for b in range(SLOTS)]
        row_in = m.row_in
        row_in.use(SLOTS, 1)
        onehot = Steps(nc, ctx, "b_onehot_made")
        summed = Steps(nc, ctx, "b_summed", head=3)
        added = Steps(nc, ctx, "b_added", head=3 * G, per=G)
        block = ctx.enter_context(nc.Block())

        @block.sync
        def _(sp):
            def load(q, k):
                wait_apart(m, sp, summed.sem, summed.before_reuse(q, SLOTS))
                sp.dma_start(rows[:, k, :, :], tiles_of(m.by_src, TP, q * G, 0, SROW)).then_inc(row_in.sems[k], 16)

            in_step(sp, N, SLOTS, (0, load))

        @block.tensor
        def _(pe):
            def sums(q, k):
                pe.wait_ge(added.sem, added.before_reuse(q, SLOTS))
                pe.wait_ge(onehot.sem, onehot.after(q))
                for j in range(G):
                    last = pe.matmul(sum_ps[k][:, j * F:(j + 1) * F], oh[:, k, j, :], rows[:, k, j, 0:F],
                                     start=True, stop=True)
                last.then_inc(summed.sem, 1)

            summed.start(pe)
            in_step(pe, N, SLOTS, (0, sums))

        @block.vector
        def _(v):
            def make_onehot(q, k):
                v.wait_ge(row_in.sems[k], row_in.after(q, k))
                v.wait_ge(summed.sem, summed.before_reuse(q, SLOTS))
                v.tensor_tensor(oh[:, k, :, :], rows[:, k, :, S_SLOC:S_SLOC + 1].to_broadcast([P, G, P]),
                                m.iota_nodes[:, :].unsqueeze(1).to_broadcast([P, G, P]),
                                ALU.is_equal).then_inc(onehot.sem, 1)

            add_first, add_next = adding(nc, v, m, added, m.tile_window_src,
                                         lambda k, j: sum_ps[k][:, j * F:(j + 1) * F], F)
            v.memset(m.acc[:, :, :], 0.0).then_inc(added.sem, added.head)
            in_step(v, N, SLOTS, (0, add_first(summed)), (2, make_onehot), *((0, add_next(j)) for j in range(1, G)))
        row_in.again(N)


def layer1_edges(nc, m):
    W, TP, N = m.windows, m.tiles, m.tiles // G
    with ExitStack() as ctx:
        def sb(name, shape, dt=F32):
            return ctx.enter_context(nc.sbuf_tensor(name, shape, dt))

        def bank(name, n=1, dt=F32):
            return ctx.enter_context(nc.psum_tensor(name, [P, n * BANK], dt))

        rows = sb("c_rows", [P, DEEP, G, CARRY])
        index = sb("c_index", [P, DEEP, G], I32)
        hid = sb("c_hidden", [P, DEEP, G, F + 1])
        oh_bf = sb("c_onehot_bf", [P, SLOTS, G, P], BF16)
        oh = sb("c_onehot", [P, 2, G, P])
        oh_t = sb("c_onehot_t", [P, 2, G * P])
        ef_t = sb("c_ef_t", [NEF, 2, G * P])
        oh_t_ps, ef_t_ps = bank("c_onehot_t_ps", dt=BF16), bank("c_ef_t_ps")
        own_ps = [bank(f"c_own_ps{b}") for b in range(2)]
        sum_ps = [bank(f"c_sum_ps{b}", 2) for b in range(2)]
        row_in, came = m.row_in, m.moved
        row_in.use(DEEP, 1)
        came.use(DEEP, G)
        ones = ctx.enter_context(nc.semaphore("c_ones"))
        indexed = Steps(nc, ctx, "c_indexed")
        onehot = Steps(nc, ctx, "c_onehot_made")
        turned = Steps(nc, ctx, "c_turned", head=7)
        copied = Steps(nc, ctx, "c_copied", head=1)
        owned = Steps(nc, ctx, "c_owned", head=1)
        totalled = Steps(nc, ctx, "c_totalled", head=1)
        widened = Steps(nc, ctx, "c_widened", head=3)
        gelued = Steps(nc, ctx, "c_gelued")
        summed = Steps(nc, ctx, "c_summed", head=7)
        added = Steps(nc, ctx, "c_added", head=G, per=G)
        block = ctx.enter_context(nc.Block())

        def sums(k, j):
            at = (j // 2) * BANK + (j % 2) * (F + 1)
            return sum_ps[k % 2][:, at:at + F + 1]

        @block.sync
        def _(sp):
            def load(q, k):
                wait_apart(m, sp, turned.sem, turned.before_reuse(q, DEEP))
                sp.dma_start(rows[:, k, :, :], tiles_of(m.by_src, TP, q * G, S_EF, SROW)).then_inc(row_in.sems[k], 16)

            in_step(sp, N, DEEP, (0, load))

        @block.gpsimd
        def _(pool):
            def gather(q, k):
                pool.wait_ge(summed.sem, summed.before_reuse(q, DEEP))
                wait_apart(m, pool, indexed.sem, indexed.after(q))
                for j in range(G):
                    pool.indirect_dma_start(
                        hid[:, k, j, 0:F], None, m.b_rows,
                        bass.IndirectOffsetOnAxis(ap=index[:, k, j:j + 1], axis=0)).then_inc(came.sems[k], 16)

            pool.memset(hid[:, :, :, F:F + 1], 1.0).then_inc(ones, 1)
            in_step(pool, N, DEEP, (0, gather))

        @block.vector
        def _(v):
            def make_index(q, k):
                v.wait_ge(came.sems[k], came.before(q, k))
                v.wait_ge(row_in.sems[k], row_in.after(q, k))
                v.tensor_copy(index[:, k, :], rows[:, k, :, S_DST - S_EF]).then_inc(indexed.sem, 1)

            def make_onehot(q, k):
                v.wait_ge(turned.sem, turned.before_reuse(q, SLOTS))
                v.wait_ge(widened.sem, widened.before_reuse(q, SLOTS))
                v.tensor_tensor(oh_bf[:, k % SLOTS, :, :], rows[:, k, :, CARRY - 1:CARRY].to_broadcast([P, G, P]),
                                m.iota_nodes[:, :].unsqueeze(1).to_broadcast([P, G, P]),
                                ALU.is_equal).then_inc(onehot.sem, 1)

            def total_up(q, k):
                v.wait_ge(came.sems[k], came.after(q, k))
                v.wait_ge(owned.sem, owned.after(q))
                v.tensor_tensor(hid[:, k, :, 0:F], own_ps[k % 2][:, :].rearrange("p (g f) -> p g f", g=G),
                                hid[:, k, :, 0:F], ALU.add).then_inc(totalled.sem, 1)

            add_first, add_next = adding(nc, v, m, added, m.tile_window_src, sums, F + 1)
            v.memset(m.acc[:, :, :], 0.0).then_inc(added.sem, added.head)
            totalled.start(v)
            in_step(v, N, DEEP, (0, add_first(summed)), (7, make_index), (0, add_next(1)), (5, make_onehot),
                    (0, add_next(2)), (2, total_up), (0, add_next(3)))

        @block.tensor
        def _(pe):
            def own(q, k):
                b = k % 2
                windows = window_registers(nc, pe, m.tile_window_src, q * G, W)
                pe.wait_ge(totalled.sem, totalled.before_reuse(q, 2))
                pe.wait_ge(copied.sem, copied.after(q))
                for j in range(G):
                    to, of = own_ps[b][:, j * F:(j + 1) * F], slice(j * P, (j + 1) * P)
                    pe.matmul(to, oh_t[:, b, of], m.table[:, bass.ds(windows[j], 1), :].rearrange("p w f -> p (w f)"),
                              start=True, stop=False)
                    last = pe.matmul(to, ef_t[:, b, of], m.w1_ef[:, :], start=False, stop=True)
                last.then_inc(owned.sem, 1)

            def turn(q, k):
                pe.wait_ge(copied.sem, copied.before_reuse(q, 1))
                pe.wait_ge(onehot.sem, onehot.after(q))
                for j in range(G):
                    pe.transpose(ef_t_ps[0:NEF, j * P:(j + 1) * P], rows[:, k, j, 0:NEF], m.ident[:, :])
                    last = pe.transpose(oh_t_ps[:, j * P:(j + 1) * P], oh_bf[:, k % SLOTS, j, :], m.ident_bf[:, :])
                last.then_inc(turned.sem, 1)

            def sum_up(q, k):
                pe.wait_ge(added.sem, added.before_reuse(q, 2))
                pe.wait_ge(widened.sem, widened.after(q))
                pe.wait_ge(gelued.sem, gelued.after(q))
                pe.wait_ge(ones, 1)
                for j in range(G):
                    last = pe.matmul(sums(k, j), oh[:, k % 2, j, :], hid[:, k, j, :], start=True, stop=True)
                last.then_inc(summed.sem, 1)

            turned.start(pe)
            owned.start(pe)
            summed.start(pe)
            in_step(pe, N, DEEP, (3, own), (4, turn), (1, sum_up))

        @block.scalar
        def _(act):
            def copy(q, k):
                act.wait_ge(owned.sem, owned.before_reuse(q, 2))
                act.wait_ge(turned.sem, turned.after(q))
                act.activation(ef_t[:, k % 2, :], ef_t_ps[0:NEF, :], ACT.Copy)
                act.activation(oh_t[:, k % 2, :], oh_t_ps[:, :], ACT.Copy).then_inc(copied.sem, 1)

            def widen(q, k):
                act.wait_ge(summed.sem, summed.before_reuse(q, 2))
                act.wait_ge(onehot.sem, onehot.after(q))
                act.activation(oh[:, k % 2, :, :], oh_bf[:, k % SLOTS, :, :], ACT.Copy).then_inc(widened.sem, 1)

            def bend(q, k):
                act.wait_ge(totalled.sem, totalled.after(q))
                act.activation(hid[:, k, :, 0:F], hid[:, k, :, 0:F], ACT.Gelu).then_inc(gelued.sem, 1)

            copied.start(act)
            widened.start(act)
            in_step(act, N, DEEP, (2, widen), (4, copy), (2, bend))
        row_in.again(N)
        came.again(N)


def sums_by_dst(nc, m, layer, source, columns, weighted):
    W, TP, N = m.windows, m.tiles, m.tiles // G
    with ExitStack() as ctx:
        def sb(name, shape, dt=F32):
            return ctx.enter_context(nc.sbuf_tensor(name, shape, dt))

        def bank(name):
            return ctx.enter_context(nc.psum_tensor(name, [P, BANK], F32))

        rows = sb(f"d_rows_{layer}", [P, SLOTS, G, ROW])
        other = sb(f"d_other_{layer}", [P, SLOTS, G, columns])
        oh = sb(f"d_onehot_{layer}", [P, SLOTS, G, P])
        sum_ps = [bank(f"d_sum_ps{b}_{layer}") for b in range(2)]
        sh_t_ps = [bank(f"d_sh_t_ps{b}_{layer}") for b in range(2)]
        path_ps = [bank(f"d_path_ps{b}_{layer}") for b in range(2)]
        sh_t = sb(f"d_sh_t_{layer}", [NSH, 2, G * P])
        value = sb(f"d_value_{layer}", [P, 2, G, columns])
        row_in = m.row_in
        row_in.use(SLOTS, 1)
        came = m.moved
        came.use(SLOTS, G)
        onehot = Steps(nc, ctx, f"d_onehot_made_{layer}", head=3)
        if weighted:
            turned = Steps(nc, ctx, f"d_turned_{layer}", head=3)
            copied = Steps(nc, ctx, f"d_copied_{layer}", head=1)
            pathed = Steps(nc, ctx, f"d_pathed_{layer}", head=1)
            valued = Steps(nc, ctx, f"d_valued_{layer}", head=3)
        summed = Steps(nc, ctx, f"d_summed_{layer}", head=3)
        added = Steps(nc, ctx, f"d_added_{layer}", head=G, per=G)
        block = ctx.enter_context(nc.Block())
        users = valued if weighted else summed

        @block.sync
        def _(sp):
            def load(q, k):
                wait_apart(m, sp, came.sems[k], came.before(q, k))
                if weighted:
                    sp.wait_ge(turned.sem, turned.before_reuse(q, SLOTS))
                wait_apart(m, sp, onehot.sem, onehot.before_reuse(q, SLOTS))
                sp.dma_start(rows[:, k, :, :], tiles_of(m.by_dst, TP, q * G, 0, ROW)).then_inc(row_in.sems[k], 16)

            in_step(sp, N, SLOTS, (0, load))

        @block.gpsimd
        def _(pool):
            def gather(q, k):
                pool.wait_ge(users.sem, users.before_reuse(q, SLOTS))
                wait_apart(m, pool, row_in.sems[k], row_in.after(q, k))
                for j in range(G):
                    pool.indirect_dma_start(
                        other[:, k, j, :], None, source,
                        bass.IndirectOffsetOnAxis(ap=rows[:, k, j, C_SRC:C_SRC + 1].bitcast(I32), axis=0)
                    ).then_inc(came.sems[k], 16)

            in_step(pool, N, SLOTS, (0, gather))

        @block.vector
        def _(v):
            def make_onehot(q, k):
                v.wait_ge(row_in.sems[k], row_in.after(q, k))
                v.wait_ge(summed.sem, summed.before_reuse(q, SLOTS))
                v.tensor_tensor(oh[:, k, :, :], rows[:, k, :, C_DLOC:C_DLOC + 1].to_broadcast([P, G, P]),
                                m.iota_nodes[:, :].unsqueeze(1).to_broadcast([P, G, P]),
                                ALU.is_equal).then_inc(onehot.sem, 1)

            def weigh(q, k):
                b = k % 2
                v.wait_ge(came.sems[k], came.after(q, k))
                v.wait_ge(summed.sem, summed.before_reuse(q, 2))
                v.wait_ge(pathed.sem, pathed.after(q))
                v.tensor_tensor(value[:, b, :, :],
                                path_ps[b][:, 0:G * columns].rearrange("p (g f) -> p g f", g=G),
                                other[:, k, :, :], ALU.mult).then_inc(valued.sem, 1)

            add_first, add_next = adding(nc, v, m, added, m.tile_window_dst,
                                         lambda k, j: sum_ps[k % 2][:, j * columns:(j + 1) * columns], columns)
            if weighted:
                v.memset(m.acc[:, :, :], 0.0).then_inc(added.sem, added.head)
            else:
                added.start(v)
            onehot.start(v)
            if weighted:
                valued.start(v)
                in_step(v, N, SLOTS, (0, add_first(summed)), (2, make_onehot), (0, add_next(1)), (1, weigh),
                        (0, add_next(2)), (0, add_next(3)))
            else:
                in_step(v, N, SLOTS, (0, add_first(summed)), (2, make_onehot), *((0, add_next(j)) for j in range(1, G)))

        @block.tensor
        def _(pe):
            def turn(q, k):
                pe.wait_ge(row_in.sems[k], row_in.after(q, k))
                pe.wait_ge(copied.sem, copied.before_reuse(q, 2))
                for j in range(G):
                    last = pe.transpose(sh_t_ps[k % 2][0:NSH, j * P:(j + 1) * P],
                                        rows[:, k, j, C_SH:C_SH + NSH], m.ident[:, :])
                last.then_inc(turned.sem, 1)

            def path(q, k):
                b = k % 2
                pe.wait_ge(valued.sem, valued.before_reuse(q, 2))
                pe.wait_ge(copied.sem, copied.after(q))
                for j in range(G):
                    last = pe.matmul(path_ps[b][:, j * columns:(j + 1) * columns],
                                     sh_t[:, b, j * P:(j + 1) * P], m.pick_sh[:, :], start=True, stop=True)
                last.then_inc(pathed.sem, 1)

            def sum_up(q, k):
                b = k % 2
                pe.wait_ge(added.sem, added.before_reuse(q, 2))
                if weighted:
                    pe.wait_ge(valued.sem, valued.after(q))
                    of = value[:, b, :, :]
                else:
                    pe.wait_ge(came.sems[k], came.after(q, k))
                    of = other[:, k, :, :]
                pe.wait_ge(onehot.sem, onehot.after(q))
                for j in range(G):
                    last = pe.matmul(sum_ps[b][:, j * columns:(j + 1) * columns], oh[:, k, j, :], of[:, j, :],
                                     start=True, stop=True)
                last.then_inc(summed.sem, 1)

            summed.start(pe)
            if weighted:
                turned.start(pe)
                pathed.start(pe)
                in_step(pe, N, SLOTS, (2, turn), (1, path), (0, sum_up))
            else:
                in_step(pe, N, SLOTS, (0, sum_up))

        @block.scalar
        def _(act):
            def copy(q, k):
                act.wait_ge(pathed.sem, pathed.before_reuse(q, 2))
                act.wait_ge(turned.sem, turned.after(q))
                act.activation(sh_t[:, k % 2, :], sh_t_ps[k % 2][0:NSH, :], ACT.Copy).then_inc(copied.sem, 1)

            if weighted:
                copied.start(act)
                in_step(act, N, SLOTS, (1, copy))
        row_in.again(N)
        came.again(N)


def keep_h(nc, m):
    with ExitStack() as ctx:
        relued, stored = ctx.enter_context(nc.semaphore("h_relued")), ctx.enter_context(nc.semaphore("h_stored"))
        block = ctx.enter_context(nc.Block())

        @block.scalar
        def _(act):
            act.activation(m.acc[:, :, 0:F], m.table[:, :, :], ACT.Relu).then_inc(relued, 1)

        @block.sync
        def _(sp):
            sp.wait_ge(relued, 1)
            sp.dma_start(m.h_rows.rearrange("(w p) f -> p w f", p=P), m.acc[:, :, 0:F]).then_inc(stored, 16)
            sp.wait_ge(stored, 16)


def add_sums(nc, m):
    with nc.Block() as block:
        @block.vector
        def _(v):
            v.tensor_tensor(m.x[:, :, :], m.x[:, :, :], m.acc[:, :, 0:F], ALU.add)


def store(nc, m, out):
    full, rest = m.nodes // P, m.nodes % P
    with ExitStack() as ctx:
        stored = ctx.enter_context(nc.semaphore("stored"))
        block = ctx.enter_context(nc.Block())

        @block.sync
        def _(sp):
            sp.dma_start(out[0:full * P, :].rearrange("(w p) f -> p w f", p=P), m.x[:, 0:full, :]).then_inc(stored, 16)
            if rest:
                sp.dma_start(out[full * P:m.nodes, :], m.x[0:rest, full, :]).then_inc(stored, 16)
            sp.wait_ge(stored, 16 * (1 + (rest > 0)))


def program(nc, out, nodes, edge_count, src_keys, dst_keys, edges, **w):
    with ExitStack() as ctx:
        m = Memory()
        m.nodes, m.windows = nodes, -(-nodes // (2 * P)) * 2
        m.edge_tiles, m.tiles = edge_tiles(edge_count), ordered_tiles(edge_count, m.windows)
        allocate(nc, ctx, m)
        load_constants(nc, m, w)
        count_windows(nc, m, src_keys, dst_keys)
        order_edges(nc, m, edges)
        normalise(nc, m, 0, m.table[:, :, :])
        project(nc, m, 0, m.w_in2f[:, :], F, None, F, None, 0)
        layer0_messages(nc, m)
        layer0_sums(nc, m)
        update_nodes(nc, m, 0)
        normalise(nc, m, 1, m.table[:, :, :])
        project(nc, m, 1, m.w1_ab[:, :], 2 * F, m.b1[:, :], F, m.b_rows, F)
        layer1_edges(nc, m)
        update_nodes(nc, m, 1)
        normalise(nc, m, 2, m.table[:, :, :])
        keep_h(nc, m)
        sums_by_dst(nc, m, 2, m.h_rows, F, False)
        add_sums(nc, m)
        normalise(nc, m, 3, m.table[:, :, :])
        project(nc, m, 3, m.pick_in[:, :], NPATH, None, 0, m.g_rows, NPATH)
        sums_by_dst(nc, m, 3, m.g_rows, NPATH, True)
        update_nodes(nc, m, 3)
        store(nc, m, out)


def kernel(**inputs):
    import numpy as np
    import concourse.bacc as bacc
    from concourse.bass_utils import run_bass_kernel_spmd as run

    a = {k: np.ascontiguousarray(v) for k, v in inputs.items()}
    nodes, count = a["x"].shape[0], a["src"].shape[0]
    T, windows = edge_tiles(count), -(-nodes // (2 * P)) * 2
    x = np.zeros((windows * P, F), np.float32)
    x[:nodes] = a["x"]
    edges = np.zeros((P * T, ROW), np.float32)
    edges[:count, C_RBF:C_ONE] = a["edge_attr_20"]
    edges[:, C_ONE] = 1.0
    edges[:count, C_WEIGHT] = a["edge_weight"]
    edges[:count, C_SH:C_SH + NSH] = a["edge_attr_16"]
    edges[:count, C_SRC] = a["src"].astype(np.int32, copy=False).view(np.float32)
    edges[:count, C_EF:C_EF + NEF] = a["edge_attr_32"]
    keys = np.full((2, P * T), -1, np.int32)
    keys[0, :count], keys[1, :count] = a["src"], a["dst"]
    arrays = {
        "src_keys": keys[0].reshape(P, T), "dst_keys": keys[1].reshape(P, T), "edges": edges, "x": x,
        "w_in2f_t": a["L0_gnn_W_in2f"].T, "w_f1_t": a["L0_gnn_W_f1"].T, "b_f1": a["L0_gnn_b_f1"],
        "w_f2_t": a["L0_gnn_W_f2"].T, "b_f2": a["L0_gnn_b_f2"], "w_o1_t": a["L0_gnn_W_o1"].T,
        "b_o1": a["L0_gnn_b_o1"], "w_o2_t": a["L0_gnn_W_o2"].T, "b_o2": a["L0_gnn_b_o2"],
        "w1": a["L1_gnn_W1"], "b1": a["L1_gnn_b1"], "w2": a["L1_gnn_W2"], "b2": a["L1_gnn_b2"],
        "coeff": a["L3_gnn_coeff"], "ki": a["L3_gnn_ki"], "kj": a["L3_gnn_kj"], "ko": a["L3_gnn_ko"],
    }
    arrays = {f"in_{k}": np.ascontiguousarray(v) for k, v in arrays.items()}
    nc = bacc.Bacc("TRN2", target_bir_lowering=False, num_devices=1)
    aps = {k[3:]: nc.dram_tensor(k, v.shape, mybir.dt.from_np(v.dtype), kind="ExternalInput").ap()
           for k, v in arrays.items()}
    out = nc.dram_tensor("out_0", (nodes, F), F32, kind="ExternalOutput").ap()
    program(nc, out, nodes, count, **aps)
    return run(nc, [arrays], core_ids=[0]).results[0]["out_0"]
```

```python
from contextlib import ExitStack

import concourse.bass as bass
from concourse import mybir

F32 = mybir.dt.float32
BF16 = mybir.dt.bfloat16
F16 = mybir.dt.float16
I32 = mybir.dt.int32
I16 = mybir.dt.int16
ALU = mybir.AluOpType
ACT = mybir.ActivationFunctionType
AX = mybir.AxisListType

P = 128
F = 128
G = 4
SLOTS = 4
BODY = G * SLOTS
DEEP = 8
BANK = 512
NRBF, NEF, NSH, NPATH = 20, 32, 16, 64

C_RBF, C_ONE, C_WEIGHT, C_SH = 0, NRBF, NRBF + 1, NRBF + 2
C_SRC = C_SH + NSH
C_POS = C_SRC + 1
C_DLOC = C_POS + 1
C_EF = C_DLOC + 1
C_DST = C_EF + NEF
C_SLOC = C_DST + 1
ROW = C_SLOC + 2
CARRY = C_SLOC + 1 - C_EF
S_EF, S_DST, S_SLOC = F, F + NEF, F + NEF + 1
SROW = F + CARRY

FAR = float(1 << 22)
SMU = 2.5 * 0.99 * 2.0 ** 0.5
SMU_LIN = 0.01 / 0.99 * SMU
EPS = 1e-5


def edge_tiles(edges):
    return -(-edges // (P * BODY)) * BODY


def ordered_tiles(edges, windows):
    return -(-((edges + windows * (P - 1)) // P) // (G * DEEP)) * (G * DEEP)


class Memory:
    pass


def parts_of(tensor, *columns):
    flat, parts, at = tensor[:, :, :].rearrange("p w f -> p (w f)"), [], 0
    for n in columns:
        assert at + n <= flat.shape[1]
        parts.append(flat[:, at:at + n])
        at += n
    return parts


def allocate(nc, ctx, m):
    def sb(name, shape, dt=F32):
        return ctx.enter_context(nc.sbuf_tensor(name, shape, dt))

    W = m.windows
    m.blanks_d = ctx.enter_context(nc.semaphore("blanks_d"))
    m.blanks_s = ctx.enter_context(nc.semaphore("blanks_s"))
    m.norm_chain, m.norm_rooted = (ctx.enter_context(nc.semaphore(n)) for n in ("norm_chain", "norm_rooted"))
    m.project_steps = [Steps(nc, ctx, f"p_{n}", before)
                       for n, before in (("relued", 0), ("turned", 3), ("copied", 3), ("multiplied", 3), ("taken", 3))]
    m.waits_apart = {e.engine: ctx.enter_context(nc.semaphore(f"waits_apart_{n}"))
                     for n, e in (("sp", nc.sync), ("pool", nc.gpsimd), ("pe", nc.tensor))}
    m.blanks = 16 * (m.tiles // BODY)
    m.row_in, m.moved = Moves(nc, ctx, "row_in", DEEP), Moves(nc, ctx, "moved", DEEP)
    m.x = sb("x_nodes", [P, W, F])
    m.table = sb("node_table", [P, W, F])
    m.acc = sb("segment_sums", [P, W, F + 1])
    T = m.edge_tiles
    keys, pre_dst, pre_src, windows, some_slots = parts_of(m.acc, 2 * T, T, T, 2 * T, T)
    m.some_slots = some_slots[0:W, :].bitcast(I32)
    m.keys = keys.bitcast(I32).rearrange("p (k t) -> p k t", k=2)
    m.key_windows = windows.rearrange("p (k t) -> p k t", k=2)
    m.pre_dst, m.pre_src = pre_dst[0:W, :], pre_src[0:W, :]
    parts = parts_of(m.table, BODY * ROW, BODY * SROW, 2 * T, m.tiles, m.tiles, m.tiles // 2)
    m.blank_d, m.blank_s = (p.rearrange("p (t c) -> p t c", t=BODY) for p in parts[:2])
    m.shifted = parts[2].bitcast(I32).rearrange("p (k t) -> p k t", k=2)
    m.next_slot = parts[2][0:W, :].bitcast(F16).rearrange("w (k t c) -> w k t c", k=2, c=2)
    assert m.tiles <= 2048
    m.tile_iota, m.tile_iota_f = parts[3][0:W, :].bitcast(I32), parts[4][0:W, :]
    m.started = parts[5][0:W, :].bitcast(BF16)
    m.iota_nodes = sb("iota_nodes", [P, P])
    m.iota_windows = sb("iota_windows", [P, W])
    m.ident = sb("ident", [P, P])
    m.ident_bf = sb("ident_bf", [P, P], BF16)
    m.before_bf = sb("before_bf", [P, P], BF16)
    m.before = sb("before", [P, P])
    m.ones_bf = sb("ones_bf", [P, 1], BF16)
    m.ones = sb("ones", [P, 1])
    m.eps = sb("eps", [P, 1])
    m.tile_window_dst = sb("tile_window_dst", [1, m.tiles], I16)
    m.tile_window_src = sb("tile_window_src", [1, m.tiles], I16)
    m.stats = sb("stats", [P, W, 6])
    m.mean, m.gap, m.std, m.shift = (sb(n, [P, W]) for n in ("mean", "gap", "std", "shift"))
    m.rstd = sb("rstd", [P, W])
    m.w_in2f = sb("w_in2f", [F, F])
    m.w_f1 = sb("w_f1", [NRBF + 1, F])
    m.w_f2 = sb("w_f2", [F, F])
    m.b_f2 = sb("b_f2", [P, F])
    m.w_o1 = sb("w_o1", [F, F])
    m.b_o1 = sb("b_o1", [F, 1])
    m.b_o1_gelu = sb("b_o1_gelu", [F, 1])
    m.b_o1_lin = sb("b_o1_lin", [F, 1])
    m.w_o2 = sb("w_o2", [F, F])
    m.b_o2 = sb("b_o2", [P, F])
    m.w1_ab = sb("w1_ab", [F, 2 * F])
    m.w1_ef = sb("w1_ef", [NEF, F])
    m.b1 = sb("b1", [P, F])
    m.w2 = sb("w2", [F, F])
    m.b2 = sb("b2", [P, F])
    m.pick_in = sb("pick_in", [F, NPATH])
    m.pick_sh = sb("pick_sh", [NSH, NPATH])
    m.pick_out = sb("pick_out", [NPATH, F])

    def dram(name, shape):
        return nc.dram_tensor(name, shape, F32, kind="Internal").ap()

    m.by_dst = dram("edges_by_dst", [P * m.tiles, ROW])
    m.by_src = dram("edges_by_src", [P * m.tiles, SROW])
    m.b_rows = dram("b_rows", [W * P, F])
    m.h_rows = dram("h_rows", [W * P, F])
    m.g_rows = dram("g_rows", [W * P, NPATH])


def tiles_of(table, tiles, t, first, last):
    return table.rearrange("(p t) c -> p t c", t=tiles)[:, bass.ds(t, G), first:last]


def window_registers(nc, eng, tile_window, t, windows):
    _, got = nc.values_load_multi_w_load_instructions(
        tile_window[0:1, bass.ds(t, G)], engines=[eng.engine], min_val=0, max_val=windows - 1,
        skip_runtime_bounds_check_because="each entry is a count of 1 to `windows` bases, less one")
    return got


class Steps:

    def __init__(self, nc, ctx, name, before=0, per=1):
        self.sem, self.per = ctx.enter_context(nc.semaphore(name)), per
        self.head = self.first = (before + 1) * per if before else 0

    def after(self, q):
        return q * self.per + (self.head + self.per)

    def before_reuse(self, q, slots):
        return q * self.per + (self.head + self.per - self.per * slots)

    def start(self, eng):
        eng.sem_inc(self.sem, self.first)

    def again(self, groups):
        self.head += self.per * groups + self.first


class Moves:

    def __init__(self, nc, ctx, name, slots):
        self.sems = [ctx.enter_context(nc.semaphore(f"{name}{k}")) for k in range(slots)]
        self.head = [0] * slots

    def use(self, slots, per):
        self.slots, self.per = slots, 16 * per

    def before(self, q, k):
        return (q - k) * (self.per // self.slots) + self.head[k]

    def after(self, q, k):
        return (q - k) * (self.per // self.slots) + (self.head[k] + self.per)

    def again(self, groups):
        for k in range(self.slots):
            self.head[k] += self.per * len(range(k, groups, self.slots))


def wait_apart(m, eng, sem, value):
    eng.wait_ge(sem, value).then_inc(m.waits_apart[eng.engine], 1)


def in_step(eng, groups, slots, *stages):
    most = max(lead for lead, _ in stages)

    def step(q, at):
        for lead, emit in stages:
            if not isinstance(q, int) or 0 <= q + lead < groups:
                emit(q + lead, (at + lead) % slots)

    for q in range(-most, 0):
        step(q, q)
    looped = max(groups - most, 0) // slots * slots
    if looped:
        with eng.Fori(0, looped // slots) as turn:
            for k in range(slots):
                step(turn * slots + k, k)
    for q in range(looped, groups):
        step(q, q)


def load_constants(nc, m, w):
    with ExitStack() as ctx:
        def sem(name):
            return ctx.enter_context(nc.semaphore(name))

        loaded, made, cast, dve = sem("c_loaded"), sem("c_made"), sem("c_cast"), sem("c_dve")
        iota_i = ctx.enter_context(nc.sbuf_tensor("iota_i", [P, P], I32))
        ki = ctx.enter_context(nc.sbuf_tensor("ki", [F, NPATH], I32))
        kj = ctx.enter_context(nc.sbuf_tensor("kj", [NSH, NPATH], I32))
        ko = ctx.enter_context(nc.sbuf_tensor("ko", [NPATH, 1], I32))
        ki_f = ctx.enter_context(nc.sbuf_tensor("ki_f", [F, NPATH], F32))
        kj_f = ctx.enter_context(nc.sbuf_tensor("kj_f", [NSH, NPATH], F32))
        ko_f = ctx.enter_context(nc.sbuf_tensor("ko_f", [NPATH, 1], F32))
        place = ctx.enter_context(nc.sbuf_tensor("place", [P, 1], F32))
        coeff = ctx.enter_context(nc.sbuf_tensor("coeff", [NSH, NPATH], F32))
        block = ctx.enter_context(nc.Block())

        def rows(v, n):
            return v.rearrange("(a n) -> a n", a=1).to_broadcast([n, v.shape[0]])

        loads = [
            (m.w_in2f[:, :], w["w_in2f_t"]), (m.w_f1[0:NRBF, :], w["w_f1_t"]),
            (m.w_f1[NRBF:NRBF + 1, :], rows(w["b_f1"], 1)),
            (m.w_f2[:, :], w["w_f2_t"]), (m.b_f2[:, :], rows(w["b_f2"], P)),
            (m.w_o1[:, :], w["w_o1_t"]), (m.b_o1[:, :], w["b_o1"].rearrange("(n a) -> n a", a=1)),
            (m.w_o2[:, :], w["w_o2_t"]), (m.b_o2[:, :], rows(w["b_o2"], P)),
            (m.w1_ab[:, 0:F], w["w1"][0:F, :]), (m.w1_ab[:, F:2 * F], w["w1"][F:2 * F, :]),
            (m.w1_ef[:, :], w["w1"][2 * F:2 * F + NEF, :]), (m.b1[:, :], rows(w["b1"], P)),
            (m.w2[:, :], w["w2"]), (m.b2[:, :], rows(w["b2"], P)),
            (ki[:, :], rows(w["ki"], F)), (kj[:, :], rows(w["kj"], NSH)),
            (ko[:, :], w["ko"].rearrange("(n a) -> n a", a=1)), (coeff[:, :], rows(w["coeff"], NSH)),
            (m.x[:, :, :], w["x"].rearrange("(w p) f -> p w f", p=P)),
        ]

        @block.sync
        def _(sp):
            for to, of in loads:
                sp.dma_start(to, of).then_inc(loaded, 16)
            sp.wait_ge(loaded, 16 * len(loads))

        @block.gpsimd
        def _(pool):
            pool.iota(iota_i[:, :], pattern=[[1, P]], base=0, channel_multiplier=0).then_inc(made, 1)
            pool.memset(m.ident[:, :], 0.0).then_inc(made, 1)
            pool.memset(m.before[:, :], 1.0).then_inc(made, 1)
            pool.memset(m.ones_bf[:, :], 1.0)
            pool.memset(m.ones[:, :], 1.0)
            pool.memset(m.eps[:, :], EPS)
            pool.wait_ge(made, 3)
            pool.affine_select(out=m.ident[:, :], in_=m.ident[:, :], compare_op=ALU.not_equal, fill=1.0,
                               base=0, pattern=[[-1, P]], channel_multiplier=1).then_inc(made, 1)
            pool.affine_select(out=m.before[:, :], in_=m.before[:, :], compare_op=ALU.is_gt, fill=0.0,
                               base=0, pattern=[[1, P]], channel_multiplier=-1).then_inc(made, 1)

        @block.vector
        def _(v):
            v.wait_ge(made, 5)
            v.tensor_copy(m.iota_nodes[:, :], iota_i[:, :]).then_inc(cast, 1)
            v.tensor_copy(m.iota_windows[:, :], iota_i[:, 0:m.windows])
            v.tensor_copy(m.ident_bf[:, :], m.ident[:, :])
            v.tensor_copy(m.before_bf[:, :], m.before[:, :])
            v.wait_ge(cast, 1)
            v.tensor_tensor(m.table[:, 0, :], m.iota_nodes[:, :], m.ident[:, :], ALU.mult).then_inc(dve, 1)
            v.wait_ge(dve, 1)
            v.tensor_reduce(place[:, :], m.table[:, 0, :], AX.X, ALU.add).then_inc(dve, 1)
            v.wait_ge(loaded, 16 * len(loads))
            v.tensor_copy(ki_f[:, :], ki[:, :])
            v.tensor_copy(kj_f[:, :], kj[:, :])
            v.tensor_copy(ko_f[:, :], ko[:, :]).then_inc(dve, 1)
            v.tensor_scalar(m.w_f2[:, :], m.w_f2[:, :], 0.99 / SMU, None, ALU.mult)
            v.tensor_scalar(m.w_o2[:, :], m.w_o2[:, :], 0.99 / SMU, None, ALU.mult)
            v.tensor_scalar(m.b_o1_gelu[:, :], m.b_o1[:, :], SMU, None, ALU.mult)
            v.tensor_scalar(m.b_o1_lin[:, :], m.b_o1[:, :], SMU_LIN, None, ALU.mult)
            v.wait_ge(dve, 3)
            v.tensor_scalar(m.pick_in[:, :], ki_f[:, :], place[:, 0:1], None, ALU.is_equal)
            v.scalar_tensor_tensor(m.pick_sh[:, :], kj_f[:, :], place[0:NSH, 0:1], coeff[:, :],
                                   ALU.is_equal, ALU.mult)
            v.tensor_scalar(m.pick_out[:, :], m.iota_nodes[0:NPATH, :], ko_f[:, 0:1], None, ALU.is_equal)


def count_windows(nc, m, src_keys, dst_keys):
    W, T, TP = m.windows, m.edge_tiles, m.tiles
    with ExitStack() as ctx:
        def sem(name):
            return ctx.enter_context(nc.semaphore(name))

        keys_in, keys_done, split = sem("k_keys_in"), sem("k_keys_done"), sem("k_split")
        onehot, counted, scan = Steps(nc, ctx, "k_onehot"), Steps(nc, ctx, "k_counted", 1), sem("k_scan")
        based, tabled, blank_made = sem("k_based"), sem("k_tabled"), sem("k_blank_made")
        iotas, started_ready = sem("k_iotas"), sem("k_started_ready")
        halved, placed = sem("k_halved"), sem("k_placed")
        shifted, tile_iota, tile_iota_f, started = m.shifted, m.tile_iota, m.tile_iota_f, m.started
        oh = ctx.enter_context(nc.sbuf_tensor("count_onehot", [P, 2, 2, G, W], BF16))
        blank_d, blank_s, blanks_d, blanks_s = m.blank_d, m.blank_s, m.blanks_d, m.blanks_s
        n_i = ctx.enter_context(nc.sbuf_tensor("n_i", [W, 2], I32))
        n_t = ctx.enter_context(nc.sbuf_tensor("n_t", [W, 2], I32))
        n_f = ctx.enter_context(nc.sbuf_tensor("n_f", [W, 2], F32))
        base = ctx.enter_context(nc.sbuf_tensor("base", [W, 2], F32))
        base_slot = ctx.enter_context(nc.sbuf_tensor("base_slot", [W, 2], F32))
        banks = -(-max(T, TP) // BANK)
        pres = (m.pre_dst, m.pre_src)
        tile_windows = (m.tile_window_dst, m.tile_window_src)

        counts = [ctx.enter_context(nc.psum_tensor(f"counts{k}", [P, banks * BANK], F32)) for k in range(2)]
        with nc.Block() as block:
            @block.sync
            def _(sp):
                sp.dma_start(m.keys[:, 0, :], dst_keys).then_inc(keys_in, 16)
                sp.dma_start(m.keys[:, 1, :], src_keys).then_inc(keys_in, 16)
                sp.wait_ge(blank_made, 2)
                with sp.Fori(0, TP // BODY) as t:
                    sp.dma_start(m.by_dst.rearrange("(p t) c -> p t c", t=TP)[:, bass.ds(t * BODY, BODY), :],
                                 blank_d[:, :, :]).then_inc(blanks_d, 16)
                with sp.Fori(0, TP // BODY) as t:
                    sp.dma_start(m.by_src.rearrange("(p t) c -> p t c", t=TP)[:, bass.ds(t * BODY, BODY), :],
                                 blank_s[:, :, :]).then_inc(blanks_s, 16)

            @block.gpsimd
            def _(pool):
                pool.memset(blank_d[:, :, :], 0.0)
                pool.memset(blank_s[:, :, :], 0.0)
                pool.iota(tile_iota[:, :], pattern=[[1, TP]], base=0, channel_multiplier=0).then_inc(iotas, 1)
                pool.wait_ge(iotas, 1)
                pool.memset(blank_d[:, :, C_DLOC:C_DLOC + 1], -1.0)
                pool.memset(blank_d[:, :, C_SLOC:C_SLOC + 1], -1.0)
                pool.memset(blank_d[:, :, C_POS:C_POS + 1].bitcast(I32), int(FAR)).then_inc(blank_made, 1)
                pool.memset(blank_s[:, :, S_SLOC:S_SLOC + 1], -1.0).then_inc(blank_made, 1)

            @block.vector
            def _(v):
                v.wait_ge(keys_in, 32)
                v.tensor_scalar(shifted[:, :, :], m.keys, 7, None, ALU.arith_shift_right).then_inc(split, 1)
                v.wait_ge(split, 1)
                v.tensor_copy(m.key_windows, shifted[:, :, :]).then_inc(split, 1)
                v.wait_ge(split, 2)

                def make_onehot(q, k):
                    v.wait_ge(counted.sem, counted.before_reuse(q, 2))
                    v.tensor_tensor(
                        oh[:, k, :, :, :],
                        m.key_windows[:, :, bass.ds(q * G, G)].unsqueeze(3).to_broadcast([P, 2, G, W]),
                        m.iota_windows[:, :].unsqueeze(1).unsqueeze(1).to_broadcast([P, 2, G, W]),
                        ALU.is_equal).then_inc(onehot.sem, 1)

                in_step(v, T // G, 2, (0, make_onehot))

            @block.tensor
            def _(pe):
                def count(q, k):
                    pe.wait_ge(onehot.sem, onehot.after(q))
                    for key in range(2):
                        for j in range(G):
                            last = pe.matmul(counts[key][0:W, bass.ds(q * G + j, 1)], oh[:, k, key, j, :],
                                             m.ones_bf[:, 0:1], start=True, stop=True)
                    last.then_inc(counted.sem, 1)

                counted.start(pe)
                in_step(pe, T // G, 2, (0, count))

        with nc.Block() as block:
            @block.vector
            def _(v):
                v.tensor_copy(tile_iota_f[:, :], tile_iota[:, :]).then_inc(iotas, 1)
                for k, pre in enumerate(pres):
                    v.tensor_tensor_scan(pre, m.ones[0:W, 0:1].to_broadcast([W, T]), counts[k][0:W, 0:T],
                                         0.0, ALU.mult, ALU.add).then_inc(scan, 1)
                v.wait_ge(scan, 2)
                for k, pre in enumerate(pres):
                    v.tensor_scalar(n_i[:, k:k + 1], pre[:, T - 1:T], float(P - 1), None, ALU.add).then_inc(scan, 1)
                v.wait_ge(scan, 4)
                v.tensor_scalar(n_t[:, :], n_i[:, :], 7, None, ALU.arith_shift_right).then_inc(scan, 1)
                v.wait_ge(scan, 5)
                v.tensor_copy(n_f[:, :], n_t[:, :]).then_inc(scan, 1)
                for k, pre in enumerate(pres):
                    v.tensor_tensor(pre, pre, counts[k][0:W, 0:T], ALU.subtract).then_inc(scan, 1)
                v.wait_ge(scan, 8)

        with nc.Block() as block:
            @block.tensor
            def _(pe):
                pe.matmul(counts[0][0:W, 0:2], m.before[0:W, 0:W], n_f[:, :], start=True, stop=True).then_inc(based, 1)
                for k in range(2):
                    pe.wait_ge(started_ready, k + 1)
                    for c in range(0, TP, BANK):
                        n = min(BANK, TP - c)
                        last = pe.matmul(counts[1 - k][0:1, c:c + n], m.ones_bf[0:W, 0:1], started[:, c:c + n],
                                         start=True, stop=True)
                    last.then_inc(tabled, 1)

            @block.vector
            def _(v):
                v.wait_ge(based, 1)
                v.tensor_copy(base[:, :], counts[0][0:W, 0:2]).then_inc(based, 1)
                v.wait_ge(based, 2)
                v.tensor_scalar(base_slot[:, :], base[:, :], float(P), None, ALU.mult).then_inc(based, 1)
                v.wait_ge(based, 3)
                for k, pre in enumerate(pres):
                    v.tensor_scalar(pre, pre, base_slot[:, k:k + 1], None, ALU.add).then_inc(based, 1)
                    if k:
                        v.wait_ge(tabled, k)
                    v.tensor_scalar(started[:, :], tile_iota_f[:, :], base[:, k:k + 1], None,
                                    ALU.is_ge).then_inc(started_ready, 1)
                n = 0
                for k, pre in enumerate(pres):
                    for half, (op, by) in enumerate(((ALU.arith_shift_right, 7), (ALU.bitwise_and, P - 1))):
                        if not half:
                            v.wait_ge(based, 4 + k)
                            v.wait_ge(placed, 3 * k)
                            v.tensor_copy(pre.bitcast(I32), pre).then_inc(placed, 1)
                        v.wait_ge(placed, n + k + 1)
                        v.tensor_scalar(m.some_slots, pre.bitcast(I32), by, None, op).then_inc(halved, 1)
                        v.wait_ge(halved, n + 1)
                        v.tensor_copy(m.next_slot[:, k, :, half], m.some_slots).then_inc(placed, 1)
                        n += 1
                for k, tile_window in enumerate(tile_windows):
                    v.wait_ge(tabled, k + 1)
                    v.tensor_scalar(tile_window[:, :], counts[1 - k][0:1, 0:TP], -1.0, None, ALU.add)


def order_edges(nc, m, edges):
    W, T, TP = m.windows, m.edge_tiles, m.tiles
    with ExitStack() as ctx:
        def sb(name, shape, dt=F32):
            return ctx.enter_context(nc.sbuf_tensor(name, shape, dt))

        def bank(name, shape, dt=F32):
            return ctx.enter_context(nc.psum_tensor(name, shape, dt))

        rows = sb("o_rows", [P, SLOTS, G, ROW])
        index = sb("o_index", [P, SLOTS, G], I32)
        oh = sb("o_onehot", [P, 2, 2, G, W], BF16)
        oh_t = sb("o_onehot_t", [W, 2, 2 * G * P], BF16)
        place_in = sb("o_place_in", [P, 2, 2, G])
        prod = sb("o_prod", [P, 2, G, W])
        rank = sb("o_rank", [P, 2, 2, G])
        slot_i = sb("o_slot_i", [P, 2, G], I32)
        lo = sb("o_lo", [P, 2, G], I32)
        hi = sb("o_hi", [P, 2, G], I32)
        row = sb("o_row", [P, 2, G])
        none = sb("o_none", [P, G])
        rank_ps = [[bank(f"o_rank_ps{b}{k}", [P, BANK]) for k in range(2)] for b in range(2)]
        oh_t_ps = bank("o_onehot_t_ps", [P, 2 * BANK], BF16)
        look_ps = [bank(f"o_look_ps{b}", [P, BANK]) for b in range(2)]

        row_in, sent = m.row_in, m.moved
        row_in.use(SLOTS, 1)
        sent.use(SLOTS, G)
        onehot = Steps(nc, ctx, "o_onehot_made")
        turned = Steps(nc, ctx, "o_turned", before=1)
        copied = Steps(nc, ctx, "o_copied", before=1)
        looked = Steps(nc, ctx, "o_looked", before=1)
        multiplied = Steps(nc, ctx, "o_multiplied", before=1)
        ranked = Steps(nc, ctx, "o_ranked", before=1)
        slotted = Steps(nc, ctx, "o_slotted", before=1)
        summed = Steps(nc, ctx, "o_summed", before=1)
        halved = Steps(nc, ctx, "o_halved", before=1)
        rowed = Steps(nc, ctx, "o_rowed", before=1)
        placed = Steps(nc, ctx, "o_placed", before=1)
        block = ctx.enter_context(nc.Block())

        @block.sync
        def _(sp):
            def load(q, k):
                wait_apart(m, sp, sent.sems[k], sent.before(q, k))
                sp.dma_start(rows[:, k, :, :], tiles_of(edges, T, q * G, 0, ROW)).then_inc(row_in.sems[k], 16)

            in_step(sp, T // G, SLOTS, (SLOTS, load))
            sp.wait_ge(m.blanks_s, m.blanks)

        @block.vector
        def _(v):
            def make_onehot(q, k):
                v.wait_ge(turned.sem, turned.before_reuse(q, 2))
                v.wait_ge(multiplied.sem, multiplied.before_reuse(q, 2))
                v.tensor_tensor(
                    oh[:, k % 2, :, :, :],
                    m.key_windows[:, :, bass.ds(q * G, G)].unsqueeze(3).to_broadcast([P, 2, G, W]),
                    m.iota_windows[:, :].unsqueeze(1).unsqueeze(1).to_broadcast([P, 2, G, W]),
                    ALU.is_equal).then_inc(onehot.sem, 1)

            def multiply(q, k):
                b = k % 2
                v.wait_ge(ranked.sem, ranked.before_reuse(q, 1))
                v.wait_ge(turned.sem, turned.after(q))
                for key in range(2):
                    last = v.tensor_tensor(prod[:, key, :, :],
                                           rank_ps[b][key][:, 0:G * W].rearrange("p (g w) -> p g w", g=G),
                                           oh[:, b, key, :, :], ALU.mult)
                last.then_inc(multiplied.sem, 1)

            def reduce(q, k):
                v.wait_ge(summed.sem, summed.before_reuse(q, 2))
                v.wait_ge(multiplied.sem, multiplied.after(q))
                v.tensor_reduce(rank[:, k % 2, :, :], prod[:, :, :, :], AX.X, ALU.add).then_inc(ranked.sem, 1)

            def looked_up(q, k):
                return look_ps[k % 2][:, 0:4 * G].rearrange("p (k g c) -> p k g c", k=2, c=2)

            def add_rank(q, k):
                v.wait_ge(slotted.sem, slotted.before_reuse(q, 2))
                v.wait_ge(ranked.sem, ranked.after(q))
                v.wait_ge(looked.sem, looked.after(q))
                v.tensor_tensor(place_in[:, k % 2, :, :], rank[:, k % 2, :, :], looked_up(q, k)[:, :, :, 1],
                                ALU.add).then_inc(summed.sem, 1)

            def find_slot(q, k):
                v.wait_ge(halved.sem, halved.before_reuse(q, 1))
                v.wait_ge(summed.sem, summed.after(q))
                v.scalar_tensor_tensor(slot_i[:, :, :], looked_up(q, k)[:, :, :, 0], float(P),
                                       place_in[:, k % 2, :, :], ALU.mult, ALU.add).then_inc(slotted.sem, 1)

            def fill_in(q, k):
                keys, windows = m.keys[:, :, bass.ds(q * G, G)], m.key_windows[:, :, bass.ds(q * G, G)]
                v.wait_ge(row_in.sems[k], row_in.after(q, k))
                v.scalar_tensor_tensor(
                    rows[:, k, :, C_DLOC:C_SLOC + 1:C_SLOC - C_DLOC].rearrange("p g k -> p k g"),
                    windows, -float(P), keys, ALU.mult, ALU.add)
                v.tensor_copy(rows[:, k, :, C_DST], keys[:, 0, :])
                v.wait_ge(placed.sem, placed.before_reuse(q, 1))
                v.tensor_scalar(none[:, :], windows[:, 0, :], 0.0, FAR, ALU.is_lt, ALU.mult)

            def halve(q, k):
                v.wait_ge(rowed.sem, rowed.before_reuse(q, 1))
                v.wait_ge(slotted.sem, slotted.after(q))
                v.tensor_scalar(lo[:, :, :], slot_i[:, :, :], P - 1, None, ALU.bitwise_and)
                v.tensor_scalar(hi[:, :, :], slot_i[:, :, :], 7, None, ALU.arith_shift_right).then_inc(halved.sem, 1)

            def make_row(q, k):
                v.wait_ge(placed.sem, placed.before_reuse(q, 1))
                v.wait_ge(halved.sem, halved.after(q))
                v.scalar_tensor_tensor(row[:, :, :], lo[:, :, :], float(TP), hi[:, :, :], ALU.mult,
                                       ALU.add).then_inc(rowed.sem, 1)

            def place(q, k):
                v.wait_ge(rowed.sem, rowed.after(q))
                v.tensor_copy(rows[:, k, :, C_POS].bitcast(I32), row[:, 1, :])
                v.tensor_tensor(index[:, k, :], row[:, 0, :], none[:, :], ALU.add).then_inc(placed.sem, 1)

            multiplied.start(v)
            ranked.start(v)
            slotted.start(v)
            summed.start(v)
            placed.start(v)
            halved.start(v)
            rowed.start(v)
            in_step(v, T // G, SLOTS, (2, make_onehot), (0, add_rank), (0, fill_in), (0, find_slot),
                    (1, multiply), (0, halve), (1, reduce), (0, make_row), (0, place))

        @block.tensor
        def _(pe):
            def rank_and_turn(q, k):
                b = k % 2
                pe.wait_ge(multiplied.sem, multiplied.before_reuse(q, 2))
                pe.wait_ge(onehot.sem, onehot.after(q))
                for key in range(2):
                    pe.matmul(rank_ps[b][key][:, 0:G * W], m.before_bf[:, :],
                              oh[:, b, key, :, :].rearrange("p g w -> p (g w)"), start=True, stop=True)
                pe.wait_ge(copied.sem, copied.before_reuse(q, 1))
                for key in range(2):
                    for j in range(G):
                        c = (key * G + j) * P
                        last = pe.transpose(oh_t_ps[0:W, c:c + P], oh[:, b, key, j, :], m.ident_bf[:, :])
                last.then_inc(turned.sem, 1)

            def look_up(q, k):
                b = k % 2
                pe.wait_ge(slotted.sem, slotted.before_reuse(q, 2))
                pe.wait_ge(copied.sem, copied.after(q))
                for key in range(2):
                    for j in range(G):
                        c = key * G + j
                        last = pe.matmul(look_ps[b][:, 2 * c:2 * c + 2], oh_t[:, b, c * P:(c + 1) * P],
                                         m.next_slot[:, key, bass.ds(q * G + j, 1), :].rearrange("w t c -> w (t c)"),
                                         start=True, stop=True)
                last.then_inc(looked.sem, 1)

            turned.start(pe)
            looked.start(pe)
            in_step(pe, T // G, SLOTS, (2, rank_and_turn), (1, look_up))

        @block.scalar
        def _(act):
            def copy(q, k):
                act.wait_ge(looked.sem, looked.before_reuse(q, 2))
                act.wait_ge(turned.sem, turned.after(q))
                act.activation(oh_t[:, k % 2, :], oh_t_ps[0:W, :], ACT.Copy).then_inc(copied.sem, 1)

            copied.start(act)
            in_step(act, T // G, SLOTS, (1, copy))

        @block.gpsimd
        def _(pool):
            def send(q, k):
                pool.wait_ge(m.blanks_d, m.blanks)
                wait_apart(m, pool, placed.sem, placed.after(q))
                for j in range(G):
                    pool.indirect_dma_start(
                        m.by_dst, bass.IndirectOffsetOnAxis(ap=index[:, k, j:j + 1], axis=0),
                        rows[:, k, j, :], None, bounds_check=P * TP - 1, oob_is_err=False
                    ).then_inc(sent.sems[k], 16)

            in_step(pool, T // G, SLOTS, (0, send))
            for k in range(SLOTS):
                pool.wait_ge(sent.sems[k], sent.after(T // G - SLOTS + k, k))
        row_in.again(T // G)
        sent.again(T // G)


def take_stats(v, m, w):
    return v.bn_stats(m.stats[:, bass.ds(w, 1), :].rearrange("p w s -> p (w s)"),
                      m.x[:, bass.ds(w, 1), :].rearrange("p w f -> p (w f)"))


def first_stats(nc, m):
    with nc.Block() as block:
        @block.vector
        def _(v):
            in_step(v, m.windows, 14, (0, lambda w, k: take_stats(v, m, w)))


def normalise(nc, m, layer):
    with ExitStack() as ctx:
        chain, rooted = m.norm_chain, m.norm_rooted
        done = 6 * layer
        block = ctx.enter_context(nc.Block())
        mean_even, mean_odd = m.stats[:, :, 1], m.stats[:, :, 4]
        square_even, square_odd = m.stats[:, :, 2], m.stats[:, :, 5]
        total, gap, std = m.mean, m.gap, m.std

        @block.vector
        def _(v):
            v.tensor_tensor(gap[:, :], mean_even, mean_odd, ALU.subtract).then_inc(chain, 1)
            v.tensor_tensor(total[:, :], mean_even, mean_odd, ALU.add)
            v.tensor_tensor(std[:, :], square_even, square_odd, ALU.add)
            v.wait_ge(chain, done + 1)
            v.scalar_tensor_tensor(gap[:, :], gap[:, :], F / 4.0, gap[:, :], ALU.mult, ALU.mult).then_inc(chain, 1)
            v.wait_ge(chain, done + 2)
            v.tensor_tensor(std[:, :], std[:, :], gap[:, :], ALU.add).then_inc(chain, 1)
            v.wait_ge(rooted, layer + 1)
            v.reciprocal(m.rstd[:, :], std[:, :]).then_inc(chain, 1)
            v.wait_ge(chain, done + 4)
            v.scalar_tensor_tensor(m.shift[:, :], total[:, :], -0.5, m.rstd[:, :], ALU.mult,
                                   ALU.mult).then_inc(chain, 1)
            v.wait_ge(chain, done + 5)
            v.sem_inc(chain, 1)

        @block.scalar
        def _(act):
            act.wait_ge(chain, done + 3)
            act.activation(std[:, :], std[:, :], ACT.Sqrt, bias=m.eps[:, 0:1], scale=1.0 / F).then_inc(rooted, 1)


def relu_of(act, m, to, w):
    return act.activation(to, m.x[:, bass.ds(w, 1), :].rearrange("p w f -> p (w f)"), ACT.Relu,
                          bias=m.shift[:, bass.ds(w, 1)], scale=m.rstd[:, bass.ds(w, 1)])


def project(nc, m, layer, weights, columns, bias, kept, rows_out, out_columns):
    W = m.windows
    with ExitStack() as ctx:
        def sb(name, shape, dt=F32):
            return ctx.enter_context(nc.sbuf_tensor(name, shape, dt))

        h = sb(f"p_h_{layer}", [P, SLOTS, F])
        h_t = sb(f"p_h_t_{layer}", [F, SLOTS, P])
        away = sb(f"p_away_{layer}", [P, SLOTS, out_columns or 2])
        turn_ps = [ctx.enter_context(nc.psum_tensor(f"p_turn{b}_{layer}", [P, BANK], F32)) for b in range(SLOTS)]
        prod_ps = [ctx.enter_context(nc.psum_tensor(f"p_prod{b}_{layer}", [P, BANK], F32)) for b in range(SLOTS)]
        relued, turned, copied, multiplied, taken = m.project_steps
        stored = m.row_in
        stored.use(SLOTS, 1)
        block = ctx.enter_context(nc.Block())

        @block.scalar
        def _(act):
            def relu(w, b):
                act.wait_ge(turned.sem, turned.before_reuse(w, SLOTS))
                relu_of(act, m, h[:, b, :], w).then_inc(relued.sem, 1)

            in_step(act, W, SLOTS, (1, relu))

        @block.tensor
        def _(pe):
            def turn(w, b):
                pe.wait_ge(copied.sem, copied.before_reuse(w, SLOTS))
                pe.wait_ge(relued.sem, relued.after(w))
                pe.transpose(turn_ps[b][:, 0:P], h[:, b, :], m.ident[:, :]).then_inc(turned.sem, 1)

            def multiply(w, b):
                pe.wait_ge(taken.sem, taken.before_reuse(w, SLOTS))
                pe.wait_ge(copied.sem, copied.after(w))
                pe.matmul(prod_ps[b][:, 0:columns], h_t[:, b, :], weights, start=True,
                          stop=True).then_inc(multiplied.sem, 1)

            turned.start(pe)
            multiplied.start(pe)
            in_step(pe, W, SLOTS, (2, turn), (0, multiply))

        @block.vector
        def _(v):
            def copy(w, b):
                v.wait_ge(multiplied.sem, multiplied.before_reuse(w, SLOTS))
                v.wait_ge(turned.sem, turned.after(w))
                v.tensor_copy(h_t[:, b, :], turn_ps[b][:, 0:P]).then_inc(copied.sem, 1)

            def take(w, b):
                if out_columns:
                    v.wait_ge(stored.sems[b], stored.before(w, b))
                v.wait_ge(multiplied.sem, multiplied.after(w))
                window = m.table[:, bass.ds(w, 1), :].rearrange("p w f -> p (w f)")
                if kept and bias is not None:
                    last = v.tensor_tensor(window, prod_ps[b][:, 0:kept], bias, ALU.add)
                elif kept:
                    last = v.tensor_copy(window, prod_ps[b][:, 0:kept])
                if out_columns:
                    last = v.tensor_copy(away[:, b, :], prod_ps[b][:, kept:kept + out_columns])
                last.then_inc(taken.sem, 1)

            copied.start(v)
            taken.start(v)
            in_step(v, W, SLOTS, (2, copy), (0, take))

        if out_columns:
            @block.sync
            def _(sp):
                def store(w, b):
                    wait_apart(m, sp, taken.sem, taken.after(w))
                    sp.dma_start(rows_out.rearrange("(w p) c -> p w c", p=P)[:, bass.ds(w, 1), :],
                                 away[:, b:b + 1, :]).then_inc(stored.sems[b], 16)

                in_step(sp, W, SLOTS, (0, store))
                for w in range(W - SLOTS, W):
                    sp.wait_ge(stored.sems[w % SLOTS], stored.after(w, w % SLOTS))
            stored.again(W)
        for steps in m.project_steps:
            steps.again(W)


def update_nodes(nc, m, layer):
    W = m.windows
    K = NPATH if layer == 3 else F
    with ExitStack() as ctx:
        def sb(name, shape, dt=F32):
            return ctx.enter_context(nc.sbuf_tensor(name, shape, dt))

        sums = sb(f"u_sums_{layer}", [P, SLOTS, K])
        sums_t = sb(f"u_sums_t_{layer}", [K, SLOTS, P])
        gelu = sb(f"u_gelu_{layer}", [F, SLOTS, P])
        line = sb(f"u_line_{layer}", [F, SLOTS, P])
        smu = sb(f"u_smu_{layer}", [F, SLOTS, P])
        part = sb(f"u_part_{layer}", [P, SLOTS, F])
        spread = 2 if layer == 0 else SLOTS
        turn_ps, hid_ps, out_ps = (
            [ctx.enter_context(nc.psum_tensor(f"u_{n}{b}_{layer}", [P, BANK], F32))[:, 0:P] for b in range(count)]
            for n, count in (("turn", spread), ("hidden", spread if layer == 0 else 0), ("out", SLOTS)))
        staged, turned = Steps(nc, ctx, f"u_staged_{layer}"), Steps(nc, ctx, f"u_turned_{layer}", 3)
        copied, mapped = Steps(nc, ctx, f"u_copied_{layer}", 3), Steps(nc, ctx, f"u_mapped_{layer}", 3)
        parted, added = Steps(nc, ctx, f"u_parted_{layer}"), Steps(nc, ctx, f"u_added_{layer}", 3)
        if layer == 0:
            hidden, bent, summed = (Steps(nc, ctx, f"u_{n}", 3) for n in ("hidden", "bent", "summed"))
        weights = {0: m.w_o2, 1: m.w2, 3: m.pick_out}[layer]
        block = ctx.enter_context(nc.Block())

        @block.scalar
        def _(act):
            def stage(w, b):
                act.wait_ge(turned.sem, turned.before_reuse(w, SLOTS))
                act.activation(sums[:, b, :], m.acc[:, bass.ds(w, 1), 0:K].rearrange("p w f -> p (w f)"),
                               ACT.Copy).then_inc(staged.sem, 1)

            def bend(w, b):
                act.wait_ge(summed.sem, summed.before_reuse(w, SLOTS))
                act.wait_ge(hidden.sem, hidden.after(w))
                act.activation(gelu[:, b, :], hid_ps[b % spread], ACT.Gelu, bias=m.b_o1_gelu[:, 0:1], scale=SMU)
                act.activation(line[:, b, :], hid_ps[b % spread], ACT.Identity, bias=m.b_o1_lin[:, 0:1],
                               scale=SMU_LIN).then_inc(bent.sem, 1)

            if layer == 0:
                bent.start(act)
                in_step(act, W, SLOTS, (4, stage), (2, bend))
            else:
                in_step(act, W, SLOTS, (2, stage))

        @block.tensor
        def _(pe):
            def turn(w, b):
                pe.wait_ge(copied.sem, copied.before_reuse(w, spread))
                wait_apart(m, pe, staged.sem, staged.after(w))
                pe.transpose(turn_ps[b % spread][0:K, :], sums[:, b, :], m.ident[:, :]).then_inc(turned.sem, 1)

            def hide(w, b):
                pe.wait_ge(bent.sem, bent.before_reuse(w, spread))
                pe.wait_ge(copied.sem, copied.after(w))
                pe.matmul(hid_ps[b % spread], m.w_o1[:, :], sums_t[:, b, :], start=True,
                          stop=True).then_inc(hidden.sem, 1)

            def map_out(w, b):
                pe.wait_ge(added.sem, added.before_reuse(w, SLOTS))
                if layer == 0:
                    pe.wait_ge(summed.sem, summed.after(w))
                    left = smu[:, b, :]
                else:
                    pe.wait_ge(copied.sem, copied.after(w))
                    left = sums_t[:, b, :]
                pe.matmul(out_ps[b], left, weights[:, :], start=True, stop=True).then_inc(mapped.sem, 1)

            turned.start(pe)
            mapped.start(pe)
            if layer == 0:
                hidden.start(pe)
                in_step(pe, W, SLOTS, (4, turn), (2, hide), (0, map_out))
            else:
                in_step(pe, W, SLOTS, (2, turn), (0, map_out))

        @block.vector
        def _(v):
            def copy(w, b):
                reader = hidden if layer == 0 else mapped
                v.wait_ge(reader.sem, reader.before_reuse(w, SLOTS))
                v.wait_ge(turned.sem, turned.after(w))
                v.tensor_copy(sums_t[:, b, :], turn_ps[b % spread][0:K, :]).then_inc(copied.sem, 1)

            def sum_smu(w, b):
                v.wait_ge(mapped.sem, mapped.before_reuse(w, SLOTS))
                v.wait_ge(bent.sem, bent.after(w))
                v.tensor_tensor(smu[:, b, :], gelu[:, b, :], line[:, b, :], ALU.add).then_inc(summed.sem, 1)

            def part_up(w, b):
                out = out_ps[b]
                v.wait_ge(mapped.sem, mapped.after(w))
                if layer == 0:
                    v.tensor_tensor(part[:, b, :], m.b_o2[:, :], out, ALU.add).then_inc(parted.sem, 1)
                else:
                    v.scalar_tensor_tensor(part[:, b, :], m.b2[:, :],
                                           m.acc[:, bass.ds(w, 1), F:F + 1].rearrange("p w f -> p (w f)"), out,
                                           ALU.mult, ALU.add).then_inc(parted.sem, 1)

            def add(w, b):
                if layer == 3:
                    v.wait_ge(mapped.sem, mapped.after(w))
                    of = out_ps[b]
                else:
                    v.wait_ge(parted.sem, parted.after(w))
                    of = part[:, b, :]
                node = m.x[:, bass.ds(w, 1), :].rearrange("p w f -> p (w f)")
                v.tensor_tensor(node, node, of, ALU.add).then_inc(added.sem, 1)

            def stats(w, b):
                v.wait_ge(added.sem, added.after(w))
                take_stats(v, m, w)

            copied.start(v)
            added.start(v)
            if layer == 0:
                summed.start(v)
                in_step(v, W, SLOTS, (1, part_up), (5, copy), (3, sum_smu), (1, add), (0, stats))
            elif layer == 1:
                in_step(v, W, SLOTS, (1, part_up), (3, copy), (1, add), (0, stats))
            else:
                in_step(v, W, SLOTS, (0, add), (2, copy))


def layer0_messages(nc, m):
    W, TP, N = m.windows, m.tiles, m.tiles // G
    with ExitStack() as ctx:
        def sb(name, shape, dt=F32):
            return ctx.enter_context(nc.sbuf_tensor(name, shape, dt))

        def bank(name):
            return ctx.enter_context(nc.psum_tensor(name, [P, BANK], F32))

        rows = sb("a_rows", [P, DEEP, G, ROW])
        index = sb("a_index", [P, SLOTS, G], I32)
        GP = G * P
        out, oh, oh_t, rbf_t, gelu, smu, own, filt = parts_of(
            m.acc, SLOTS * G * SROW, 2 * GP, SLOTS * GP, 2 * GP, 2 * GP, 2 * GP, 2 * GP, 2 * GP)
        out = out.rearrange("p (s g c) -> p s g c", s=SLOTS, g=G)
        oh = oh.bitcast(BF16).rearrange("p (s g f) -> p s g f", s=SLOTS, g=G)
        own, filt = (a.rearrange("p (b g f) -> p b g f", b=2, g=G) for a in (own, filt))
        gelu, smu = (a.rearrange("p (b e) -> p b e", b=2) for a in (gelu, smu))
        oh_t = oh_t.rearrange("p (s e) -> p s e", s=SLOTS)
        rbf_t = rbf_t[0:NRBF + 1, :].rearrange("p (b e) -> p b e", b=2)
        oh_t_ps = ctx.enter_context(nc.psum_tensor("a_onehot_t_ps", [P, BANK], BF16))
        rbf_t_ps = bank("a_rbf_t_ps")
        hid_ps = [bank(f"a_hidden{b}") for b in range(2)]
        own_ps = [bank(f"a_own_ps{b}") for b in range(2)]
        filt_ps = [bank(f"a_filt_ps{b}") for b in range(2)]

        row_in, sent = m.row_in, m.moved
        row_in.use(DEEP, 1)
        sent.use(SLOTS, G)
        onehot = Steps(nc, ctx, "a_onehot_made", before=1)
        turned = Steps(nc, ctx, "a_turned", before=3)
        copied = Steps(nc, ctx, "a_copied", before=1)
        hidden = Steps(nc, ctx, "a_hidden", before=1)
        gelued = Steps(nc, ctx, "a_gelued", before=1)
        smued = Steps(nc, ctx, "a_smued", before=1)
        filtered = Steps(nc, ctx, "a_filtered", before=3)
        scaled = Steps(nc, ctx, "a_scaled", before=7)
        biased = Steps(nc, ctx, "a_biased", before=1)
        made = Steps(nc, ctx, "a_made", before=7)
        block = ctx.enter_context(nc.Block())

        @block.sync
        def _(sp):
            def load(q, k):
                sp.wait_ge(scaled.sem, scaled.before_reuse(q, DEEP))
                wait_apart(m, sp, made.sem, made.before_reuse(q, DEEP))
                sp.dma_start(rows[:, k, :, :], tiles_of(m.by_dst, TP, q * G, 0, ROW)).then_inc(row_in.sems[k], 16)

            in_step(sp, N, DEEP, (0, load))

        @block.vector
        def _(v):
            def bias(q, k):
                v.wait_ge(made.sem, made.before_reuse(q, 2))
                v.wait_ge(filtered.sem, filtered.after(q))
                v.tensor_tensor(filt[:, k % 2, :, :], filt_ps[k % 2][:, :].rearrange("p (g f) -> p g f", g=G),
                                m.b_f2[:, :].unsqueeze(1).to_broadcast([P, G, F]), ALU.add).then_inc(biased.sem, 1)

            def make_onehot(q, k):
                v.wait_ge(row_in.sems[k], row_in.after(q, k))
                v.wait_ge(turned.sem, turned.before_reuse(q, SLOTS))
                v.tensor_tensor(oh[:, k % SLOTS, :, :], rows[:, k, :, C_DLOC:C_DLOC + 1].to_broadcast([P, G, P]),
                                m.iota_nodes[:, :].unsqueeze(1).to_broadcast([P, G, P]),
                                ALU.is_equal).then_inc(onehot.sem, 1)

            def message(q, k):
                s = k % SLOTS
                v.wait_ge(sent.sems[s], sent.before(q, s))
                v.tensor_copy(index[:, s, :], rows[:, k, :, C_POS].bitcast(I32))
                v.wait_ge(scaled.sem, scaled.after(q))
                v.wait_ge(biased.sem, biased.after(q))
                v.tensor_tensor(out[:, s, :, 0:F], filt[:, k % 2, :, :], own[:, k % 2, :, :],
                                ALU.mult).then_inc(made.sem, 1)

            def sum_smu(q, k):
                b = k % 2
                v.wait_ge(filtered.sem, filtered.before_reuse(q, 2))
                v.wait_ge(gelued.sem, gelued.after(q))
                v.scalar_tensor_tensor(smu[:, b, :], hid_ps[b][:, :], SMU_LIN, gelu[:, b, :], ALU.mult,
                                       ALU.add).then_inc(smued.sem, 1)

            smued.start(v)
            biased.start(v)
            made.start(v)
            onehot.start(v)
            in_step(v, N, DEEP, (0, bias), (4, make_onehot), (0, message), (2, sum_smu))

        @block.tensor
        def _(pe):
            def hide(q, k):
                pe.wait_ge(copied.sem, copied.after(q))
                pe.wait_ge(smued.sem, smued.before_reuse(q, 2))
                pe.matmul(hid_ps[k % 2][:, :], m.w_f1[:, :], rbf_t[:, k % 2, :], start=True,
                          stop=True).then_inc(hidden.sem, 1)

            def turn(q, k):
                pe.wait_ge(copied.sem, copied.before_reuse(q, 1))
                pe.wait_ge(onehot.sem, onehot.after(q))
                for j in range(G):
                    pe.transpose(rbf_t_ps[0:NRBF + 1, j * P:(j + 1) * P], rows[:, k, j, C_RBF:C_ONE + 1],
                                 m.ident[:, :])
                    last = pe.transpose(oh_t_ps[:, j * P:(j + 1) * P], oh[:, k % SLOTS, j, :], m.ident_bf[:, :])
                last.then_inc(turned.sem, 1)

            def products(q, k):
                b = k % 2
                windows = window_registers(nc, pe, m.tile_window_dst, q * G, W)
                pe.wait_ge(scaled.sem, scaled.before_reuse(q, 2))
                pe.wait_ge(biased.sem, biased.before_reuse(q, 2))
                for j in range(G):
                    pe.matmul(own_ps[b][:, j * F:(j + 1) * F], oh_t[:, k % SLOTS, j * P:(j + 1) * P],
                              m.table[:, bass.ds(windows[j], 1), :].rearrange("p w f -> p (w f)"),
                              start=True, stop=True)
                pe.wait_ge(smued.sem, smued.after(q))
                for j in range(G):
                    last = pe.matmul(filt_ps[b][:, j * F:(j + 1) * F], smu[:, b, j * P:(j + 1) * P],
                                     m.w_f2[:, :], start=True, stop=True)
                last.then_inc(filtered.sem, 1)

            turned.start(pe)
            hidden.start(pe)
            filtered.start(pe)
            in_step(pe, N, DEEP, (2, hide), (3, turn), (1, products))

        @block.scalar
        def _(act):
            def scale(q, k):
                b, s = k % 2, k % SLOTS
                act.wait_ge(sent.sems[s], sent.before(q, s))
                act.activation(out[:, s, :, F:SROW], rows[:, k, :, C_EF:C_EF + CARRY], ACT.Copy)
                act.wait_ge(made.sem, made.before_reuse(q, 2))
                act.wait_ge(filtered.sem, filtered.after(q))
                for j in range(G):
                    last = act.activation(own[:, b, j, :], own_ps[b][:, j * F:(j + 1) * F], ACT.Copy,
                                          scale=rows[:, k, j, C_WEIGHT:C_WEIGHT + 1])
                last.then_inc(scaled.sem, 1)

            def bend(q, k):
                act.wait_ge(smued.sem, smued.before_reuse(q, 2))
                act.wait_ge(hidden.sem, hidden.after(q))
                act.activation(gelu[:, k % 2, :], hid_ps[k % 2][:, :], ACT.Gelu, scale=SMU).then_inc(gelued.sem, 1)

            def copy(q, k):
                act.wait_ge(hidden.sem, hidden.before_reuse(q, 2))
                act.wait_ge(filtered.sem, filtered.before_reuse(q, SLOTS))
                act.wait_ge(turned.sem, turned.after(q))
                act.activation(rbf_t[:, k % 2, :], rbf_t_ps[0:NRBF + 1, :], ACT.Copy)
                act.activation(oh_t[:, k % SLOTS, :], oh_t_ps[:, :], ACT.Copy).then_inc(copied.sem, 1)

            copied.start(act)
            gelued.start(act)
            scaled.start(act)
            in_step(act, N, DEEP, (0, scale), (2, bend), (3, copy))

        @block.gpsimd
        def _(pool):
            def send(q, k):
                pool.wait_ge(m.blanks_s, m.blanks)
                pool.wait_ge(scaled.sem, scaled.after(q))
                wait_apart(m, pool, made.sem, made.after(q))
                for j in range(G):
                    pool.indirect_dma_start(
                        m.by_src, bass.IndirectOffsetOnAxis(ap=index[:, k, j:j + 1], axis=0),
                        out[:, k, j, :], None, bounds_check=P * TP - 1, oob_is_err=False
                    ).then_inc(sent.sems[k], 16)

            in_step(pool, N, SLOTS, (0, send))
            for k in range(SLOTS):
                pool.wait_ge(sent.sems[k], sent.after(N - SLOTS + k, k))
        row_in.again(N)
        sent.again(N)


def adding(nc, v, m, added, tile_window, totals_ps, columns):
    windows = [None] * G

    def add(j, q, k):
        acc = m.acc[:, bass.ds(windows[j], 1), 0:columns].rearrange("p w f -> p (w f)")
        v.wait_ge(added.sem, added.after(q) - added.per + j)
        v.tensor_tensor(acc, acc, totals_ps(k, j), ALU.add).then_inc(added.sem, 1)

    def add_first(summed):
        def stage(q, k):
            windows[:] = window_registers(nc, v, tile_window, q * G, m.windows)
            v.wait_ge(summed.sem, summed.after(q))
            add(0, q, k)
        return stage

    def add_next(j):
        return lambda q, k: add(j, q, k)

    return add_first, add_next


def layer0_sums(nc, m):
    TP, N = m.tiles, m.tiles // G
    with ExitStack() as ctx:
        rows = ctx.enter_context(nc.sbuf_tensor("b_rows_in", [P, SLOTS, G, SROW], F32))
        oh = ctx.enter_context(nc.sbuf_tensor("b_onehot", [P, SLOTS, G, P], F32))
        sum_ps = [ctx.enter_context(nc.psum_tensor(f"b_sum_ps{b}", [P, BANK], F32)) for b in range(SLOTS)]
        row_in = m.row_in
        row_in.use(SLOTS, 1)
        onehot = Steps(nc, ctx, "b_onehot_made")
        summed = Steps(nc, ctx, "b_summed", before=3)
        added = Steps(nc, ctx, "b_added", before=3, per=G)
        block = ctx.enter_context(nc.Block())

        @block.sync
        def _(sp):
            def load(q, k):
                wait_apart(m, sp, summed.sem, summed.before_reuse(q, SLOTS))
                sp.dma_start(rows[:, k, :, :], tiles_of(m.by_src, TP, q * G, 0, SROW)).then_inc(row_in.sems[k], 16)

            in_step(sp, N, SLOTS, (0, load))

        @block.tensor
        def _(pe):
            def sums(q, k):
                pe.wait_ge(added.sem, added.before_reuse(q, SLOTS))
                pe.wait_ge(onehot.sem, onehot.after(q))
                for j in range(G):
                    last = pe.matmul(sum_ps[k][:, j * F:(j + 1) * F], oh[:, k, j, :], rows[:, k, j, 0:F],
                                     start=True, stop=True)
                last.then_inc(summed.sem, 1)

            summed.start(pe)
            in_step(pe, N, SLOTS, (0, sums))

        @block.vector
        def _(v):
            def make_onehot(q, k):
                v.wait_ge(row_in.sems[k], row_in.after(q, k))
                v.wait_ge(summed.sem, summed.before_reuse(q, SLOTS))
                v.tensor_tensor(oh[:, k, :, :], rows[:, k, :, S_SLOC:S_SLOC + 1].to_broadcast([P, G, P]),
                                m.iota_nodes[:, :].unsqueeze(1).to_broadcast([P, G, P]),
                                ALU.is_equal).then_inc(onehot.sem, 1)

            add_first, add_next = adding(nc, v, m, added, m.tile_window_src,
                                         lambda k, j: sum_ps[k][:, j * F:(j + 1) * F], F)
            v.memset(m.acc[:, :, :], 0.0).then_inc(added.sem, added.head)
            in_step(v, N, SLOTS, (0, add_first(summed)), (2, make_onehot), *((0, add_next(j)) for j in range(1, G)))
        row_in.again(N)


def layer1_edges(nc, m):
    W, TP, N = m.windows, m.tiles, m.tiles // G
    with ExitStack() as ctx:
        def sb(name, shape, dt=F32):
            return ctx.enter_context(nc.sbuf_tensor(name, shape, dt))

        def bank(name, n=1, dt=F32):
            return ctx.enter_context(nc.psum_tensor(name, [P, n * BANK], dt))

        rows = sb("c_rows", [P, DEEP, G, CARRY])
        index = sb("c_index", [P, DEEP, G], I32)
        hid = sb("c_hidden", [P, DEEP, G, F + 1])
        oh_bf = sb("c_onehot_bf", [P, SLOTS, G, P], BF16)
        oh = sb("c_onehot", [P, 2, G, P])
        oh_t = sb("c_onehot_t", [P, 2, G * P])
        ef_t = sb("c_ef_t", [NEF, 2, G * P])
        oh_t_ps, ef_t_ps = bank("c_onehot_t_ps", dt=BF16), bank("c_ef_t_ps")
        own_ps = [bank(f"c_own_ps{b}") for b in range(2)]
        sum_ps = [bank(f"c_sum_ps{b}", 2) for b in range(2)]
        row_in, came = m.row_in, m.moved
        row_in.use(DEEP, 1)
        came.use(DEEP, G)
        ones = ctx.enter_context(nc.semaphore("c_ones"))
        indexed = Steps(nc, ctx, "c_indexed")
        onehot = Steps(nc, ctx, "c_onehot_made")
        turned = Steps(nc, ctx, "c_turned", before=7)
        copied = Steps(nc, ctx, "c_copied", before=1)
        owned = Steps(nc, ctx, "c_owned", before=1)
        totalled = Steps(nc, ctx, "c_totalled", before=1)
        widened = Steps(nc, ctx, "c_widened", before=3)
        gelued = Steps(nc, ctx, "c_gelued")
        summed = Steps(nc, ctx, "c_summed", before=7)
        added = Steps(nc, ctx, "c_added", before=1, per=G)
        block = ctx.enter_context(nc.Block())

        def sums(k, j):
            at = (j // 2) * BANK + (j % 2) * (F + 1)
            return sum_ps[k % 2][:, at:at + F + 1]

        @block.sync
        def _(sp):
            def load(q, k):
                wait_apart(m, sp, turned.sem, turned.before_reuse(q, DEEP))
                sp.dma_start(rows[:, k, :, :], tiles_of(m.by_src, TP, q * G, S_EF, SROW)).then_inc(row_in.sems[k], 16)

            in_step(sp, N, DEEP, (0, load))

        @block.gpsimd
        def _(pool):
            def gather(q, k):
                pool.wait_ge(summed.sem, summed.before_reuse(q, DEEP))
                wait_apart(m, pool, indexed.sem, indexed.after(q))
                for j in range(G):
                    pool.indirect_dma_start(
                        hid[:, k, j, 0:F], None, m.b_rows,
                        bass.IndirectOffsetOnAxis(ap=index[:, k, j:j + 1], axis=0)).then_inc(came.sems[k], 16)

            pool.memset(hid[:, :, :, F:F + 1], 1.0).then_inc(ones, 1)
            in_step(pool, N, DEEP, (0, gather))

        @block.vector
        def _(v):
            def make_index(q, k):
                v.wait_ge(came.sems[k], came.before(q, k))
                v.wait_ge(row_in.sems[k], row_in.after(q, k))
                v.tensor_copy(index[:, k, :], rows[:, k, :, S_DST - S_EF]).then_inc(indexed.sem, 1)

            def make_onehot(q, k):
                v.wait_ge(turned.sem, turned.before_reuse(q, SLOTS))
                v.wait_ge(widened.sem, widened.before_reuse(q, SLOTS))
                v.tensor_tensor(oh_bf[:, k % SLOTS, :, :], rows[:, k, :, CARRY - 1:CARRY].to_broadcast([P, G, P]),
                                m.iota_nodes[:, :].unsqueeze(1).to_broadcast([P, G, P]),
                                ALU.is_equal).then_inc(onehot.sem, 1)

            def total_up(q, k):
                v.wait_ge(came.sems[k], came.after(q, k))
                v.wait_ge(owned.sem, owned.after(q))
                v.tensor_tensor(hid[:, k, :, 0:F], own_ps[k % 2][:, :].rearrange("p (g f) -> p g f", g=G),
                                hid[:, k, :, 0:F], ALU.add).then_inc(totalled.sem, 1)

            add_first, add_next = adding(nc, v, m, added, m.tile_window_src, sums, F + 1)
            v.memset(m.acc[:, :, :], 0.0).then_inc(added.sem, added.head)
            totalled.start(v)
            in_step(v, N, DEEP, (0, add_first(summed)), (DEEP, make_index), (0, add_next(1)), (5, make_onehot),
                    (0, add_next(2)), (2, total_up), (0, add_next(3)))

        @block.tensor
        def _(pe):
            def own(q, k):
                b = k % 2
                windows = window_registers(nc, pe, m.tile_window_src, q * G, W)
                pe.wait_ge(totalled.sem, totalled.before_reuse(q, 2))
                pe.wait_ge(copied.sem, copied.after(q))
                for j in range(G):
                    to, of = own_ps[b][:, j * F:(j + 1) * F], slice(j * P, (j + 1) * P)
                    pe.matmul(to, oh_t[:, b, of], m.table[:, bass.ds(windows[j], 1), :].rearrange("p w f -> p (w f)"),
                              start=True, stop=False)
                    last = pe.matmul(to, ef_t[:, b, of], m.w1_ef[:, :], start=False, stop=True)
                last.then_inc(owned.sem, 1)

            def turn(q, k):
                pe.wait_ge(copied.sem, copied.before_reuse(q, 1))
                pe.wait_ge(onehot.sem, onehot.after(q))
                for j in range(G):
                    pe.transpose(ef_t_ps[0:NEF, j * P:(j + 1) * P], rows[:, k, j, 0:NEF], m.ident[:, :])
                    last = pe.transpose(oh_t_ps[:, j * P:(j + 1) * P], oh_bf[:, k % SLOTS, j, :], m.ident_bf[:, :])
                last.then_inc(turned.sem, 1)

            def sum_up(q, k):
                pe.wait_ge(added.sem, added.before_reuse(q, 2))
                pe.wait_ge(widened.sem, widened.after(q))
                pe.wait_ge(gelued.sem, gelued.after(q))
                pe.wait_ge(ones, 1)
                for j in range(G):
                    last = pe.matmul(sums(k, j), oh[:, k % 2, j, :], hid[:, k, j, :], start=True, stop=True)
                last.then_inc(summed.sem, 1)

            turned.start(pe)
            owned.start(pe)
            summed.start(pe)
            in_step(pe, N, DEEP, (3, own), (4, turn), (1, sum_up))

        @block.scalar
        def _(act):
            def copy(q, k):
                act.wait_ge(owned.sem, owned.before_reuse(q, 2))
                act.wait_ge(turned.sem, turned.after(q))
                act.activation(ef_t[:, k % 2, :], ef_t_ps[0:NEF, :], ACT.Copy)
                act.activation(oh_t[:, k % 2, :], oh_t_ps[:, :], ACT.Copy).then_inc(copied.sem, 1)

            def widen(q, k):
                act.wait_ge(summed.sem, summed.before_reuse(q, 2))
                act.wait_ge(onehot.sem, onehot.after(q))
                act.activation(oh[:, k % 2, :, :], oh_bf[:, k % SLOTS, :, :], ACT.Copy).then_inc(widened.sem, 1)

            def bend(q, k):
                act.wait_ge(totalled.sem, totalled.after(q))
                act.activation(hid[:, k, :, 0:F], hid[:, k, :, 0:F], ACT.Gelu).then_inc(gelued.sem, 1)

            copied.start(act)
            widened.start(act)
            in_step(act, N, DEEP, (2, widen), (4, copy), (2, bend))
        row_in.again(N)
        came.again(N)


def sums_by_dst(nc, m, layer, source, columns, weighted):
    W, TP, N = m.windows, m.tiles, m.tiles // G
    with ExitStack() as ctx:
        def sb(name, shape, dt=F32):
            return ctx.enter_context(nc.sbuf_tensor(name, shape, dt))

        def bank(name):
            return ctx.enter_context(nc.psum_tensor(name, [P, BANK], F32))

        rows = sb(f"d_rows_{layer}", [P, SLOTS, G, ROW])
        other = sb(f"d_other_{layer}", [P, SLOTS, G, columns])
        oh = sb(f"d_onehot_{layer}", [P, SLOTS, G, P])
        sum_ps = [bank(f"d_sum_ps{b}_{layer}") for b in range(2)]
        sh_t_ps = [bank(f"d_sh_t_ps{b}_{layer}") for b in range(2)]
        path_ps = [bank(f"d_path_ps{b}_{layer}") for b in range(2)]
        sh_t = sb(f"d_sh_t_{layer}", [NSH, 2, G * P])
        value = sb(f"d_value_{layer}", [P, 2, G, columns])
        row_in = m.row_in
        row_in.use(SLOTS, 1)
        came = m.moved
        came.use(SLOTS, G)
        onehot = Steps(nc, ctx, f"d_onehot_made_{layer}", before=3)
        if weighted:
            turned = Steps(nc, ctx, f"d_turned_{layer}", before=3)
            copied = Steps(nc, ctx, f"d_copied_{layer}", before=1)
            pathed = Steps(nc, ctx, f"d_pathed_{layer}", before=1)
            valued = Steps(nc, ctx, f"d_valued_{layer}", before=3)
        summed = Steps(nc, ctx, f"d_summed_{layer}", before=3)
        added = Steps(nc, ctx, f"d_added_{layer}", before=1, per=G)
        block = ctx.enter_context(nc.Block())
        users = valued if weighted else summed

        @block.sync
        def _(sp):
            def load(q, k):
                wait_apart(m, sp, came.sems[k], came.before(q, k))
                if weighted:
                    sp.wait_ge(turned.sem, turned.before_reuse(q, SLOTS))
                wait_apart(m, sp, onehot.sem, onehot.before_reuse(q, SLOTS))
                sp.dma_start(rows[:, k, :, :], tiles_of(m.by_dst, TP, q * G, 0, ROW)).then_inc(row_in.sems[k], 16)

            in_step(sp, N, SLOTS, (0, load))

        @block.gpsimd
        def _(pool):
            def gather(q, k):
                pool.wait_ge(users.sem, users.before_reuse(q, SLOTS))
                wait_apart(m, pool, row_in.sems[k], row_in.after(q, k))
                for j in range(G):
                    pool.indirect_dma_start(
                        other[:, k, j, :], None, source,
                        bass.IndirectOffsetOnAxis(ap=rows[:, k, j, C_SRC:C_SRC + 1].bitcast(I32), axis=0)
                    ).then_inc(came.sems[k], 16)

            in_step(pool, N, SLOTS, (0, gather))

        @block.vector
        def _(v):
            def make_onehot(q, k):
                v.wait_ge(row_in.sems[k], row_in.after(q, k))
                v.wait_ge(summed.sem, summed.before_reuse(q, SLOTS))
                v.tensor_tensor(oh[:, k, :, :], rows[:, k, :, C_DLOC:C_DLOC + 1].to_broadcast([P, G, P]),
                                m.iota_nodes[:, :].unsqueeze(1).to_broadcast([P, G, P]),
                                ALU.is_equal).then_inc(onehot.sem, 1)

            def weigh(q, k):
                b = k % 2
                v.wait_ge(came.sems[k], came.after(q, k))
                v.wait_ge(summed.sem, summed.before_reuse(q, 2))
                v.wait_ge(pathed.sem, pathed.after(q))
                v.tensor_tensor(value[:, b, :, :],
                                path_ps[b][:, 0:G * columns].rearrange("p (g f) -> p g f", g=G),
                                other[:, k, :, :], ALU.mult).then_inc(valued.sem, 1)

            add_first, add_next = adding(nc, v, m, added, m.tile_window_dst,
                                         lambda k, j: sum_ps[k % 2][:, j * columns:(j + 1) * columns], columns)
            if weighted:
                v.memset(m.acc[:, :, :], 0.0).then_inc(added.sem, added.head)
            else:
                added.start(v)
            onehot.start(v)
            if weighted:
                valued.start(v)
                in_step(v, N, SLOTS, (0, add_first(summed)), (2, make_onehot), (0, add_next(1)), (1, weigh),
                        (0, add_next(2)), (0, add_next(3)))
            else:
                in_step(v, N, SLOTS, (0, add_first(summed)), (2, make_onehot), *((0, add_next(j)) for j in range(1, G)))

        @block.tensor
        def _(pe):
            def turn(q, k):
                pe.wait_ge(row_in.sems[k], row_in.after(q, k))
                pe.wait_ge(copied.sem, copied.before_reuse(q, 2))
                for j in range(G):
                    last = pe.transpose(sh_t_ps[k % 2][0:NSH, j * P:(j + 1) * P],
                                        rows[:, k, j, C_SH:C_SH + NSH], m.ident[:, :])
                last.then_inc(turned.sem, 1)

            def path(q, k):
                b = k % 2
                pe.wait_ge(valued.sem, valued.before_reuse(q, 2))
                pe.wait_ge(copied.sem, copied.after(q))
                for j in range(G):
                    last = pe.matmul(path_ps[b][:, j * columns:(j + 1) * columns],
                                     sh_t[:, b, j * P:(j + 1) * P], m.pick_sh[:, :], start=True, stop=True)
                last.then_inc(pathed.sem, 1)

            def sum_up(q, k):
                b = k % 2
                pe.wait_ge(added.sem, added.before_reuse(q, 2))
                if weighted:
                    pe.wait_ge(valued.sem, valued.after(q))
                    of = value[:, b, :, :]
                else:
                    pe.wait_ge(came.sems[k], came.after(q, k))
                    of = other[:, k, :, :]
                pe.wait_ge(onehot.sem, onehot.after(q))
                for j in range(G):
                    last = pe.matmul(sum_ps[b][:, j * columns:(j + 1) * columns], oh[:, k, j, :], of[:, j, :],
                                     start=True, stop=True)
                last.then_inc(summed.sem, 1)

            summed.start(pe)
            if weighted:
                turned.start(pe)
                pathed.start(pe)
                in_step(pe, N, SLOTS, (2, turn), (1, path), (0, sum_up))
            else:
                in_step(pe, N, SLOTS, (0, sum_up))

        @block.scalar
        def _(act):
            def copy(q, k):
                act.wait_ge(pathed.sem, pathed.before_reuse(q, 2))
                act.wait_ge(turned.sem, turned.after(q))
                act.activation(sh_t[:, k % 2, :], sh_t_ps[k % 2][0:NSH, :], ACT.Copy).then_inc(copied.sem, 1)

            if weighted:
                copied.start(act)
                in_step(act, N, SLOTS, (1, copy))
        row_in.again(N)
        came.again(N)


def keep_h(nc, m):
    W, part = m.windows, 14
    with ExitStack() as ctx:
        relued, stored = ctx.enter_context(nc.semaphore("h_relued")), ctx.enter_context(nc.semaphore("h_stored"))
        block = ctx.enter_context(nc.Block())
        h_rows = m.h_rows.rearrange("(w p) f -> p w f", p=P)

        @block.scalar
        def _(act):
            in_step(act, W, part, (0, lambda w, k: relu_of(
                act, m, m.acc[:, bass.ds(w, 1), 0:F].rearrange("p w f -> p (w f)"), w).then_inc(relued, 1)))

        @block.sync
        def _(sp):
            parts = range(0, W, part)
            for w in parts:
                end = min(w + part, W)
                sp.wait_ge(relued, end)
                sp.dma_start(h_rows[:, w:end, :], m.acc[:, w:end, 0:F]).then_inc(stored, 16)
            sp.wait_ge(stored, 16 * len(parts))


def add_sums(nc, m):
    W, part = m.windows, 14
    with ExitStack() as ctx:
        added = ctx.enter_context(nc.semaphore("s_added"))
        block = ctx.enter_context(nc.Block())

        @block.vector
        def _(v):
            parts = [slice(w, min(w + part, W)) for w in range(0, W, part)]
            for n in range(len(parts) + 1):
                if n < len(parts):
                    x = m.x[:, parts[n], :]
                    v.tensor_tensor(x, x, m.acc[:, parts[n], 0:F], ALU.add).then_inc(added, 1)
                if n:
                    v.wait_ge(added, n)
                    for w in range(parts[n - 1].start, parts[n - 1].stop):
                        take_stats(v, m, w)


def store(nc, m, out):
    full, rest = m.nodes // P, m.nodes % P
    with ExitStack() as ctx:
        stored = ctx.enter_context(nc.semaphore("stored"))
        block = ctx.enter_context(nc.Block())

        @block.sync
        def _(sp):
            sp.dma_start(out[0:full * P, :].rearrange("(w p) f -> p w f", p=P), m.x[:, 0:full, :]).then_inc(stored, 16)
            if rest:
                sp.dma_start(out[full * P:m.nodes, :], m.x[0:rest, full, :]).then_inc(stored, 16)
            sp.wait_ge(stored, 16 * (1 + (rest > 0)))


def program(nc, out, nodes, edge_count, src_keys, dst_keys, edges, **w):
    with ExitStack() as ctx:
        m = Memory()
        m.nodes, m.windows = nodes, -(-nodes // (2 * P)) * 2
        m.edge_tiles, m.tiles = edge_tiles(edge_count), ordered_tiles(edge_count, m.windows)
        allocate(nc, ctx, m)
        load_constants(nc, m, w)
        count_windows(nc, m, src_keys, dst_keys)
        order_edges(nc, m, edges)
        first_stats(nc, m)
        normalise(nc, m, 0)
        project(nc, m, 0, m.w_in2f[:, :], F, None, F, None, 0)
        layer0_messages(nc, m)
        layer0_sums(nc, m)
        update_nodes(nc, m, 0)
        normalise(nc, m, 1)
        project(nc, m, 1, m.w1_ab[:, :], 2 * F, m.b1[:, :], F, m.b_rows, F)
        layer1_edges(nc, m)
        update_nodes(nc, m, 1)
        normalise(nc, m, 2)
        keep_h(nc, m)
        sums_by_dst(nc, m, 2, m.h_rows, F, False)
        add_sums(nc, m)
        normalise(nc, m, 3)
        project(nc, m, 3, m.pick_in[:, :], NPATH, None, 0, m.g_rows, NPATH)
        sums_by_dst(nc, m, 3, m.g_rows, NPATH, True)
        update_nodes(nc, m, 3)
        store(nc, m, out)


def kernel(**inputs):
    import numpy as np
    import concourse.bacc as bacc
    from concourse.bass_utils import run_bass_kernel_spmd as run

    a = {k: np.ascontiguousarray(v) for k, v in inputs.items()}
    nodes, count = a["x"].shape[0], a["src"].shape[0]
    T, windows = edge_tiles(count), -(-nodes // (2 * P)) * 2
    x = np.zeros((windows * P, F), np.float32)
    x[:nodes] = a["x"]
    edges = np.zeros((P * T, ROW), np.float32)
    edges[:count, C_RBF:C_ONE] = a["edge_attr_20"]
    edges[:, C_ONE] = 1.0
    edges[:count, C_WEIGHT] = a["edge_weight"]
    edges[:count, C_SH:C_SH + NSH] = a["edge_attr_16"]
    edges[:count, C_SRC] = a["src"].astype(np.int32, copy=False).view(np.float32)
    edges[:count, C_EF:C_EF + NEF] = a["edge_attr_32"]
    keys = np.full((2, P * T), -1, np.int32)
    keys[0, :count], keys[1, :count] = a["src"], a["dst"]
    arrays = {
        "src_keys": keys[0].reshape(P, T), "dst_keys": keys[1].reshape(P, T), "edges": edges, "x": x,
        "w_in2f_t": a["L0_gnn_W_in2f"].T, "w_f1_t": a["L0_gnn_W_f1"].T, "b_f1": a["L0_gnn_b_f1"],
        "w_f2_t": a["L0_gnn_W_f2"].T, "b_f2": a["L0_gnn_b_f2"], "w_o1_t": a["L0_gnn_W_o1"].T,
        "b_o1": a["L0_gnn_b_o1"], "w_o2_t": a["L0_gnn_W_o2"].T, "b_o2": a["L0_gnn_b_o2"],
        "w1": a["L1_gnn_W1"], "b1": a["L1_gnn_b1"], "w2": a["L1_gnn_W2"], "b2": a["L1_gnn_b2"],
        "coeff": a["L3_gnn_coeff"], "ki": a["L3_gnn_ki"], "kj": a["L3_gnn_kj"], "ko": a["L3_gnn_ko"],
    }
    arrays = {f"in_{k}": np.ascontiguousarray(v) for k, v in arrays.items()}
    nc = bacc.Bacc("TRN2", target_bir_lowering=False, num_devices=1)
    aps = {k[3:]: nc.dram_tensor(k, v.shape, mybir.dt.from_np(v.dtype), kind="ExternalInput").ap()
           for k, v in arrays.items()}
    out = nc.dram_tensor("out_0", (nodes, F), F32, kind="ExternalOutput").ap()
    program(nc, out, nodes, count, **aps)
    return run(nc, [arrays], core_ids=[0]).results[0]["out_0"]
```
